# Optimizing a Trainium2 kernel written in Bass

```python
import numpy as np
import jax
import jax.numpy as jnp

def _softmax(x, axis=-1):
    return jax.nn.softmax(x, axis=axis)
def _gelu(x):
    return jax.nn.gelu(x, approximate=True)
def _silu(x):
    return jax.nn.silu(x)
def _sigmoid(x):
    return jax.nn.sigmoid(x)
def _layernorm(x, axis=-1, eps=1e-5):
    m = jnp.mean(x, axis=axis, keepdims=True)
    v = jnp.var(x, axis=axis, keepdims=True)
    return (x - m) / jnp.sqrt(v + eps)
def _scatter_add(tgt, idx, src, axis=0):
    return tgt.at[idx].add(src)
def _segment_sum(src, seg, n):
    return jax.ops.segment_sum(src, seg, n)

kernel_name = 'mk_metaformer_d1_conv_nchw256_2f6f80'

def setup_inputs(seed: int = 0):
    np.random.seed(seed)
    _w = jnp.asarray
    def _rec_inputs():
        import jax
        import jax.numpy as jnp
        _gk = jax.random.key(seed)
        x = -0.0002928 + 1 * jax.random.normal(jax.random.fold_in(_gk, 1), (16, 256, 32, 32), jnp.float32)
        return x
    x = _rec_inputs()
    def _L0_conv_setup():
        import jax, jax.numpy as jnp
        import numpy as np
        key = jax.random.key(seed)
        k1, k2 = jax.random.split(key)
        B, D, H, W = (16, 256, 32, 32)
        K = 2048
        z = jax.random.normal(k1, (B, D, H, W), dtype=jnp.float32)
        codebook = jax.random.uniform(k2, (K, D), dtype=jnp.float32, minval=-1.0 / K, maxval=1.0 / K)
        return {'z': z, 'codebook': codebook}
    _L0_conv_all = _L0_conv_setup()
    _L0_conv_in = {k: v for k, v in _L0_conv_all.items() if k in ('codebook', )}
    del _L0_conv_all

    def _L0_ffn_setup():
        import jax, jax.numpy as jnp
        import numpy as np
        B, N, D = (16, 4096, 256)
        NUM_EXPERTS, TOP_K, HEADS = (4, 2, 4)
        N_EDGES = 1048576
        LN_EPS = 1e-05

        def _layernorm(x, g, b):
            mu = x.mean(-1, keepdims=True)
            var = ((x - mu) ** 2).mean(-1, keepdims=True)
            return (x - mu) * jax.lax.rsqrt(var + LN_EPS) * g + b

        def _forward(x, edge_index, W_gat, att_src, att_dst, b_gat, ln_gamma, ln_beta, W1, b1, W2, b2):
            Bc, Nc, Dc = x.shape
            M = Bc * Nc
            x_flat = x.reshape(M, Dc)
            h = (x_flat @ W_gat).reshape(M, HEADS, NUM_EXPERTS)
            loops = jnp.arange(M, dtype=edge_index.dtype)
            src = jnp.concatenate([edge_index[0], loops])
            dst = jnp.concatenate([edge_index[1], loops])
            a_src = (h * att_src).sum(-1)
            a_dst = (h * att_dst).sum(-1)
            e = jax.nn.leaky_relu(a_src[src] + a_dst[dst], negative_slope=0.2)
            e_max = jax.ops.segment_max(e, dst, num_segments=M)
            ee = jnp.exp(e - e_max[dst])
            denom = jax.ops.segment_sum(ee, dst, num_segments=M)
            alpha = ee / (denom[dst] + 1e-16)
            msg = h[src] * alpha[:, :, None]
            agg = jax.ops.segment_sum(msg, dst, num_segments=M).reshape(M, HEADS * NUM_EXPERTS) + b_gat
            scores = _layernorm(agg, ln_gamma, ln_beta).reshape(M, HEADS, NUM_EXPERTS).mean(1)
            scores = scores.reshape(Bc, Nc, NUM_EXPERTS)
            topk_s, topk_i = jax.lax.top_k(scores, TOP_K)
            w = jax.nn.softmax(topk_s, axis=-1)
            out = jnp.zeros_like(x)
            for ei in range(NUM_EXPERTS):
                g = jnp.where(topk_i == ei, w, 0.0).sum(-1)
                hh = jax.nn.gelu(x @ W1[ei] + b1[ei], approximate=False)
                out = out + g[..., None] * (hh @ W2[ei] + b2[ei])
            return out
        key = jax.random.key(seed)
        ks = jax.random.split(key, 8)
        s = 0.05
        return {'x': jax.random.normal(ks[0], (B, N, D), jnp.float32), 'W_gat': jax.random.normal(ks[1], (D, HEADS * NUM_EXPERTS), jnp.float32) * s, 'att_src': jax.random.normal(ks[2], (HEADS, NUM_EXPERTS), jnp.float32) * s, 'att_dst': jax.random.normal(ks[3], (HEADS, NUM_EXPERTS), jnp.float32) * s, 'b_gat': jnp.zeros((HEADS * NUM_EXPERTS,), jnp.float32), 'ln_gamma': jnp.ones((HEADS * NUM_EXPERTS,), jnp.float32), 'ln_beta': jnp.zeros((HEADS * NUM_EXPERTS,), jnp.float32), 'W1': jax.random.normal(ks[4], (NUM_EXPERTS, D, 2 * D), jnp.float32) * s, 'b1': jnp.zeros((NUM_EXPERTS, 2 * D), jnp.float32), 'W2': jax.random.normal(ks[5], (NUM_EXPERTS, 2 * D, D), jnp.float32) * s, 'b2': jnp.zeros((NUM_EXPERTS, D), jnp.float32), 'edge_index': jax.random.randint(ks[6], (2, N_EDGES), 0, B * N, jnp.int32)}
    _L0_ffn_all = _L0_ffn_setup()
    _L0_ffn_in = {k: v for k, v in _L0_ffn_all.items() if k in ('W_gat', 'att_src', 'att_dst', 'b_gat', 'ln_gamma', 'ln_beta', 'W1', 'b1', 'W2', 'b2', 'edge_index', )}
    del _L0_ffn_all

    return {
        "x": x,
        "L0_conv_codebook": _L0_conv_in["codebook"],
        "L0_ffn_W_gat": _L0_ffn_in["W_gat"],
        "L0_ffn_att_src": _L0_ffn_in["att_src"],
        "L0_ffn_att_dst": _L0_ffn_in["att_dst"],
        "L0_ffn_b_gat": _L0_ffn_in["b_gat"],
        "L0_ffn_ln_gamma": _L0_ffn_in["ln_gamma"],
        "L0_ffn_ln_beta": _L0_ffn_in["ln_beta"],
        "L0_ffn_W1": _L0_ffn_in["W1"],
        "L0_ffn_b1": _L0_ffn_in["b1"],
        "L0_ffn_W2": _L0_ffn_in["W2"],
        "L0_ffn_b2": _L0_ffn_in["b2"],
        "L0_ffn_edge_index": _L0_ffn_in["edge_index"],
    }

def reference(x, L0_conv_codebook, L0_ffn_W_gat, L0_ffn_att_src, L0_ffn_att_dst, L0_ffn_b_gat, L0_ffn_ln_gamma, L0_ffn_ln_beta, L0_ffn_W1, L0_ffn_b1, L0_ffn_W2, L0_ffn_b2, L0_ffn_edge_index):
    import jax
    import jax.numpy as jnp
    def _L0_conv_ref(z, codebook):
        import jax, jax.numpy as jnp
        import numpy as np
        B, D, H, W = z.shape
        z_flat = jnp.transpose(z, (0, 2, 3, 1)).reshape(-1, D)
        z_norm = z_flat
        codebook_norm = codebook
        distance = jnp.sum(z_norm * z_norm, axis=1, keepdims=True) + jnp.sum(codebook_norm * codebook_norm, axis=1) - 2.0 * jnp.matmul(z_norm, codebook_norm.T)
        vq_indices = jnp.argmin(distance, axis=1)
        z_q = codebook_norm[vq_indices]
        z_q_st = z_norm + jax.lax.stop_gradient(z_q - z_norm)
        out = z_q_st.reshape(B, H, W, D).transpose(0, 3, 1, 2)
        return out

    def _L0_ffn_ref(x, W_gat, att_src, att_dst, b_gat, ln_gamma, ln_beta, W1, b1, W2, b2, edge_index):
        import jax, jax.numpy as jnp
        import numpy as np
        B, N, D = (16, 4096, 256)
        NUM_EXPERTS, TOP_K, HEADS = (4, 2, 4)
        N_EDGES = 1048576
        LN_EPS = 1e-05

        def _layernorm(x, g, b):
            mu = x.mean(-1, keepdims=True)
            var = ((x - mu) ** 2).mean(-1, keepdims=True)
            return (x - mu) * jax.lax.rsqrt(var + LN_EPS) * g + b

        def _forward(x, edge_index, W_gat, att_src, att_dst, b_gat, ln_gamma, ln_beta, W1, b1, W2, b2):
            Bc, Nc, Dc = x.shape
            M = Bc * Nc
            x_flat = x.reshape(M, Dc)
            h = (x_flat @ W_gat).reshape(M, HEADS, NUM_EXPERTS)
            loops = jnp.arange(M, dtype=edge_index.dtype)
            src = jnp.concatenate([edge_index[0], loops])
            dst = jnp.concatenate([edge_index[1], loops])
            a_src = (h * att_src).sum(-1)
            a_dst = (h * att_dst).sum(-1)
            e = jax.nn.leaky_relu(a_src[src] + a_dst[dst], negative_slope=0.2)
            e_max = jax.ops.segment_max(e, dst, num_segments=M)
            ee = jnp.exp(e - e_max[dst])
            denom = jax.ops.segment_sum(ee, dst, num_segments=M)
            alpha = ee / (denom[dst] + 1e-16)
            msg = h[src] * alpha[:, :, None]
            agg = jax.ops.segment_sum(msg, dst, num_segments=M).reshape(M, HEADS * NUM_EXPERTS) + b_gat
            scores = _layernorm(agg, ln_gamma, ln_beta).reshape(M, HEADS, NUM_EXPERTS).mean(1)
            scores = scores.reshape(Bc, Nc, NUM_EXPERTS)
            topk_s, topk_i = jax.lax.top_k(scores, TOP_K)
            w = jax.nn.softmax(topk_s, axis=-1)
            out = jnp.zeros_like(x)
            for ei in range(NUM_EXPERTS):
                g = jnp.where(topk_i == ei, w, 0.0).sum(-1)
                hh = jax.nn.gelu(x @ W1[ei] + b1[ei], approximate=False)
                out = out + g[..., None] * (hh @ W2[ei] + b2[ei])
            return out
        return _forward(x, edge_index, W_gat, att_src, att_dst, b_gat, ln_gamma, ln_beta, W1, b1, W2, b2)

    def _gn(v, G=32, eps=1e-5):
        B_, C_, H_, W_ = v.shape
        g = v.reshape(B_, G, C_ // G, H_, W_)
        m = jnp.mean(g, axis=(2, 3, 4), keepdims=True)
        s = jnp.var(g, axis=(2, 3, 4), keepdims=True)
        return ((g - m) / jnp.sqrt(s + eps)).reshape(v.shape)

    def _ln_c(v, eps=1e-6):
        m = jnp.mean(v, axis=1, keepdims=True)
        s = jnp.var(v, axis=1, keepdims=True)
        return (v - m) / jnp.sqrt(s + eps)

    def _ln_t(v, eps=1e-5):
        m = jnp.mean(v, axis=-1, keepdims=True)
        s = jnp.var(v, axis=-1, keepdims=True)
        return (v - m) / jnp.sqrt(s + eps)

    def _to_tokens(v):
        B_, C_, H_, W_ = v.shape
        return v.reshape(B_, C_, H_ * W_).transpose(0, 2, 1)
    def _from_tokens(t, like):
        B_, C_, H_, W_ = like.shape
        return t.transpose(0, 2, 1).reshape(B_, C_, H_, W_)

    x = x + _L0_conv_ref(_ln_c(x), L0_conv_codebook)
    t = _to_tokens(x)
    t = t + _L0_ffn_ref(_ln_t(t), L0_ffn_W_gat, L0_ffn_att_src, L0_ffn_att_dst, L0_ffn_b_gat, L0_ffn_ln_gamma, L0_ffn_ln_beta, L0_ffn_W1, L0_ffn_b1, L0_ffn_W2, L0_ffn_b2, L0_ffn_edge_index)
    x = _from_tokens(t, x)
    return x


_drawn_inputs = setup_inputs


def setup_inputs(seed=0):
    import zlib

    import numpy as np

    out = dict(_drawn_inputs(seed))
    spreads = {'L0_ffn_b_gat': (0.0, 0.1),
     'L0_ffn_ln_gamma': (1.0, 0.2),
     'L0_ffn_ln_beta': (0.0, 0.1),
     'L0_ffn_b1': (0.0, 0.1),
     'L0_ffn_b2': (0.0, 0.1)}
    factors = {'L0_conv_codebook': 24.982}
    for name, (base, spread) in spreads.items():
        noise = np.random.default_rng([zlib.crc32(name.encode()), seed]).standard_normal(out[name].shape)
        drawn = base * np.exp(spread * noise) if base else spread * noise
        out[name] = jnp.asarray(drawn.astype(out[name].dtype))
    for name, factor in factors.items():
        out[name] = (out[name] * factor).astype(out[name].dtype)
    return out
```

```python
from contextlib import ExitStack

import concourse.bass as bass
from concourse import mybir

ALU = mybir.AluOpType
ACT = mybir.ActivationFunctionType
AX = mybir.AxisListType
F32 = mybir.dt.float32
BF16 = mybir.dt.bfloat16
I32 = mybir.dt.int32
U32 = mybir.dt.uint32

P = 128
D = 256
NC = D // P
UNROLL = 4
BANK = 512
BIG = 2.0 ** 100


class Tile:

    def __init__(self, j, r):
        self.j, self.r = j, r

    def back(self, n):
        return Tile(self.j, self.r - n)

    def slot(self, n):
        return self.r % n

    def n(self, per=1, plus=0):
        return self.j * (UNROLL * per) + (self.r * per + plus)

    def dmas(self, n):
        return self.j * (16 * UNROLL // n) + 16 * (self.r // n + 1)


def held(eng, sem, value):
    eng.wait_ge(sem, value)
    eng.nop(nofuse=True)


def steps(eng, tiles, depth, step):
    first = -(-depth // UNROLL) * UNROLL
    for s in range(first):
        step(Tile(0, s), lambda k, s=s: 0 <= s - k < tiles)
    with eng.Fori(first // UNROLL, tiles // UNROLL) as j:
        for r in range(UNROLL):
            step(Tile(j, r), lambda k: True)
    for s in range(tiles, tiles + depth):
        step(Tile(tiles // UNROLL, s - tiles), lambda k, s=s: 0 <= s - k < tiles)


def metaformer(nc, x, cbT, cb, wgat, att, b_gat, gamma, beta, w1, b1, w2, b2, edges, out):
    M = x.shape[0]
    K = cb.shape[0]
    _, NE, F = w1.shape
    FC = F // P
    NF = NE * FC
    HE = wgat.shape[1]
    HEADS = HE // NE
    E = edges.shape[1]
    NT = M // P
    G = BANK // P
    NG = M // BANK
    ET = E // P
    QN = K // BANK
    ROW = HE + 2 * HEADS
    ST = HE + 3 * HEADS

    t_d = nc.dram_tensor("t_scratch", [M, D], F32, kind="Internal").ap()
    tnT_d = nc.dram_tensor("tnT_scratch", [P, NC, M], F32, kind="Internal").ap()
    row_d = nc.dram_tensor("node_rows", [M, ROW], F32, kind="Internal").ap()
    st_d = nc.dram_tensor("node_states", [M, ST], F32, kind="Internal").ap()

    with ExitStack() as ctx:
        def sb(name, shape, dt=F32):
            return ctx.enter_context(nc.sbuf_tensor(name, shape, dt))

        def ps(name, shape):
            return ctx.enter_context(nc.psum_tensor(name, shape, F32))

        def sem(name):
            return ctx.enter_context(nc.semaphore(name))

        ident = sb("ident", [P, P])
        lower = sb("lower", [P, P])
        ones3 = sb("ones3", [3, P], BF16)
        sel3 = sb("sel3", [3, 3])
        halves = sb("halves", [P, 3])
        eps_c = sb("eps_c", [P, 1])
        eps_t = sb("eps_t", [P, 1])
        cbT_s = sb("cbT_s", [P, NC, K])
        w1_s = sb("w1_s", [P, NC, NE, F])
        w2_s = sb("w2_s", [P, NF, D])
        wg_s = sb("wg_s", [P, NC, HE])
        att_s = sb("att_s", [P, 2, HE])
        b1_s = sb("b1_s", [P, NF])
        gbb = sb("gbb", [P, 3, HE])
        nrm3 = sb("nrm3", [3, K], BF16)
        b23 = sb("b23", [3, NE * D], BF16)
        xt = sb("xt", [P, 4, D])
        stat = sb("stat", [P, 2, 6])
        mv = sb("mv", [P, 2, 2])
        std = sb("std", [P, 2])
        rstd = sb("rstd", [P, 2])
        xn = sb("xn", [P, 4, D])
        zT = sb("zT", [P, 2, NC, P])
        sc = sb("sc", [P, 2, K])
        mx = sb("mx", [P, 2, 8])
        ix = sb("ix", [P, 2, 8], U32)
        zq = sb("zq", [P, 2, D])
        zd = sb("zd", [P, 2, D])
        zs = sb("zs", [P, 2, D])
        tt = sb("tt", [P, 2, D])
        stat2 = sb("stat2", [P, 2, 6])
        mv2 = sb("mv2", [P, 2, 2])
        std2 = sb("std2", [P, 2])
        rstd2 = sb("rstd2", [P, 2])
        tn = sb("tn", [P, 2, D])
        tnT = sb("tnT", [P, 2, NC, P])
        row = sb("row", [P, 2, ROW])
        prod = sb("prod", [P, 2, 2, HE])
        S = sb("S", [P, NT, ST])
        T = sb("T", [P, NT, ROW])
        gA, gB = (sc[:, k, :].rearrange("p (i k) -> p i k", k=HE) for k in range(2))
        g1 = sb("g1", [P, NT])
        g2 = sb("g2", [P, NT])
        sE = sb("sE", [P, NT, NE])
        rk = sb("rk", [P, NT, NE])
        tE = sb("tE", [P, NT, NE])
        gate = sb("gate", [P, NT, NE])
        hh = sb("hh", [P, NF, BANK])
        hv = hh[:].rearrange("p f n -> p (f n)")
        n3, rest, b2f, part = hv[0:3, 0:K], hv[0:3, K:2 * K], hv[0:3, 2 * K:2 * K + NE * D], hv[0:3, 3 * K:4 * K].bitcast(BF16)
        tnG = sb("tnG", [P, 2, NC, BANK])
        tG = sb("tG", [P, 2, G, D])
        acc = sb("acc", [P, 2, D])

        banks = [ps(f"bank{i}", [P, BANK]) for i in range(8)]

        names = """const wld nrm_sq nrm_ps n_chain b_chain d_stat d_mv a_std d_rstd xn_ready pzT zT_ready
        sc_ready sc_evac d_mx ix_ready z_diff z_st t_ready d_stat2 d_mv2 a_std2 d_rstd2 tn_ready ptT tnT_ready
        h_ps h_evac d_prod row_ready conv_done""".split()
        s = {n: sem(n) for n in names}
        x_ld = [sem(f"x_ld{i}") for i in range(4)]
        zq_ld = [sem(f"zq_ld{i}") for i in range(2)]
        t_st = [sem(f"t_st{i}") for i in range(2)]
        tnT_st = [sem(f"tnT_st{i}") for i in range(2)]
        row_st = [sem(f"row_st{i}") for i in range(2)]
        tnG_ld = [sem(f"tnG_ld{i}") for i in range(2)]
        tG_ld = [sem(f"tG_ld{i}") for i in range(2)]
        out_st = [sem(f"out_st{i}") for i in range(2)]
        g_ld, g_chain, g_exp, gates_ready = sem("g_ld"), sem("g_chain"), sem("g_exp"), sem("gates_ready")
        w_ps, hh_ready, y_ps, acc_chain, acc_ready = (sem(n) for n in
                                                      ("w_ps", "hh_ready", "y_ps", "acc_chain", "acc_ready"))
        st_chain, st_init, g_sq = sem("st_chain"), sem("st_init"), sem("g_sq")

        GENERAL = general_path(nc, ctx, sb, sem, banks, row_d, st_d, edges, ident, lower, M, ROW, ST, HE, HEADS, ET, g_ld)

        ALL_T = 16 * NT // 2
        x_v = x
        block = ctx.enter_context(nc.Block())

        @block.sync
        def _(sp):
            sp.dma_start(cbT_s[:], cbT.rearrange("(c p) k -> p c k", p=P)).then_inc(s["wld"], 16)
            sp.dma_start(wg_s[:], wgat.rearrange("(c p) h -> p c h", p=P)).then_inc(s["wld"], 16)
            sp.dma_start(att_s[:], att.rearrange("(o a) h -> o a h", o=1).broadcast_to([P, 2, HE])).then_inc(s["wld"], 16)
            for k, v in enumerate((b_gat, gamma, beta)):
                sp.dma_start(gbb[:, k, :], v.rearrange("(o h) -> o h", o=1).broadcast_to([P, HE])).then_inc(s["wld"], 16)
            sp.dma_start(b2f, b2.rearrange("(o e) d -> o (e d)", o=1).broadcast_to([3, NE * D])).then_inc(s["wld"], 16)
            sp.dma_start(b1_s[:], b1).then_inc(s["wld"], 16)
            sp.dma_start(w1_s[:], w1.rearrange("(c p) e f -> p c e f", p=P)).then_inc(s["wld"], 16)
            sp.dma_start(w2_s[:], w2.rearrange("e (c p) d -> p (e c) d", p=P)).then_inc(s["wld"], 16)

            def step(i, live):
                if live(0):
                    if live(4):
                        held(sp, s["t_ready"], i.back(4).n(1, 1))
                    sp.dma_start(xt[:, i.slot(4), :], x_v[bass.ds(i.n(P), P), :]).then_inc(x_ld[i.slot(4)], 16)
                if live(3):
                    k = i.back(3)
                    held(sp, s["t_ready"], k.n(1, 1))
                    sp.dma_start(t_d[bass.ds(k.n(P), P), :], tt[:, k.slot(2), :]).then_inc(t_st[k.slot(2)], 16)
                if live(4):
                    k = i.back(4)
                    held(sp, s["tnT_ready"], k.n(1, 1))
                    sp.dma_start(tnT_d[:, :, bass.ds(k.n(P), P)], tnT[:, k.slot(2), :, :]).then_inc(tnT_st[k.slot(2)], 16)
                    held(sp, s["row_ready"], k.n(1, 1))
                    sp.dma_start(row_d[bass.ds(k.n(P), P), :], row[:, k.slot(2), :]).then_inc(row_st[k.slot(2)], 16)
            steps(sp, NT, 4, step)
            for q in t_st + tnT_st + row_st:
                sp.wait_ge(q, ALL_T)
            sp.dma_start(T[:], row_d.rearrange("(i p) k -> p i k", p=P)).then_inc(g_ld, 16)
            sp.wait_ge(st_init, 1)
            sp.dma_start(st_d.rearrange("(i p) k -> p i k", p=P), S[:]).then_inc(g_ld, 16)
            sp.wait_ge(g_ld, 32)
            GENERAL.sync(sp)
            sp.dma_start(S[:], st_d.rearrange("(i p) k -> p i k", p=P)).then_inc(g_ld, 16)

            def group(i, live):
                if live(0):
                    b = i.slot(2)
                    if live(2):
                        held(sp, w_ps, i.back(2).n(NF, NF))
                        held(sp, acc_ready, i.back(2).n(G, G))
                    sp.dma_start(tnG[:, b, :, :], tnT_d[:, :, bass.ds(i.n(BANK), BANK)]).then_inc(tnG_ld[b], 16)
                    sp.dma_start(tG[:, b, :, :], t_d[bass.ds(i.n(BANK), BANK), :].rearrange("(k p) d -> p k d", p=P)).then_inc(tG_ld[b], 16)
                if live(1):
                    g = i.back(1)
                    for k in range(G):
                        held(sp, acc_ready, g.n(G, k + 1))
                        sp.dma_start(out[bass.ds(g.n(BANK, k * P), P), :], acc[:, k % 2, :]).then_inc(out_st[k % 2], 16)
            steps(sp, NG, 2, group)
            for q in out_st:
                sp.wait_ge(q, ALL_T)

        @block.gpsimd
        def _(pool):
            pool.memset(ident[:], 0.0).then_inc(s["const"], 1)
            pool.memset(lower[:], 1.0).then_inc(s["const"], 1)
            pool.memset(ones3[:], 1.0).then_inc(s["const"], 1)
            pool.memset(halves[:], -0.5).then_inc(s["const"], 1)
            pool.memset(eps_c[:], 1e-6).then_inc(s["const"], 1)
            pool.memset(eps_t[:], 1e-5).then_inc(s["const"], 1)
            pool.memset(sel3[:], 0.0).then_inc(s["const"], 1)
            pool.wait_ge(s["const"], 7)
            pool.affine_select(out=ident[:], in_=ident[:], compare_op=ALU.not_equal, fill=1.0, base=0,
                               pattern=[[-1, P]], channel_multiplier=1).then_inc(s["const"], 1)
            pool.affine_select(out=lower[:], in_=lower[:], compare_op=ALU.is_gt, fill=0.0, base=0,
                               pattern=[[-1, P]], channel_multiplier=1).then_inc(s["const"], 1)
            pool.affine_select(out=sel3[:], in_=sel3[:], compare_op=ALU.not_equal, fill=1.0, base=0,
                               pattern=[[-1, 3]], channel_multiplier=1).then_inc(s["const"], 1)

            def step(i, live):
                if live(2):
                    k = i.back(2)
                    b = k.slot(2)
                    held(pool, s["ix_ready"], k.n(1, 1))
                    if live(4):
                        held(pool, s["z_diff"], k.back(2).n(1, 1))
                    pool.indirect_dma_start(out=zq[:, b, :], out_offset=None, in_=cb,
                                            in_offset=bass.IndirectOffsetOnAxis(ap=ix[:, b, 0:1], axis=0),
                                            bounds_check=K - 1, oob_is_err=False).then_inc(zq_ld[b], 16)
            steps(pool, NT, 5, step)
            GENERAL.gpsimd(pool)

        @block.scalar
        def _(act):
            act.wait_ge(s["wld"], 160)
            for c in range(NC):
                act.activation(sc[:, c, :], cbT_s[:, c, :], ACT.Square).then_inc(s["nrm_sq"], 1)

            def step(i, live):
                if live(0):
                    act.wait_ge(s["d_mv"], i.n(1, 1))
                    if live(2):
                        act.wait_ge(s["d_rstd"], i.back(2).n(1, 1))
                    act.activation(std[:, i.slot(2):i.slot(2) + 1], mv[:, i.slot(2), 1:2], ACT.Sqrt, bias=eps_c[:]).then_inc(s["a_std"], 1)
                if live(1):
                    k = i.back(1)
                    b = k.slot(2)
                    act.wait_ge(s["pzT"], k.n(1, 1))
                    if live(3):
                        act.wait_ge(s["sc_ready"], k.back(2).n(QN, QN))
                    act.activation(zT[:, b, :, :], banks[4][:, 0:D].rearrange("p (c t) -> p c t", c=NC), ACT.Copy).then_inc(s["zT_ready"], 1)
                    for q in range(QN):
                        act.wait_ge(s["sc_ready"], k.n(QN, q + 1))
                        if live(3) and q == 0:
                            act.wait_ge(s["ix_ready"], k.back(2).n(1, 1))
                        act.activation(sc[:, b, q * BANK:(q + 1) * BANK], banks[q][:], ACT.Copy).then_inc(s["sc_evac"], 1)
                if live(3):
                    k = i.back(3)
                    b = k.slot(2)
                    act.wait_ge(s["d_mv2"], k.n(1, 1))
                    if live(5):
                        act.wait_ge(s["d_rstd2"], k.back(2).n(1, 1))
                    act.activation(std2[:, b:b + 1], mv2[:, b, 1:2], ACT.Sqrt, bias=eps_t[:]).then_inc(s["a_std2"], 1)
                    act.wait_ge(s["ptT"], k.n(1, 1))
                    if live(5):
                        act.wait_ge(tnT_st[b], k.back(2).dmas(2))
                        act.wait_ge(s["h_ps"], k.back(2).n(1, 1))
                    act.activation(tnT[:, b, :, :], banks[5][:, 0:D].rearrange("p (c t) -> p c t", c=NC), ACT.Copy).then_inc(s["tnT_ready"], 1)
                    act.wait_ge(s["h_ps"], k.n(1, 1))
                    if live(5):
                        act.wait_ge(row_st[b], k.back(2).dmas(2))
                        act.wait_ge(s["d_prod"], k.back(2).n(1, 1))
                    act.activation(row[:, b, 0:HE], banks[6][:, 0:HE], ACT.Copy).then_inc(s["h_evac"], 1)
            steps(act, NT, 5, step)
            GENERAL.scalar(act)
            act.wait_ge(g_sq, 1)
            act.activation(g2[:], g1[:], ACT.Sqrt, bias=eps_t[:]).then_inc(g_sq, 1)
            act.wait_ge(g_exp, 1)
            act.activation(tE[:], tE[:], ACT.Exp).then_inc(g_exp, 1)

            def group(i, live):
                if live(0):
                    for f in range(NF):
                        act.wait_ge(w_ps, i.n(NF, f + 1))
                        if live(1) and f == 0:
                            act.wait_ge(y_ps, i.back(1).n(G, G))
                        act.activation(hh[:, f, :], banks[f % 4][:], ACT.Gelu, bias=b1_s[:, f:f + 1]).then_inc(hh_ready, 1)
            steps(act, NG, 2, group)

        @block.tensor
        def _(pe):
            pe.wait_ge(s["nrm_sq"], NC)
            pe.wait_ge(s["const"], 10)
            for q in range(QN):
                for c in range(NC):
                    mm = pe.matmul(banks[q][0:3, :], halves[:], sc[:, c, q * BANK:(q + 1) * BANK], start=c == 0, stop=c == NC - 1)
            mm.then_inc(s["nrm_ps"], 1)
            pe.wait_ge(s["n_chain"], QN + 2 * 9)

            def step(i, live):
                if live(0):
                    pe.wait_ge(s["xn_ready"], i.n(1, 1))
                    if live(1):
                        pe.wait_ge(s["zT_ready"], i.back(1).n(1, 1))
                    for c in range(NC):
                        mm = pe.transpose(banks[4][:, c * P:(c + 1) * P], xn[:, i.slot(4), c * P:(c + 1) * P], ident[:])
                    mm.then_inc(s["pzT"], 1)
                if live(1):
                    k = i.back(1)
                    pe.wait_ge(s["zT_ready"], k.n(1, 1))
                    for q in range(QN):
                        if live(2):
                            pe.wait_ge(s["sc_evac"], k.back(1).n(QN, q + 1))
                        cols = slice(q * BANK, (q + 1) * BANK)
                        pe.matmul(banks[q][:], ones3[:], nrm3[:, cols], start=True, stop=False)
                        for c in range(NC):
                            mm = pe.matmul(banks[q][:], zT[:, k.slot(2), c, :], cbT_s[:, c, cols], start=False, stop=c == NC - 1)
                        mm.then_inc(s["sc_ready"], 1)
                if live(3):
                    k = i.back(3)
                    b = k.slot(2)
                    pe.wait_ge(s["tn_ready"], k.n(1, 1))
                    if live(4):
                        pe.wait_ge(s["tnT_ready"], k.back(1).n(1, 1))
                    for c in range(NC):
                        mm = pe.transpose(banks[5][:, c * P:(c + 1) * P], tn[:, b, c * P:(c + 1) * P], ident[:])
                    mm.then_inc(s["ptT"], 1)
                    pe.wait_ge(s["tnT_ready"], k.n(1, 1))
                    if live(4):
                        pe.wait_ge(s["h_evac"], k.back(1).n(1, 1))
                    for c in range(NC):
                        mm = pe.matmul(banks[6][:, 0:HE], tnT[:, b, c, :], wg_s[:, c, :], start=c == 0, stop=c == NC - 1)
                    mm.then_inc(s["h_ps"], 1)
            steps(pe, NT, 5, step)
            GENERAL.tensor(pe)

            def group(i, live):
                if live(0):
                    b = i.slot(2)
                    pe.wait_ge(tnG_ld[b], i.dmas(2))
                    for f in range(NF):
                        e, c2 = divmod(f, FC)
                        if f >= 4:
                            pe.wait_ge(hh_ready, i.n(NF, f - 3))
                        elif live(1):
                            pe.wait_ge(hh_ready, i.n(NF, f - 3))
                        for c in range(NC):
                            mm = pe.matmul(banks[f % 4][:], w1_s[:, c, e, c2 * P:(c2 + 1) * P], tnG[:, b, c, :], start=c == 0, stop=c == NC - 1)
                        mm.then_inc(w_ps, 1)
                    for k in range(G):
                        y = banks[4 + 2 * (k % 2):6 + 2 * (k % 2)]
                        if k >= 2 or live(1):
                            pe.wait_ge(acc_ready, i.n(G, k - 1))
                        for e in range(NE):
                            yb = y[e // 2][:, (e % 2) * D:(e % 2 + 1) * D]
                            if e % 2 == 0:
                                pe.matmul(y[e // 2][:], ones3[:], b23[:, e * D:(e + 2) * D], start=True, stop=False, skip_group_check=True)
                            for c2 in range(FC):
                                f = e * FC + c2
                                if k == 0:
                                    pe.wait_ge(hh_ready, i.n(NF, f + 1))
                                mm = pe.matmul(yb, hh[:, f, k * P:(k + 1) * P], w2_s[:, f, :], start=False, stop=c2 == FC - 1, skip_group_check=True)
                        mm.then_inc(y_ps, 1)
            steps(pe, NG, 2, group)

        @block.vector
        def _(v):
            def split(dst, src, n, chain, at):
                for k in range(3):
                    v.tensor_copy(part[:, 0:n], rest[:, 0:n] if k else src).then_inc(chain, 1)
                    at += 1
                    v.wait_ge(chain, at)
                    if k == 0:
                        v.tensor_scalar(dst[:], part[:, 0:n], sel3[:, 0:1], None, ALU.mult).then_inc(chain, 1)
                    else:
                        v.scalar_tensor_tensor(out=dst[:], in0=part[:, 0:n], scalar=sel3[:, k:k + 1], in1=dst[:], op0=ALU.mult, op1=ALU.add).then_inc(chain, 1)
                    v.tensor_tensor(rest[:, 0:n], rest[:, 0:n] if k else src, part[:, 0:n], ALU.subtract).then_inc(chain, 1)
                    at += 2
                    v.wait_ge(chain, at)
                return at

            v.wait_ge(s["nrm_ps"], 1)
            for q in range(QN):
                v.tensor_copy(n3[:, q * BANK:(q + 1) * BANK], banks[q][0:3, :]).then_inc(s["n_chain"], 1)
            v.wait_ge(s["n_chain"], QN)
            v.wait_ge(s["const"], 10)
            at = split(nrm3, n3, K, s["n_chain"], QN)
            v.wait_ge(s["wld"], 160)
            split(b23, b2f, NE * D, s["n_chain"], at)

            def step(i, live):
                if live(2):
                    k = i.back(2)
                    b = k.slot(2)
                    held(v, s["sc_evac"], k.n(QN, QN))
                    v.max(mx[:, b, :], sc[:, b, :]).then_inc(s["d_mx"], 1)
                if live(0):
                    b = i.slot(2)
                    held(v, x_ld[i.slot(4)], i.dmas(4))
                    if live(2):
                        held(v, s["d_mv"], i.back(2).n(1, 1))
                    v.bn_stats(stat[:, b, :], xt[:, i.slot(4), :]).then_inc(s["d_stat"], 1)
                    held(v, s["d_stat"], i.n(1, 1))
                    if live(2):
                        held(v, s["xn_ready"], i.back(2).n(1, 1))
                        held(v, s["a_std"], i.back(2).n(1, 1))
                    v.bn_aggr(mv[:, b, :], stat[:, b, :]).then_inc(s["d_mv"], 1)
                if live(2):
                    k = i.back(2)
                    b = k.slot(2)
                    held(v, s["d_mx"], k.n(1, 1))
                    if live(4):
                        held(v, zq_ld[b], k.back(2).dmas(2))
                    v.max_index(ix[:, b, :], mx[:, b, :], sc[:, b, :]).then_inc(s["ix_ready"], 1)
                if live(0):
                    b = i.slot(2)
                    held(v, s["a_std"], i.n(1, 1))
                    v.reciprocal(rstd[:, b:b + 1], std[:, b:b + 1]).then_inc(s["d_rstd"], 1)
                    held(v, s["d_rstd"], i.n(1, 1))
                    v.tensor_scalar(xn[:, i.slot(4), :], xt[:, i.slot(4), :], mv[:, b, 0:1], rstd[:, b:b + 1], ALU.subtract, ALU.mult).then_inc(s["xn_ready"], 1)
                if live(3):
                    k = i.back(3)
                    b = k.slot(2)
                    held(v, zq_ld[b], k.dmas(2))
                    if live(5):
                        held(v, s["z_st"], k.back(2).n(1, 1))
                    v.tensor_tensor(zd[:, b, :], zq[:, b, :], xn[:, k.slot(4), :], ALU.subtract).then_inc(s["z_diff"], 1)
                    held(v, s["z_diff"], k.n(1, 1))
                    if live(5):
                        held(v, s["t_ready"], k.back(2).n(1, 1))
                    v.tensor_tensor(zs[:, b, :], xn[:, k.slot(4), :], zd[:, b, :], ALU.add).then_inc(s["z_st"], 1)
                    held(v, s["z_st"], k.n(1, 1))
                    if live(5):
                        held(v, t_st[b], k.back(2).dmas(2))
                        held(v, s["tn_ready"], k.back(2).n(1, 1))
                    v.tensor_tensor(tt[:, b, :], xt[:, k.slot(4), :], zs[:, b, :], ALU.add).then_inc(s["t_ready"], 1)
                    held(v, s["t_ready"], k.n(1, 1))
                    v.bn_stats(stat2[:, b, :], tt[:, b, :]).then_inc(s["d_stat2"], 1)
                    held(v, s["d_stat2"], k.n(1, 1))
                    v.bn_aggr(mv2[:, b, :], stat2[:, b, :]).then_inc(s["d_mv2"], 1)
                    held(v, s["a_std2"], k.n(1, 1))
                    v.reciprocal(rstd2[:, b:b + 1], std2[:, b:b + 1]).then_inc(s["d_rstd2"], 1)
                    held(v, s["d_rstd2"], k.n(1, 1))
                    if live(5):
                        held(v, s["ptT"], k.back(2).n(1, 1))
                    v.tensor_scalar(tn[:, b, :], tt[:, b, :], mv2[:, b, 0:1], rstd2[:, b:b + 1], ALU.subtract, ALU.mult).then_inc(s["tn_ready"], 1)
                if live(4):
                    k = i.back(4)
                    b = k.slot(2)
                    held(v, s["h_evac"], k.n(1, 1))
                    if live(6):
                        held(v, s["row_ready"], k.back(2).n(1, 1))
                    v.tensor_tensor(prod[:, b, :, :], row[:, b, 0:HE].unsqueeze(1).broadcast_to([P, 2, HE]), att_s[:], ALU.mult).then_inc(s["d_prod"], 1)
                    held(v, s["d_prod"], k.n(1, 1))
                    if live(6):
                        held(v, row_st[b], k.back(2).dmas(2))
                    v.tensor_reduce(row[:, b, HE:ROW], prod[:, b, :, :].rearrange("p a (h e) -> p (a h) e", h=HEADS), AX.X, ALU.add).then_inc(s["row_ready"], 1)
            steps(v, NT, 5, step)

            v.wait_ge(g_ld, 16)
            v.tensor_copy(S[:, :, 0:HE], T[:, :, 0:HE]).then_inc(st_chain, 1)
            v.memset(S[:, :, HE:HE + HEADS], 1.0).then_inc(st_chain, 1)
            v.tensor_copy(S[:, :, HE + 2 * HEADS:ST], T[:, :, HE + HEADS:ROW]).then_inc(st_chain, 1)
            v.tensor_tensor(sE[:], T[:, :, HE:HE + HEADS], T[:, :, HE + HEADS:ROW], ALU.add).then_inc(st_chain, 1)
            v.wait_ge(st_chain, 4)
            v.scalar_tensor_tensor(out=S[:, :, HE + HEADS:HE + 2 * HEADS], in0=sE[:], scalar=0.2, in1=sE[:], op0=ALU.mult, op1=ALU.max).then_inc(st_init, 1)
            GENERAL.vector(v)

            c = [0]

            def link(ins):
                ins.then_inc(g_chain, 1)
                c[0] += 1
                v.wait_ge(g_chain, c[0])

            def bc(a, n):
                return a.unsqueeze(2).broadcast_to([P, NT, n])

            v.wait_ge(g_ld, 48)
            link(v.tensor_scalar(rk[:], S[:, :, HE:HE + HEADS], 1e-16, None, ALU.add))
            link(v.reciprocal(sE[:], rk[:]))
            h4 = lambda a: a.rearrange("p i (h e) -> p i h e", h=HEADS)
            link(v.tensor_tensor(h4(gA), h4(S[:, :, 0:HE]), sE[:].unsqueeze(3).broadcast_to([P, NT, HEADS, NE]), ALU.mult))
            row3 = lambda k: gbb[:, k, :].unsqueeze(1).broadcast_to([P, NT, HE])
            link(v.tensor_tensor(gB, gA, row3(0), ALU.add))
            link(v.tensor_reduce(g1[:], gB, AX.X, ALU.add))
            link(v.tensor_scalar(g2[:], g1[:], 1.0 / HE, None, ALU.mult))
            link(v.tensor_tensor(gA, gB, bc(g2[:], HE), ALU.subtract))
            link(v.tensor_tensor(gB, gA, gA, ALU.mult))
            link(v.tensor_reduce(g2[:], gB, AX.X, ALU.add))
            v.tensor_scalar(g1[:], g2[:], 1.0 / HE, None, ALU.mult).then_inc(g_sq, 1)
            v.wait_ge(g_sq, 2)
            link(v.reciprocal(g1[:], g2[:]))
            link(v.tensor_tensor(gB, gA, bc(g1[:], HE), ALU.mult))
            link(v.tensor_tensor(gA, gB, row3(1), ALU.mult))
            link(v.tensor_tensor(gB, gA, row3(2), ALU.add))
            link(v.tensor_reduce(rk[:], gB.rearrange("p i (h e) -> p i e h", h=HEADS), AX.X, ALU.add))
            link(v.tensor_scalar(sE[:], rk[:], 1.0 / HEADS, None, ALU.mult))
            link(v.tensor_reduce(g1[:], sE[:], AX.X, ALU.max))
            v.tensor_tensor(tE[:], sE[:], bc(g1[:], NE), ALU.subtract).then_inc(g_exp, 1)
            link(v.memset(rk[:], 0.0))
            for e in range(NE):
                for o in range(NE):
                    if o != e:
                        link(v.tensor_tensor(g2[:], sE[:, :, o], sE[:, :, e], ALU.is_ge if o < e else ALU.is_gt))
                        link(v.tensor_tensor(rk[:, :, e], rk[:, :, e], g2[:], ALU.add))
            v.wait_ge(g_exp, 2)
            link(v.scalar_tensor_tensor(out=gate[:], in0=rk[:], scalar=2.0, in1=tE[:], op0=ALU.is_lt, op1=ALU.mult))
            link(v.tensor_reduce(g1[:], gate[:], AX.X, ALU.add))
            link(v.reciprocal(g2[:], g1[:]))
            link(v.tensor_tensor(gate[:], gate[:], bc(g2[:], NE), ALU.mult))

            gate_v = gate[:].rearrange("p i e -> p (i e)")

            def group(i, live):
                if live(0):
                    b = i.slot(2)
                    held(v, tG_ld[b], i.dmas(2))
                    for k in range(G):
                        held(v, y_ps, i.n(G, k + 1))
                        if k >= 2 or live(1):
                            t = out_seen(i, k)
                            held(v, out_st[k % 2], t)
                        for e in range(NE):
                            y = banks[4 + 2 * (k % 2) + e // 2][:, (e % 2) * D:(e % 2 + 1) * D]
                            src = tG[:, b, k, :] if e == 0 else acc[:, k % 2, :]
                            g = gate_v[:, bass.ds(i.n(G * NE, k * NE + e), 1)]
                            ins = v.scalar_tensor_tensor(out=acc[:, k % 2, :], in0=y, scalar=g, in1=src, op0=ALU.mult, op1=ALU.add)
                            if e < NE - 1:
                                ins.then_inc(acc_chain, 1)
                                v.wait_ge(acc_chain, i.n(G * (NE - 1), k * (NE - 1) + e + 1))
                            else:
                                ins.then_inc(acc_ready, 1)

            def out_seen(i, k):
                return i.n(2 * 16, 16 * (k // 2))
            steps(v, NG, 2, group)


class general_path:

    def __init__(self, nc, ctx, sb, sem, banks, row_d, st_d, edges, ident, lower, M, ROW, ST, HE, HEADS, ET, states_stored):
        self.banks, self.row_d, self.st_d, self.edges, self.ident, self.lower = banks, row_d, st_d, edges, ident, lower
        self.M, self.ROW, self.ST, self.HE, self.HEADS, self.ET = M, ROW, ST, HE, HEADS, ET
        self.states_stored = states_stored
        self.ends = sb("ends", [P, 2], I32)
        self.isrc = sb("isrc", [P, 1], U32)
        self.idst = sb("idst", [P, 1], U32)
        self.iwr = sb("iwr", [P, 1], U32)
        self.dstf = sb("dstf", [P, 1])
        self.rs = sb("rs", [P, ROW])
        self.so = sb("so", [P, ST])
        self.sn = sb("sn", [P, ST])
        self.ee = sb("ee", [P, 2, HEADS])
        self.eq = sb("eq", [P, P])
        self.pen = sb("pen", [P, P])
        self.msk = sb("msk", [P, HEADS, P])
        self.tm = sb("tm", [P, HEADS])
        self.df = sb("df", [P, 2, HEADS])
        self.ex = sb("ex", [P, 2, HEADS])
        self.vv = sb("vv", [P, HE + HEADS])
        self.oc = sb("oc", [P, HE + HEADS])
        self.cnt = sb("cnt", [P, 1])
        self.s = {n: sem("gp_" + n) for n in "init ld eq_ps eT_ps v sum_ps exp".split()}
        self.PARTS = 4
        self.dma = [{n: sem(f"gp_{n}{k}") for n in ("rows", "states", "wr")} for k in range(self.PARTS)]

    V = 21

    def sync(self, sp):
        s = self.s
        with sp.Fori(0, self.ET) as i:
            for k in range(2):
                sp.dma_start(self.ends[:, k:k + 1], self.edges[k, bass.ds(i * P, P)].rearrange("(p o) -> p o", o=1)).then_inc(s["ld"], 16)
            held(sp, s["v"], i * self.V + 3)
        for part in self.dma:
            sp.wait_ge(part["wr"], 16 * self.ET // self.PARTS)

    def gpsimd(self, pool):
        s = self.s
        pool.wait_ge(self.states_stored, 32)
        pool.wait_ge(s["init"], 2)
        at = bass.IndirectOffsetOnAxis
        N = self.ET // self.PARTS
        for part, d in enumerate(self.dma):
          with pool.Fori(0, N) as n:
            i = n + part * N
            held(pool, s["v"], i * self.V + 3)
            pool.indirect_dma_start(out=self.rs[:], out_offset=None, in_=self.row_d, in_offset=at(ap=self.isrc[:], axis=0),
                                    bounds_check=self.M - 1, oob_is_err=False).then_inc(d["rows"], 16)
            pool.indirect_dma_start(out=self.so[:], out_offset=None, in_=self.st_d, in_offset=at(ap=self.idst[:], axis=0),
                                    bounds_check=self.M - 1, oob_is_err=False).then_inc(d["states"], 16)
            held(pool, s["v"], i * self.V + self.V)
            pool.indirect_dma_start(out=self.st_d, out_offset=at(ap=self.iwr[:], axis=0), in_=self.sn[:], in_offset=None,
                                    bounds_check=self.M - 1, oob_is_err=False).then_inc(d["wr"], 16)
            held(pool, d["wr"], n * 16 + 16)

    def scalar(self, act):
        s = self.s
        with act.Fori(0, self.ET) as i:
            act.wait_ge(s["v"], i * self.V + 12)
            act.activation(self.ex[:], self.df[:], ACT.Exp).then_inc(s["exp"], 1)

    def tensor(self, pe):
        s, b, H = self.s, self.banks, self.HEADS
        with pe.Fori(0, self.ET) as i:
            pe.wait_ge(s["v"], i * self.V + 3)
            pe.matmul(b[0][:, 0:P], self.dstf[:].broadcast_to([P, P]), self.ident[:], start=True, stop=True).then_inc(s["eq_ps"], 1)
            pe.wait_ge(s["v"], i * self.V + 5)
            for h in range(H):
                mm = pe.matmul(b[1][:, h * P:(h + 1) * P], self.ee[:, 1, h:h + 1].broadcast_to([P, P]), self.ident[:], start=True, stop=True)
            mm.then_inc(s["eT_ps"], 1)
            pe.wait_ge(s["v"], i * self.V + 14)
            pe.matmul(b[2][:, 0:self.HE + H], self.eq[:], self.vv[:], start=True, stop=True).then_inc(s["sum_ps"], 1)

    def vector(self, v):
        s, b, H, HE, M = self.s, self.banks, self.HEADS, self.HE, self.M
        NE = HE // H
        v.memset(self.rs[:], 0.0).then_inc(s["init"], 1)
        v.memset(self.so[:], 0.0).then_inc(s["init"], 1)
        rs, so, sn, ee, eq, pen, msk = self.rs, self.so, self.sn, self.ee, self.eq, self.pen, self.msk
        N = self.ET // self.PARTS
        for part, d in enumerate(self.dma):
          with v.Fori(0, N) as n:
            i = n + part * N
            c = [0]

            def do(ins, wait=True):
                ins.then_inc(s["v"], 1)
                c[0] += 1
                if wait:
                    held(v, s["v"], i * self.V + c[0])
            held(v, s["ld"], i * 32 + 32)
            do(v.tensor_scalar(self.isrc[:], self.ends[:, 0:1], float(M - 1), None, ALU.min), False)
            do(v.tensor_copy(self.idst[:], self.ends[:, 1:2]), False)
            do(v.tensor_copy(self.dstf[:], self.ends[:, 1:2]))
            held(v, d["rows"], n * 16 + 16)
            held(v, d["states"], n * 16 + 16)
            do(v.tensor_tensor(ee[:, 0, :], rs[:, HE:HE + H], so[:, HE + 2 * H:], ALU.add))
            do(v.scalar_tensor_tensor(out=ee[:, 1, :], in0=ee[:, 0, :], scalar=0.2, in1=ee[:, 0, :], op0=ALU.mult, op1=ALU.max), False)
            held(v, s["eq_ps"], i + 1)
            do(v.tensor_scalar(eq[:], b[0][:, 0:P], self.dstf[:], None, ALU.is_equal))
            do(v.tensor_scalar(pen[:], eq[:], BIG, -BIG, ALU.mult, ALU.add))
            held(v, s["eT_ps"], i + 1)
            do(v.tensor_tensor(msk[:], b[1][:].rearrange("p (h j) -> p h j", h=H), pen[:].unsqueeze(1).broadcast_to([P, H, P]), ALU.add))
            do(v.tensor_reduce(self.tm[:], msk[:], AX.X, ALU.max))
            do(v.tensor_tensor(sn[:, HE + H:HE + 2 * H], so[:, HE + H:HE + 2 * H], self.tm[:], ALU.max))
            do(v.tensor_tensor(self.df[:, 0, :], ee[:, 1, :], sn[:, HE + H:HE + 2 * H], ALU.subtract), False)
            do(v.tensor_tensor(self.df[:, 1, :], so[:, HE + H:HE + 2 * H], sn[:, HE + H:HE + 2 * H], ALU.subtract), False)
            held(v, s["exp"], i + 1)
            do(v.tensor_copy(self.vv[:, HE:], self.ex[:, 0, :]), False)
            he = lambda a: a.rearrange("p (h e) -> p h e", h=H)
            do(v.tensor_tensor(he(self.vv[:, 0:HE]), he(rs[:, 0:HE]), self.ex[:, 0, :].unsqueeze(2).broadcast_to([P, H, NE]), ALU.mult), False)
            do(v.tensor_tensor(he(self.oc[:, 0:HE]), he(so[:, 0:HE]), self.ex[:, 1, :].unsqueeze(2).broadcast_to([P, H, NE]), ALU.mult), False)
            do(v.tensor_tensor(self.oc[:, HE:], so[:, HE:HE + H], self.ex[:, 1, :], ALU.mult), False)
            do(v.tensor_tensor(pen[:], eq[:], self.lower[:], ALU.mult))
            do(v.tensor_reduce(self.cnt[:], pen[:], AX.X, ALU.add))
            do(v.scalar_tensor_tensor(out=self.iwr[:], in0=self.cnt[:], scalar=65536.0, in1=self.dstf[:], op0=ALU.mult, op1=ALU.add), False)
            do(v.tensor_copy(sn[:, HE + 2 * H:], so[:, HE + 2 * H:]))
            held(v, s["sum_ps"], i + 1)
            do(v.tensor_tensor(sn[:, 0:HE + H], self.oc[:], b[2][:, 0:HE + H], ALU.add))
            assert c[0] == self.V


_INS = ["x", "cbT", "cb", "wgat", "att", "b_gat", "gamma", "beta", "w1", "b1", "w2", "b2", "edges"]


def kernel(x, L0_conv_codebook, L0_ffn_W_gat, L0_ffn_att_src, L0_ffn_att_dst, L0_ffn_b_gat, L0_ffn_ln_gamma,
           L0_ffn_ln_beta, L0_ffn_W1, L0_ffn_b1, L0_ffn_W2, L0_ffn_b2, L0_ffn_edge_index):
    import numpy as np
    import concourse.bacc as bacc
    from concourse.bass_utils import run_bass_kernel_spmd

    B, C, H, W = x.shape
    arrays = {
        "x": np.ascontiguousarray(np.asarray(x).reshape(B, C, H * W).transpose(0, 2, 1).reshape(B * H * W, C)),
        "cbT": np.ascontiguousarray(np.asarray(L0_conv_codebook).T),
        "cb": np.ascontiguousarray(L0_conv_codebook),
        "wgat": np.ascontiguousarray(L0_ffn_W_gat),
        "att": np.stack([np.asarray(L0_ffn_att_src).reshape(-1), np.asarray(L0_ffn_att_dst).reshape(-1)]),
        "b_gat": np.ascontiguousarray(L0_ffn_b_gat),
        "gamma": np.ascontiguousarray(L0_ffn_ln_gamma),
        "beta": np.ascontiguousarray(L0_ffn_ln_beta),
        "w1": np.ascontiguousarray(np.asarray(L0_ffn_W1).transpose(1, 0, 2)),
        "b1": np.ascontiguousarray(np.asarray(L0_ffn_b1).reshape(-1, P).T),
        "w2": np.ascontiguousarray(L0_ffn_W2),
        "b2": np.ascontiguousarray(L0_ffn_b2),
        "edges": np.ascontiguousarray(L0_ffn_edge_index),
    }
    nc = bacc.Bacc("TRN2", target_bir_lowering=False, num_devices=1)
    aps = [nc.dram_tensor(n, arrays[n].shape, mybir.dt.from_np(arrays[n].dtype), kind="ExternalInput").ap() for n in _INS]
    out = nc.dram_tensor("out", (B * H * W, C), mybir.dt.float32, kind="ExternalOutput").ap()
    metaformer(nc, *aps, out)
    r = run_bass_kernel_spmd(nc, [arrays], core_ids=[0])
    got = r.results[0]["out"]
    return np.ascontiguousarray(got.reshape(B, H * W, C).transpose(0, 2, 1).reshape(B, C, H, W))
```

```python
from contextlib import ExitStack

import concourse.bass as bass
from concourse import mybir

ALU = mybir.AluOpType
ACT = mybir.ActivationFunctionType
AX = mybir.AxisListType
F32 = mybir.dt.float32
BF16 = mybir.dt.bfloat16
I32 = mybir.dt.int32
U32 = mybir.dt.uint32
RMAX = bass.bass_isa.ReduceOp.max

P = 128
BANK = 512
BIG = 2.0 ** 100
SPREAD = 60.0

NODE_BITS = 14
LOW_BITS = 7
CHUNK = 256
COUNTED = 88
TRUE = 40
GROUPS = 8
PLACES = 104
BATCH = 13
HOT = 8


KEYS = 10
V_PREP = 8 + 2 * (COUNTED + TRUE) // 8 - 2 + 8
ROUNDS_C = [(0, 3), (3, 6), (6, 9), (9, 11)]
HOT_AT = [(0, 3), (3, 6), (6, 9), (9, 11)]
V_EXT = 1 + 2 * BATCH - 1 + 6
EXT_AT = [(0, 1)] + [(2 * q - 1, 2 * q + 1) for q in range(1, 7)] + [(13, 13)]
GROUP_LEAST = 2.0 ** -67


GATES = 44


class Tile:

    def __init__(self, j, r, unroll):
        self.j, self.r, self.unroll = j, r, unroll

    def back(self, n):
        return Tile(self.j, self.r - n, self.unroll)

    def slot(self, n):
        return self.r % n

    def n(self, per=1, plus=0):
        return self.j * (self.unroll * per) + (self.r * per + plus)

    def dmas(self, n, each=16):
        return self.j * (each * self.unroll // n) + each * (self.r // n + 1)


def held(eng, sem, value):
    eng.wait_ge(sem, value)
    eng.nop(nofuse=True)


def steps(eng, tiles, depth, step, unroll=4):
    first = -(-depth // unroll) * unroll
    for s in range(first):
        step(Tile(0, s, unroll), lambda k, s=s: 0 <= s - k < tiles)
    with eng.Fori(first // unroll, tiles // unroll) as j:
        for r in range(unroll):
            step(Tile(j, r, unroll), lambda k: True)
    for s in range(tiles, tiles + depth):
        step(Tile(tiles // unroll, s - tiles, unroll), lambda k, s=s: 0 <= s - k < tiles)


def metaformer(nc, x, cbT, cb, wgat, att, b_gat, gamma, beta, w1, b1, w2, b2, edges, out):
    M, D = x.shape
    NC = D // P
    K = cb.shape[0]
    _, NE, F = w1.shape
    FC = F // P
    NF = NE * FC
    HE = wgat.shape[1]
    HEADS = HE // NE
    E = edges.shape[1]
    NT = M // P
    G = BANK // P
    NG = M // BANK
    ET = E // P
    QN = K // BANK
    ROW = HE + 2 * HEADS
    SUM = HE + HEADS
    ST = HE + 3 * HEADS
    CHUNKS = E // P // CHUNK
    assert M == 1 << NODE_BITS and CHUNKS * 4 == NT
    CODES = CHUNKS * TRUE
    HB = COUNTED // HOT
    GB = NT // GROUPS
    SB = PLACES // BATCH
    NB = GROUPS * SB

    t_d = nc.dram_tensor("t_scratch", [M, D], F32, kind="Internal").ap()
    tnT_d = nc.dram_tensor("tnT_scratch", [P, NC, M], F32, kind="Internal").ap()
    row_d = nc.dram_tensor("node_rows", [M, ROW], F32, kind="Internal").ap()
    st_d = nc.dram_tensor("node_states", [M, ST], F32, kind="Internal").ap()

    with ExitStack() as ctx:
        def sb(name, shape, dt=F32):
            return ctx.enter_context(nc.sbuf_tensor(name, shape, dt))

        def ps(name, shape):
            return ctx.enter_context(nc.psum_tensor(name, shape, F32))

        def sem(name):
            return ctx.enter_context(nc.semaphore(name))

        ident = sb("ident", [P, P])
        iota = sb("iota", [P, P])
        iotab = sb("iotab", [P, P, HOT], BF16)
        xor_i = sb("xor_i", [P, GROUPS + 1], I32)
        ones3 = sb("ones3", [3, P], BF16)
        sel3 = sb("sel3", [3, 3])
        halves = sb("halves", [P, 3])
        zero_b = sb("zero_b", [P, P], BF16)
        eps_c = sb("eps_c", [P, 1])
        eps_t = sb("eps_t", [P, 1])
        w1_s = sb("w1_s", [P, NC, NE, F])
        w2_s = sb("w2_s", [P, NF, D])
        wg_s = sb("wg_s", [P, NC, HE])
        att_s = sb("att_s", [P, 2, HE])
        b1_s = sb("b1_s", [P, NF])
        gbb = sb("gbb", [P, 3, HE])
        nrm3 = sb("nrm3", [3, K], BF16)
        b23 = sb("b23", [3, NE * D], BF16)
        room = sb("room", [P, 2 * K + 2 * K + 512])
        cbT_s = room[:, 0:NC * K].rearrange("p (c k) -> p c k", c=NC)
        sc = room[:, NC * K:(NC + 2) * K].rearrange("p (b k) -> p b k", b=2)
        room2 = sb("room2", [P, 2 * 4 * D + 6 * 2 * D])

        def carve(at, words, **shape):
            a = room2[:, at:at + words]
            return a.rearrange("p (" + " ".join(shape) + ") -> p " + " ".join(shape), **shape)
        xt = carve(0, 4 * D, b=4, d=D)
        stat = sb("stat", [P, 2, 6])
        mv = sb("mv", [P, 2, 2])
        std = sb("std", [P, 2])
        rstd = sb("rstd", [P, 2])
        xn = carve(4 * D, 4 * D, b=4, d=D)
        zT = sb("zT", [P, 2, NC, P])
        mx = sb("mx", [P, 2, 8])
        ix = sb("ix", [P, 2, 8], U32)
        zq, zd, zs, tt, tn = (carve((8 + 2 * k) * D, 2 * D, b=2, d=D) for k in range(5))
        tnT = carve(18 * D, 2 * D, b=2, c=NC, t=P)
        stat2 = sb("stat2", [P, 2, 6])
        mv2 = sb("mv2", [P, 2, 2])
        std2 = sb("std2", [P, 2])
        rstd2 = sb("rstd2", [P, 2])
        T = sb("T", [P, NT, ROW])
        prod = sb("prod", [P, 2, 2, HE])
        ends = sb("ends", [P, 2, CHUNK], I32)
        any_i = sb("any_i", [P, CHUNK], I32)
        code_i = sb("code_i", [P, CHUNK], I32)
        keyt = sb("keyt", [P, CHUNK])
        keyc = sb("keyc", [P, CHUNK])
        gone = sb("gone", [P, CHUNK])
        gott = sb("gott", [P, TRUE])
        gotc = sb("gotc", [P, COUNTED])
        cnt_i = sb("cnt_i", [P, COUNTED], I32)
        cnt_b = sb("cnt_b", [P, 2, COUNTED], I32)
        blk = sb("blk", [P, COUNTED], BF16)
        low = sb("low", [P, COUNTED], BF16)
        hotA = sb("hotA", [P, 2, P, HOT], BF16)
        hotB = sb("hotB", [P, 2, P, HOT], BF16)
        over = sb("over", [P, 4])
        codes = sb("codes", [P, CODES])
        cnt = sb("cnt", [P, NT])
        left = sb("left", [P, CODES])
        gotg = sb("gotg", [P, PLACES])
        src_i = sb("src_i", [P, 2, PLACES], I32)
        part_i = sb("part_i", [P, 2, PLACES], I32)
        lowg = sb("lowg", [P, 2, PLACES])
        blkg = sb("blkg", [P, 2, PLACES])
        rows = carve(8 * D, 4 * BATCH * ROW, b=4, t=BATCH, k=ROW)
        adst = sb("adst", [P, NT, HEADS])
        gm = sb("gm", [P, 4, HEADS])
        lastn = sb("lastn", [P, ROW])
        hotm = sb("hotm", [P, 4, BATCH, GB])
        adm = carve(8 * D + 4 * BATCH * ROW, BATCH * GB * HEADS, t=BATCH, m=GB, h=HEADS)
        ea = sb("ea", [P, 6, BATCH, HEADS])
        wgt = sb("wgt", [P, 2, BATCH, HEADS])
        msg = sb("msg", [P, 2, BATCH, SUM])
        outer = room[:, 0:2 * BATCH * GB * SUM].rearrange("p (b t m k) -> p b t m k", b=2, t=BATCH, m=GB)
        S = room[:, 2 * K:2 * K + NT * ST].rearrange("p (i k) -> p i k", k=ST)
        gA, gB = (room[:, k * NT * HE:(k + 1) * NT * HE].rearrange("p (i k) -> p i k", k=HE) for k in range(2))
        sums = sb("sums", [P, NT, SUM])
        g1 = sb("g1", [P, NT])
        g2 = sb("g2", [P, NT])
        sE = sb("sE", [P, NT, NE])
        rk = sb("rk", [P, NT, NE])
        tE = sb("tE", [P, NT, NE])
        gate = sb("gate", [P, NT, NE])
        hh = sb("hh", [P, NF, BANK])
        hv = hh[:].rearrange("p f n -> p (f n)")
        hotl = hv[:, 0:2 * BATCH * P].rearrange("p (b t n) -> p b t n", b=2, t=BATCH)
        hotT = hv[:, 2 * BATCH * P:4 * BATCH * P].rearrange("p (b t n) -> p b t n", b=2, t=BATCH)
        n3, rest, b2f, part = hv[0:3, 0:K], hv[0:3, K:2 * K], hv[0:3, 2 * K:2 * K + NE * D], hv[0:3, 3 * K:4 * K].bitcast(BF16)
        tnG = carve(0, 2 * NC * BANK, b=2, c=NC, n=BANK)
        tG = room[:, 0:2 * G * D].rearrange("p (b k d) -> p b k d", b=2, k=G)
        acc = sb("acc", [P, 2, D])
        flag = sb("flag", [P, 3])
        flag_i = sb("flag_i", [P, 1], I32)

        banks = [ps(f"bank{i}", [P, BANK]) for i in range(8)]

        names = """const wld nrm_sq nrm_ps n_chain d_stat d_mv a_std d_rstd xn_ready pzT zT_ready
        sc_ready sc_evac d_mx ix_ready z_diff z_st t_ready d_stat2 d_mv2 a_std2 d_rstd2 tn_ready ptT tnT_ready
        h_ps h_evac d_prod row_ready prep hot_ready hot_used cnt_ps
        node last_ld node_max flag_ready zone extract hot_l hot_m hT_ps hT_evac ad_ps ad_sum scores
        wgt_ready msg_ready outer_ready sum_ps sum_ready e_chain m_chain m_exp""".split()
        s = {n: sem(n) for n in names}
        x_ld = [sem(f"x_ld{i}") for i in range(4)]
        zq_ld = [sem(f"zq_ld{i}") for i in range(2)]
        t_st = [sem(f"t_st{i}") for i in range(2)]
        tnT_st = [sem(f"tnT_st{i}") for i in range(2)]
        row_st = [sem(f"row_st{i}") for i in range(2)]
        ends_ld = sem("ends_ld")
        rows_ld = [sem(f"rows_ld{i}") for i in range(4)]
        tnG_ld = [sem(f"tnG_ld{i}") for i in range(2)]
        tG_ld = [sem(f"tG_ld{i}") for i in range(2)]
        out_st = [sem(f"out_st{i}") for i in range(2)]
        g_chain, g_exp, g_sq = sem("g_chain"), sem("g_exp"), sem("g_sq")
        w_ps, hh_ready, y_ps, acc_chain, acc_ready = (sem(n) for n in
                                                      ("w_ps", "hh_ready", "y_ps", "acc_chain", "acc_ready"))

        GENERAL = general_path(nc, room, sem, banks, row_d, st_d, edges, ident, M, ROW, ST, HE, HEADS, ET, T, S, sums)

        T_v = T[:].rearrange("p i k -> p (i k)")
        adst_v = adst[:].rearrange("p i h -> p (i h)")
        ALL_T = 16 * NT // 2
        block = ctx.enter_context(nc.Block())

        @block.sync
        def _(sp):
            sp.dma_start(cbT_s, cbT.rearrange("(c p) k -> p c k", p=P)).then_inc(s["wld"], 16)
            sp.dma_start(wg_s[:], wgat.rearrange("(c p) h -> p c h", p=P)).then_inc(s["wld"], 16)
            sp.dma_start(att_s[:], att.rearrange("(o a) h -> o a h", o=1).broadcast_to([P, 2, HE])).then_inc(s["wld"], 16)
            for k, v in enumerate((b_gat, gamma, beta)):
                sp.dma_start(gbb[:, k, :], v.rearrange("(o h) -> o h", o=1).broadcast_to([P, HE])).then_inc(s["wld"], 16)
            sp.dma_start(b2f, b2.rearrange("(o e) d -> o (e d)", o=1).broadcast_to([3, NE * D])).then_inc(s["wld"], 16)
            sp.dma_start(b1_s[:], b1).then_inc(s["wld"], 16)
            sp.dma_start(w1_s[:], w1.rearrange("(c p) e f -> p c e f", p=P)).then_inc(s["wld"], 16)
            sp.dma_start(w2_s[:], w2.rearrange("e (c p) d -> p (e c) d", p=P)).then_inc(s["wld"], 16)

            edges_v = edges.rearrange("a (p e) -> p a e", p=P)

            def step(i, live):
                if live(0):
                    if live(4):
                        held(sp, s["t_ready"], i.back(4).n(1, 1))
                    sp.dma_start(xt[:, i.slot(4), :], x[bass.ds(i.n(P), P), :]).then_inc(x_ld[i.slot(4)], 16)
                    if i.r == 0:
                        if live(4):
                            held(sp, s["prep"], (i.j - 1) * V_PREP + KEYS)
                        sp.dma_start(ends[:], edges_v[:, :, bass.ds(i.j * CHUNK, CHUNK)]).then_inc(ends_ld, 16)
                if live(3):
                    k = i.back(3)
                    held(sp, s["t_ready"], k.n(1, 1))
                    sp.dma_start(t_d[bass.ds(k.n(P), P), :], tt[:, k.slot(2), :]).then_inc(t_st[k.slot(2)], 16)
                    held(sp, s["tnT_ready"], k.n(1, 1))
                    sp.dma_start(tnT_d[:, :, bass.ds(k.n(P), P)], tnT[:, k.slot(2), :, :]).then_inc(tnT_st[k.slot(2)], 16)
                    held(sp, s["row_ready"], k.n(1, 1))
                    sp.dma_start(row_d[bass.ds(k.n(P), P), :], T_v[:, bass.ds(k.n(ROW), ROW)]).then_inc(row_st[k.slot(2)], 16)
            steps(sp, NT, 3, step)
            for q in t_st + tnT_st + row_st:
                sp.wait_ge(q, ALL_T)
            sp.dma_start(lastn[:], row_d[M - 1:M, :].broadcast_to([P, ROW])).then_inc(s["last_ld"], 16)
            sp.wait_ge(s["flag_ready"], 1)
            bad = sp.value_load(flag_i[0:1, 0:1], min_val=0, max_val=1)
            with sp.If(bad > 0):
                GENERAL.sync(sp)

            def group(i, live):
                if live(0):
                    b = i.slot(2)
                    if live(2):
                        held(sp, w_ps, i.back(2).n(NF, NF))
                        held(sp, acc_ready, i.back(2).n(G, G))
                    sp.dma_start(tnG[:, b, :, :], tnT_d[:, :, bass.ds(i.n(BANK), BANK)]).then_inc(tnG_ld[b], 16)
                    if not live(1):
                        sp.wait_ge(g_chain, GATES)
                    sp.dma_start(tG[:, b, :, :], t_d[bass.ds(i.n(BANK), BANK), :].rearrange("(k p) d -> p k d", p=P)).then_inc(tG_ld[b], 16)
                if live(1):
                    g = i.back(1)
                    for k in range(G):
                        held(sp, acc_ready, g.n(G, k + 1))
                        sp.dma_start(out[bass.ds(g.n(BANK, k * P), P), :], acc[:, k % 2, :]).then_inc(out_st[k % 2], 16)
            steps(sp, NG, 2, group)
            for q in out_st:
                sp.wait_ge(q, ALL_T)

        @block.gpsimd
        def _(pool):
            pool.memset(ident[:], 0.0).then_inc(s["const"], 1)
            pool.memset(ones3[:], 1.0).then_inc(s["const"], 1)
            pool.memset(halves[:], -0.5).then_inc(s["const"], 1)
            pool.memset(eps_c[:], 1e-6).then_inc(s["const"], 1)
            pool.memset(eps_t[:], 1e-5).then_inc(s["const"], 1)
            pool.memset(sel3[:], 0.0).then_inc(s["const"], 1)
            pool.iota(iota[:], [[1, P]], base=0, channel_multiplier=0, allow_small_or_imprecise_dtypes=True).then_inc(s["const"], 1)
            pool.iota(iotab[:], [[1, P], [0, HOT]], base=0, channel_multiplier=0, allow_small_or_imprecise_dtypes=True).then_inc(s["const"], 1)
            pool.iota(xor_i[:], [[-1, GROUPS + 1]], base=GROUPS - 1, channel_multiplier=0).then_inc(s["const"], 1)
            pool.wait_ge(s["const"], 9)
            pool.affine_select(out=ident[:], in_=ident[:], compare_op=ALU.not_equal, fill=1.0, base=0,
                               pattern=[[-1, P]], channel_multiplier=1).then_inc(s["const"], 1)
            pool.affine_select(out=sel3[:], in_=sel3[:], compare_op=ALU.not_equal, fill=1.0, base=0,
                               pattern=[[-1, 3]], channel_multiplier=1).then_inc(s["const"], 1)

            def step(i, live):
                if live(1):
                    k = i.back(1)
                    b = k.slot(2)
                    held(pool, s["ix_ready"], k.n(1, 1))
                    if live(3):
                        held(pool, s["z_diff"], k.back(2).n(1, 1))
                    pool.indirect_dma_start(out=zq[:, b, :], out_offset=None, in_=cb,
                                            in_offset=bass.IndirectOffsetOnAxis(ap=ix[:, b, 0:1], axis=0),
                                            bounds_check=K - 1, oob_is_err=False).then_inc(zq_ld[b], 16)
                    held(pool, zq_ld[b], k.dmas(2))
                    if live(3):
                        held(pool, s["z_st"], k.back(2).n(1, 1))
                    pool.tensor_tensor(zd[:, b, :], zq[:, b, :], xn[:, k.slot(4), :], ALU.subtract).then_inc(s["z_diff"], 1)
                    held(pool, s["z_diff"], k.n(1, 1))
                    if live(3):
                        held(pool, s["t_ready"], k.back(2).n(1, 1))
                    pool.tensor_tensor(zs[:, b, :], xn[:, k.slot(4), :], zd[:, b, :], ALU.add).then_inc(s["z_st"], 1)
            steps(pool, NT, 3, step)

            pool.wait_ge(s["node"], 3)
            pool.partition_all_reduce(gm[:, 2:4, :].rearrange("p a h -> p (a h)"), gm[:, 0:2, :].rearrange("p a h -> p (a h)"), P, RMAX).then_inc(s["node_max"], 1)
            for q in row_st + t_st + tnT_st:
                pool.wait_ge(q, ALL_T)

            def batch(i, live):
                if live(0):
                    if i.r % SB == 0:
                        held(pool, s["extract"], i.j * (2 * V_EXT) + ((i.r // SB + 1) * V_EXT + 1))
                    if live(4):
                        held(pool, s["msg_ready"], i.back(4).n(1, 1))
                    g = i.r // SB % 2
                    for t in range(BATCH):
                        c = i.r % SB * BATCH + t
                        pool.indirect_dma_start(out=rows[:, i.slot(4), t, :], out_offset=None, in_=row_d,
                                                in_offset=bass.IndirectOffsetOnAxis(ap=src_i[:, g, c:c + 1].bitcast(U32), axis=0),
                                                bounds_check=M - 1, oob_is_err=False).then_inc(rows_ld[i.slot(4)], 16)
            steps(pool, NB, 3, batch, unroll=2 * SB)
            pool.wait_ge(s["zone"], 1)
            pool.partition_all_reduce(flag[:, 1:2], flag[:, 0:1], P, RMAX).then_inc(s["zone"], 1)
            pool.wait_ge(s["flag_ready"], 1)
            bad = pool.value_load(flag_i[0:1, 0:1], min_val=0, max_val=1)
            with pool.If(bad > 0):
                GENERAL.gpsimd(pool)

        @block.scalar
        def _(act):
            act.wait_ge(s["wld"], 160)
            for c in range(NC):
                act.activation(sc[:, c, :], cbT_s[:, c, :], ACT.Square).then_inc(s["nrm_sq"], 1)

            def step(i, live):
                if live(0):
                    act.wait_ge(s["d_mv"], i.n(1, 1))
                    if live(2):
                        act.wait_ge(s["d_rstd"], i.back(2).n(1, 1))
                    act.activation(std[:, i.slot(2):i.slot(2) + 1], mv[:, i.slot(2), 1:2], ACT.Sqrt, bias=eps_c[:]).then_inc(s["a_std"], 1)
                if live(2):
                    k = i.back(2)
                    b = k.slot(2)
                    act.wait_ge(s["d_mv2"], k.n(1, 1))
                    if live(4):
                        act.wait_ge(s["d_rstd2"], k.back(2).n(1, 1))
                    act.activation(std2[:, b:b + 1], mv2[:, b, 1:2], ACT.Sqrt, bias=eps_t[:]).then_inc(s["a_std2"], 1)
                if live(0):
                    b = i.slot(2)
                    act.wait_ge(s["pzT"], i.n(1, 1))
                    if live(2):
                        act.wait_ge(s["sc_ready"], i.back(2).n(QN, QN))
                    act.activation(zT[:, b, :, :], banks[4][:, 0:D].rearrange("p (c t) -> p c t", c=NC), ACT.Copy).then_inc(s["zT_ready"], 1)
                if live(2):
                    k = i.back(2)
                    b = k.slot(2)
                    act.wait_ge(s["ptT"], k.n(1, 1))
                    if live(4):
                        act.wait_ge(tnT_st[b], k.back(2).dmas(2))
                        act.wait_ge(s["h_ps"], k.back(2).n(1, 1))
                    act.activation(tnT[:, b, :, :], banks[5][:, 0:D].rearrange("p (c t) -> p c t", c=NC), ACT.Copy).then_inc(s["tnT_ready"], 1)
                    act.wait_ge(s["h_ps"], k.n(1, 1))
                    act.activation(T_v[:, bass.ds(k.n(ROW), HE)], banks[6][:, 0:HE], ACT.Copy).then_inc(s["h_evac"], 1)
                if live(0):
                    b = i.slot(2)
                    for q in range(QN):
                        act.wait_ge(s["sc_ready"], i.n(QN, q + 1))
                        if live(2) and q == 0:
                            act.wait_ge(s["ix_ready"], i.back(2).n(1, 1))
                        act.activation(sc[:, b, q * BANK:(q + 1) * BANK], banks[q][:], ACT.Copy).then_inc(s["sc_evac"], 1)
            steps(act, NT, 3, step)

            def batch(i, live):
                if live(2):
                    k = i.back(2)
                    b = k.slot(2)
                    act.wait_ge(s["scores"], k.n(1, 1))
                    if live(4):
                        act.wait_ge(s["msg_ready"], k.back(2).n(1, 1))
                    act.activation(wgt[:, b, :, :], ea[:, 5, :, :], ACT.Exp).then_inc(s["wgt_ready"], 1)
                if live(1):
                    k = i.back(1)
                    b = k.slot(2)
                    if live(3):
                        act.wait_ge(s["ad_ps"], k.back(2).n(2, 2))
                    for q in range(4):
                        t0, t1 = 4 * q, min(4 * q + 4, BATCH)
                        act.wait_ge(s["hT_ps"], k.n(4, q + 1))
                        act.activation(hotT[:, b, t0:t1, :], banks[q][:, 0:(t1 - t0) * P].rearrange("p (t n) -> p t n", n=P), ACT.Copy).then_inc(s["hT_evac"], 1)
            steps(act, NB, 3, batch, unroll=2 * SB)
            act.wait_ge(s["m_exp"], 1)
            act.activation(tE[:], tE[:], ACT.Exp).then_inc(s["m_exp"], 1)
            act.activation(rk[:], rk[:], ACT.Exp).then_inc(s["m_exp"], 1)
            act.wait_ge(s["flag_ready"], 1)
            bad = act.value_load(flag_i[0:1, 0:1], min_val=0, max_val=1)
            with act.If(bad > 0):
                GENERAL.scalar(act)
            act.wait_ge(g_sq, 1)
            act.activation(g2[:], g1[:], ACT.Sqrt, bias=eps_t[:]).then_inc(g_sq, 1)
            act.wait_ge(g_exp, 1)
            act.activation(tE[:], tE[:], ACT.Exp).then_inc(g_exp, 1)

            def group(i, live):
                if live(0):
                    for f in range(NF):
                        act.wait_ge(w_ps, i.n(NF, f + 1))
                        if live(1) and f == 0:
                            act.wait_ge(y_ps, i.back(1).n(G, G))
                        act.activation(hh[:, f, :], banks[f % 4][:], ACT.Gelu, bias=b1_s[:, f:f + 1]).then_inc(hh_ready, 1)
            steps(act, NG, 2, group)

        @block.tensor
        def _(pe):
            pe.wait_ge(s["nrm_sq"], NC)
            pe.wait_ge(s["const"], 11)
            for q in range(QN):
                for c in range(NC):
                    mm = pe.matmul(banks[q][0:3, :], halves[:], sc[:, c, q * BANK:(q + 1) * BANK], start=c == 0, stop=c == NC - 1)
            mm.then_inc(s["nrm_ps"], 1)
            pe.wait_ge(s["n_chain"], QN + 2 * 9)
            pe.wait_ge(s["prep"], 2)
            pe.matmul(banks[7][:, 0:NT], zero_b[:], zero_b[:], start=True, stop=False, skip_group_check=True)

            def counts(j, first, last):
                for h in range(first, last):
                    pe.wait_ge(s["hot_ready"], j * (2 * HB) + 2 * (h + 1))
                    for t in range(HOT):
                        mm = pe.matmul(banks[7][:, 0:NT], hotA[:, h % 2, :, t], hotB[:, h % 2, :, t], start=False, stop=False, skip_group_check=True)
                    mm.then_inc(s["hot_used"], 1)

            def step(i, live):
                if live(0):
                    pe.wait_ge(s["xn_ready"], i.n(1, 1))
                    if live(1):
                        pe.wait_ge(s["zT_ready"], i.back(1).n(1, 1))
                    for c in range(NC):
                        mm = pe.transpose(banks[4][:, c * P:(c + 1) * P], xn[:, i.slot(4), c * P:(c + 1) * P], ident[:])
                    mm.then_inc(s["pzT"], 1)
                if live(2):
                    k = i.back(2)
                    b = k.slot(2)
                    pe.wait_ge(s["tn_ready"], k.n(1, 1))
                    if live(3):
                        pe.wait_ge(s["tnT_ready"], k.back(1).n(1, 1))
                    for c in range(NC):
                        mm = pe.transpose(banks[5][:, c * P:(c + 1) * P], tn[:, b, c * P:(c + 1) * P], ident[:])
                    mm.then_inc(s["ptT"], 1)
                if live(0):
                    h0, h1 = HOT_AT[i.r] if live(4) else (0, 0)
                    pe.wait_ge(s["zT_ready"], i.n(1, 1))
                    for q in range(QN):
                        if q in (1, 2):
                            counts(i.j - 1, min(h0 + q - 1, h1), min(h0 + q, h1))
                        if live(1):
                            pe.wait_ge(s["sc_evac"], i.back(1).n(QN, q + 1))
                        cols = slice(q * BANK, (q + 1) * BANK)
                        pe.matmul(banks[q][:], ones3[:], nrm3[:, cols], start=True, stop=False)
                        for c in range(NC):
                            mm = pe.matmul(banks[q][:], zT[:, i.slot(2), c, :], cbT_s[:, c, cols], start=False, stop=c == NC - 1)
                        mm.then_inc(s["sc_ready"], 1)
                        if q == 0 and live(2):
                            k = i.back(2)
                            pe.wait_ge(s["tnT_ready"], k.n(1, 1))
                            if live(3):
                                pe.wait_ge(s["h_evac"], k.back(1).n(1, 1))
                            for c in range(NC):
                                mm = pe.matmul(banks[6][:, 0:HE], tnT[:, k.slot(2), c, :], wg_s[:, c, :], start=c == 0, stop=c == NC - 1)
                            mm.then_inc(s["h_ps"], 1)
                    counts(i.j - 1, min(h0 + 2, h1), h1)
                elif live(2):
                    k = i.back(2)
                    pe.wait_ge(s["tnT_ready"], k.n(1, 1))
                    pe.wait_ge(s["h_evac"], k.back(1).n(1, 1))
                    for c in range(NC):
                        mm = pe.matmul(banks[6][:, 0:HE], tnT[:, k.slot(2), c, :], wg_s[:, c, :], start=c == 0, stop=c == NC - 1)
                    mm.then_inc(s["h_ps"], 1)
            steps(pe, NT, 3, step)
            counts(CHUNKS - 1, 0, HB)
            pe.matmul(banks[7][:, 0:NT], zero_b[:], zero_b[:], start=False, stop=True, skip_group_check=True).then_inc(s["cnt_ps"], 1)

            pe.wait_ge(s["node"], 4)

            def batch(i, live):
                if live(3):
                    k = i.back(3)
                    b = k.slot(2)
                    pe.wait_ge(s["outer_ready"], k.n(1, 1))
                    if live(5):
                        pe.wait_ge(s["sum_ready"], k.back(2).n(1, 1))
                    for t in range(BATCH):
                        mm = pe.matmul(banks[6 + b][:, 0:GB * SUM], hotl[:, b, t, :], outer[:, b, t, :, :].rearrange("p m k -> p (m k)"), start=t == 0, stop=t == BATCH - 1)
                    mm.then_inc(s["sum_ps"], 1)
                if live(1):
                    k = i.back(1)
                    b = k.slot(2)
                    pe.wait_ge(s["hot_l"], k.n(1, 1))
                    for q in range(4):
                        if live(2):
                            pe.wait_ge(s["hT_evac"], k.back(1).n(4, q + 1))
                        for t in range(4 * q, min(4 * q + 4, BATCH)):
                            mm = pe.transpose(banks[q][:, (t % 4) * P:(t % 4 + 1) * P], hotl[:, b, t, :], ident[:])
                        mm.then_inc(s["hT_ps"], 1)
                if live(1):
                    k = i.back(1)
                    b = k.slot(2)
                    gcol = adst_v[:, bass.ds(k.j * (k.unroll // SB * GB * HEADS) + k.r // SB * GB * HEADS, GB * HEADS)]
                    pe.wait_ge(s["hT_evac"], k.n(4, 4))
                    for t in range(BATCH):
                        if t % 8 == 0 and live(2):
                            pe.wait_ge(s["ad_sum"], k.back(1).n(3, t // 8 + 1))
                        mm = pe.matmul(banks[4 + t // 8][:, (t % 8) * GB * HEADS:(t % 8 + 1) * GB * HEADS], hotT[:, b, t, :], gcol, start=True, stop=True)
                        if t in (7, BATCH - 1):
                            mm.then_inc(s["ad_ps"], 1)
            steps(pe, NB, 3, batch, unroll=2 * SB)
            pe.wait_ge(s["flag_ready"], 1)
            bad = pe.value_load(flag_i[0:1, 0:1], min_val=0, max_val=1)
            with pe.If(bad > 0):
                GENERAL.tensor(pe)

            def group(i, live):
                if live(0):
                    b = i.slot(2)
                    pe.wait_ge(tnG_ld[b], i.dmas(2))
                    for f in range(NF):
                        e, c2 = divmod(f, FC)
                        if f >= 4 or live(1):
                            pe.wait_ge(hh_ready, i.n(NF, f - 3))
                        for c in range(NC):
                            mm = pe.matmul(banks[f % 4][:], w1_s[:, c, e, c2 * P:(c2 + 1) * P], tnG[:, b, c, :], start=c == 0, stop=c == NC - 1)
                        mm.then_inc(w_ps, 1)
                    for k in range(G):
                        y = banks[4 + 2 * (k % 2):6 + 2 * (k % 2)]
                        if k >= 2 or live(1):
                            pe.wait_ge(acc_ready, i.n(G, k - 1))
                        for e in range(NE):
                            yb = y[e // 2][:, (e % 2) * D:(e % 2 + 1) * D]
                            if e % 2 == 0:
                                pe.matmul(y[e // 2][:], ones3[:], b23[:, e * D:(e + 2) * D], start=True, stop=False, skip_group_check=True)
                            for c2 in range(FC):
                                f = e * FC + c2
                                if k == 0:
                                    pe.wait_ge(hh_ready, i.n(NF, f + 1))
                                mm = pe.matmul(yb, hh[:, f, k * P:(k + 1) * P], w2_s[:, f, :], start=False, stop=c2 == FC - 1, skip_group_check=True)
                        mm.then_inc(y_ps, 1)
            steps(pe, NG, 2, group)

        @block.vector
        def _(v):
            def split(dst, src, n, chain, at):
                for k in range(3):
                    v.tensor_copy(part[:, 0:n], rest[:, 0:n] if k else src).then_inc(chain, 1)
                    at += 1
                    v.wait_ge(chain, at)
                    if k == 0:
                        v.tensor_scalar(dst[:], part[:, 0:n], sel3[:, 0:1], None, ALU.mult).then_inc(chain, 1)
                    else:
                        v.scalar_tensor_tensor(out=dst[:], in0=part[:, 0:n], scalar=sel3[:, k:k + 1], in1=dst[:], op0=ALU.mult, op1=ALU.add).then_inc(chain, 1)
                    v.tensor_tensor(rest[:, 0:n], rest[:, 0:n] if k else src, part[:, 0:n], ALU.subtract).then_inc(chain, 1)
                    at += 2
                    v.wait_ge(chain, at)
                return at

            v.memset(over[:], 0.0).then_inc(s["prep"], 1)
            v.memset(zero_b[:], 0.0).then_inc(s["prep"], 1)
            v.wait_ge(s["nrm_ps"], 1)
            for q in range(QN):
                v.tensor_copy(n3[:, q * BANK:(q + 1) * BANK], banks[q][0:3, :]).then_inc(s["n_chain"], 1)
            v.wait_ge(s["n_chain"], QN)
            v.wait_ge(s["const"], 11)
            v.tensor_scalar(xor_i[:], xor_i[:], 2 * NODE_BITS - 3, None, ALU.logical_shift_left).then_inc(s["extract"], 1)
            at = split(nrm3, n3, K, s["n_chain"], QN)
            v.wait_ge(s["wld"], 160)
            split(b23, b2f, NE * D, s["n_chain"], at)

            class Prep:

                def __init__(self):
                    self.n = 2

                def did(self, j, ins):
                    ins.then_inc(s["prep"], 1)
                    self.n += 1
                    return self.n

                def wait(self, j, n):
                    held(v, s["prep"], j * V_PREP + n)

            prep = Prep()
            done = {}

            def sort_out(j, r):
                if r == 0:
                    prep.n = 2
                    held(v, ends_ld, j * 16 + 16)
                    src, dst = ends[:, 0, :], ends[:, 1, :]
                    prep.did(j, v.tensor_tensor(any_i[:], src, dst, ALU.bitwise_or))
                    n1 = prep.did(j, v.tensor_scalar(code_i[:], dst, NODE_BITS, 1 << 2 * NODE_BITS, ALU.logical_shift_left, ALU.bitwise_or))
                    prep.did(j, v.tensor_scalar(gone[:], src, float(M), None, ALU.is_ge))
                    n2 = prep.did(j, v.tensor_scalar(keyc[:], dst, 1.0, None, ALU.add))
                    prep.wait(j, n1)
                    n3_ = prep.did(j, v.tensor_tensor(code_i[:], code_i[:], src, ALU.bitwise_or))
                    prep.wait(j, n2)
                    n4 = prep.did(j, v.tensor_tensor(keyc[:], keyc[:], gone[:], ALU.mult))
                    prep.wait(j, n3_)
                    done["t"] = prep.did(j, v.scalar_tensor_tensor(out=keyt[:], in0=any_i[:], scalar=float(M), in1=code_i[:].bitcast(F32), op0=ALU.is_lt, op1=ALU.mult))
                    prep.wait(j, n4)
                    done["c"] = prep.did(j, v.scalar_tensor_tensor(out=keyc[:], in0=dst, scalar=float(M), in1=keyc[:], op0=ALU.is_lt, op1=ALU.mult))
                    assert prep.n == KEYS
                for k in range(*ROUNDS_C[r]):
                    prep.wait(j, done["c"])
                    done["c"] = prep.did(j, v.max(gotc[:, 8 * k:8 * k + 8], keyc[:]))
                    if k < TRUE // 8:
                        prep.wait(j, done["t"])
                        done["t"] = prep.did(j, v.max(gott[:, 8 * k:8 * k + 8], keyt[:]))
                    if k < COUNTED // 8 - 1:
                        prep.wait(j, done["c"])
                        done["c"] = prep.did(j, v.match_replace(keyc[:], gotc[:, 8 * k:8 * k + 8], keyc[:], 0.0))
                    if k < TRUE // 8 - 1:
                        prep.wait(j, done["t"])
                        done["t"] = prep.did(j, v.match_replace(keyt[:], gott[:, 8 * k:8 * k + 8], keyt[:], 0.0))

            def finish(j):
                prep.wait(j, done["c"])
                prep.did(j, v.tensor_copy(codes[:, bass.ds(j * TRUE, TRUE)], gott[:]))
                prep.did(j, v.tensor_tensor(over[:, 0:1], over[:, 0:1], gotc[:, COUNTED - 1:COUNTED], ALU.max))
                prep.did(j, v.tensor_tensor(over[:, 1:2], over[:, 1:2], gott[:, TRUE - 1:TRUE], ALU.max))
                n = prep.did(j, v.tensor_scalar(cnt_i[:], gotc[:], 1.0, None, ALU.subtract))
                prep.wait(j, n)
                prep.did(j, v.tensor_scalar(cnt_b[:, 0, :], cnt_i[:], LOW_BITS, None, ALU.arith_shift_right))
                n = prep.did(j, v.tensor_scalar(cnt_b[:, 1, :], cnt_i[:], P - 1, None, ALU.bitwise_and))
                prep.wait(j, n)
                prep.did(j, v.tensor_copy(blk[:], cnt_b[:, 0, :]))
                n = prep.did(j, v.tensor_copy(low[:], cnt_b[:, 1, :]))
                assert n - 2 == V_PREP, n
                prep.wait(j, n)

            def one_hots(j, first, last):
                for h in range(first, last):
                    if h >= 2:
                        held(v, s["hot_used"], j * HB + (h - 1))
                    elif not (isinstance(j, int) and j == 0):
                        held(v, s["hot_used"], j * HB)
                    for dst, bits in ((hotA, low), (hotB, blk)):
                        v.tensor_tensor(dst[:, h % 2, :, :], iotab[:], bits[:, h * HOT:(h + 1) * HOT].unsqueeze(1).broadcast_to([P, P, HOT]), ALU.is_equal).then_inc(s["hot_ready"], 1)

            def step(i, live):
                if live(0):
                    b = i.slot(2)
                    held(v, x_ld[i.slot(4)], i.dmas(4))
                    v.bn_stats(stat[:, b, :], xt[:, i.slot(4), :]).then_inc(s["d_stat"], 1)
                if live(2):
                    k = i.back(2)
                    b = k.slot(2)
                    held(v, s["z_st"], k.n(1, 1))
                    if live(4):
                        held(v, t_st[b], k.back(2).dmas(2))
                    v.tensor_tensor(tt[:, b, :], xt[:, k.slot(4), :], zs[:, b, :], ALU.add).then_inc(s["t_ready"], 1)
                if live(0):
                    b = i.slot(2)
                    held(v, s["d_stat"], i.n(1, 1))
                    if live(2):
                        held(v, s["xn_ready"], i.back(2).n(1, 1))
                        held(v, s["a_std"], i.back(2).n(1, 1))
                    v.bn_aggr(mv[:, b, :], stat[:, b, :]).then_inc(s["d_mv"], 1)
                if live(2):
                    k = i.back(2)
                    b = k.slot(2)
                    held(v, s["t_ready"], k.n(1, 1))
                    v.bn_stats(stat2[:, b, :], tt[:, b, :]).then_inc(s["d_stat2"], 1)
                    held(v, s["d_stat2"], k.n(1, 1))
                    if live(4):
                        held(v, s["tn_ready"], k.back(2).n(1, 1))
                    v.bn_aggr(mv2[:, b, :], stat2[:, b, :]).then_inc(s["d_mv2"], 1)
                if live(1):
                    k = i.back(1)
                    held(v, s["sc_evac"], k.n(QN, QN))
                    v.max(mx[:, k.slot(2), :], sc[:, k.slot(2), :]).then_inc(s["d_mx"], 1)
                if live(0):
                    b = i.slot(2)
                    held(v, s["a_std"], i.n(1, 1))
                    v.reciprocal(rstd[:, b:b + 1], std[:, b:b + 1]).then_inc(s["d_rstd"], 1)
                if live(2):
                    k = i.back(2)
                    b = k.slot(2)
                    held(v, s["a_std2"], k.n(1, 1))
                    v.reciprocal(rstd2[:, b:b + 1], std2[:, b:b + 1]).then_inc(s["d_rstd2"], 1)
                if live(0):
                    b = i.slot(2)
                    held(v, s["d_rstd"], i.n(1, 1))
                    v.tensor_scalar(xn[:, i.slot(4), :], xt[:, i.slot(4), :], mv[:, b, 0:1], rstd[:, b:b + 1], ALU.subtract, ALU.mult).then_inc(s["xn_ready"], 1)
                if live(2):
                    k = i.back(2)
                    b = k.slot(2)
                    held(v, s["d_rstd2"], k.n(1, 1))
                    if live(4):
                        held(v, s["ptT"], k.back(2).n(1, 1))
                    v.tensor_scalar(tn[:, b, :], tt[:, b, :], mv2[:, b, 0:1], rstd2[:, b:b + 1], ALU.subtract, ALU.mult).then_inc(s["tn_ready"], 1)
                h0, h1 = HOT_AT[i.r] if live(0) and live(4) else (0, 0)
                one_hots(i.j - 1, h0, min(h0 + 1, h1))
                if live(1):
                    k = i.back(1)
                    b = k.slot(2)
                    held(v, s["d_mx"], k.n(1, 1))
                    if live(3):
                        held(v, zq_ld[b], k.back(2).dmas(2))
                    v.max_index(ix[:, b, :], mx[:, b, :], sc[:, b, :]).then_inc(s["ix_ready"], 1)
                if live(0):
                    one_hots(i.j - 1, min(h0 + 1, h1), min(h0 + 2, h1))
                    sort_out(i.j, i.r)
                    one_hots(i.j - 1, min(h0 + 2, h1), h1)
                if live(2):
                    k = i.back(2)
                    b = k.slot(2)
                    held(v, s["h_evac"], k.n(1, 1))
                    v.tensor_tensor(prod[:, b, :, :], T_v[:, bass.ds(k.n(ROW), HE)].unsqueeze(1).broadcast_to([P, 2, HE]), att_s[:], ALU.mult).then_inc(s["d_prod"], 1)
                if live(0):
                    if i.r == 3:
                        finish(i.j)
                if live(2):
                    k = i.back(2)
                    b = k.slot(2)
                    held(v, s["d_prod"], k.n(1, 1))
                    v.tensor_reduce(T_v[:, bass.ds(k.n(ROW, HE), 2 * HEADS)], prod[:, b, :, :].rearrange("p a (h e) -> p (a h) e", h=HEADS), AX.X, ALU.add).then_inc(s["row_ready"], 1)
            steps(v, NT, 3, step)

            v.wait_ge(s["row_ready"], NT)
            v.tensor_reduce(gm[:, 0, :], T[:, :, HE:SUM].rearrange("p i h -> p h i"), AX.X, ALU.max).then_inc(s["node"], 1)
            v.tensor_reduce(gm[:, 2, :], T[:, :, HE:SUM].rearrange("p i h -> p h i"), AX.X, ALU.min).then_inc(s["node"], 1)
            v.wait_ge(s["node"], 2)
            v.tensor_scalar(gm[:, 1, :], gm[:, 2, :], -1.0, None, ALU.mult).then_inc(s["node"], 1)
            v.tensor_copy(adst[:], T[:, :, SUM:ROW]).then_inc(s["node"], 1)
            v.memset(sums[:], 0.0).then_inc(s["node"], 1)
            one_hots(CHUNKS - 1, 0, HB)

            class Extract:

                def did(self, g, ins):
                    ins.then_inc(s["extract"], 1)
                    self.n += 1

                def wait(self, g):
                    held(v, s["extract"], g[0] * (2 * V_EXT) + (g[1] * V_EXT + 1 + self.n))

            ex = Extract()

            def extract(g, q, half):
                if q == 0 and half == 0:
                    ex.n = 0
                    ex.wait(g)
                    ex.did(g, v.tensor_scalar(left[:].bitcast(I32), codes[:].bitcast(I32), xor_i[:, bass.ds(g[0] * 2 + g[1], 1)], None, ALU.bitwise_xor))
                a, b = EXT_AT[q]
                mid = (a + b + 1) // 2
                for k in range(a, mid) if half == 0 else range(mid, b):
                    ex.wait(g)
                    ex.did(g, v.max(gotg[:, 8 * k:8 * k + 8], left[:]))
                    if k < BATCH - 1:
                        ex.wait(g)
                        ex.did(g, v.match_replace(left[:], gotg[:, 8 * k:8 * k + 8], left[:], 0.0))
                if q == SB - 1 and half == 1:
                    p = g[1] % 2
                    got = gotg[:].bitcast(I32)
                    ex.wait(g)
                    ex.did(g, v.tensor_tensor(over[:, 2:3], over[:, 2:3], gotg[:, PLACES - 1:PLACES], ALU.max))
                    ex.did(g, v.tensor_scalar(part_i[:, 0, :], got, NODE_BITS, P - 1, ALU.logical_shift_right, ALU.bitwise_and))
                    ex.did(g, v.tensor_scalar(part_i[:, 1, :], got, NODE_BITS + LOW_BITS, None, ALU.logical_shift_right))
                    ex.did(g, v.tensor_scalar(src_i[:, p, :], got, M - 1, None, ALU.bitwise_and))
                    ex.wait(g)
                    ex.did(g, v.tensor_copy(lowg[:, p, :], part_i[:, 0, :]))
                    ex.did(g, v.tensor_scalar(blkg[:, p, :], part_i[:, 1, :], float(2 * NT - GB), None, ALU.subtract))
                    assert ex.n == V_EXT, ex.n

            for q in range(SB):
                extract((0, 0), q, 0)
                extract((0, 0), q, 1)
            v.wait_ge(s["cnt_ps"], 1)
            v.tensor_copy(cnt[:], banks[7][:, 0:NT]).then_inc(s["node"], 1)
            v.wait_ge(s["node_max"], 1)
            for q in t_st + tnT_st:
                v.wait_ge(q, ALL_T)
            sums_v = sums[:].rearrange("p i k -> p (i k)")

            def batch(i, live):
                nxt = (i.j, i.r // SB + 1)
                q = i.r % SB
                if live(2):
                    k = i.back(2)
                    held(v, s["hot_m"], k.n(1, 1))
                    for h in range(2):
                        t0, t1 = 8 * h, min(8 * h + 8, BATCH)
                        held(v, s["ad_ps"], k.n(2, h + 1))
                        v.tensor_tensor(adm[:, t0:t1, :, :], banks[4 + h][:, 0:(t1 - t0) * GB * HEADS].rearrange("p (t m h) -> p t m h", m=GB, h=HEADS),
                                        hotm[:, k.slot(4), t0:t1, :].unsqueeze(3).broadcast_to([P, t1 - t0, GB, HEADS]), ALU.mult).then_inc(s["ad_sum"], 1)
                if live(0):
                    extract(nxt, q, 0)
                if live(2):
                    k = i.back(2)
                    held(v, s["ad_sum"], k.n(3, 2))
                    v.tensor_reduce(ea[:, 0, :, :], adm.rearrange("p t m h -> p t h m"), AX.X, ALU.add).then_inc(s["ad_sum"], 1)
                    held(v, s["ad_sum"], k.n(3, 3))
                    held(v, rows_ld[k.slot(4)], k.dmas(4, 16 * BATCH))
                    r_ = rows[:, k.slot(4), :, :]
                    v.tensor_tensor(ea[:, 1, :, :], r_[:, :, HE:SUM], ea[:, 0, :, :], ALU.add).then_inc(s["e_chain"], 1)
                    v.tensor_tensor(ea[:, 2, :, :], ea[:, 0, :, :], gm[:, 2, :].unsqueeze(1).broadcast_to([P, BATCH, HEADS]), ALU.add).then_inc(s["e_chain"], 1)
                    held(v, s["e_chain"], k.n(5, 2))
                    v.scalar_tensor_tensor(out=ea[:, 3:5, :, :], in0=ea[:, 1:3, :, :], scalar=0.2, in1=ea[:, 1:3, :, :], op0=ALU.mult, op1=ALU.max).then_inc(s["e_chain"], 1)
                    held(v, s["e_chain"], k.n(5, 3))
                    v.tensor_tensor(ea[:, 0, :, :], ea[:, 3, :, :], ea[:, 4, :, :], ALU.subtract).then_inc(s["e_chain"], 1)
                    held(v, s["e_chain"], k.n(5, 4))
                    if live(3):
                        held(v, s["wgt_ready"], k.n(1, 0))
                    v.tensor_scalar(ea[:, 5, :, :], ea[:, 0, :, :], 0.0, None, ALU.min).then_inc(s["scores"], 1)
                if live(0):
                    extract(nxt, q, 1)
                if live(1):
                    k = i.back(1)
                    g, c = k.r // SB % 2, k.r % SB * BATCH
                    held(v, s["extract"], k.j * (2 * V_EXT) + ((k.r // SB + 1) * V_EXT + 1))
                    if live(3):
                        held(v, s["sum_ps"], k.back(2).n(1, 1))
                    v.tensor_tensor(hotl[:, k.slot(2), :, :], iota[:].unsqueeze(1).broadcast_to([P, BATCH, P]),
                                    lowg[:, g, c:c + BATCH].unsqueeze(2).broadcast_to([P, BATCH, P]), ALU.is_equal).then_inc(s["hot_l"], 1)
                    v.tensor_tensor(hotm[:, k.slot(4), :, :], iota[:, 0:GB].unsqueeze(1).broadcast_to([P, BATCH, GB]),
                                    blkg[:, g, c:c + BATCH].unsqueeze(2).broadcast_to([P, BATCH, GB]), ALU.is_equal).then_inc(s["hot_m"], 1)
                if live(3):
                    k = i.back(3)
                    held(v, s["sum_ps"], k.n(1, 1))
                    if live(4):
                        held(v, s["sum_ready"], k.n(1, 0))
                    else:
                        v.wait_ge(s["node"], 5)
                    dst = sums_v[:, bass.ds(k.j * (2 * GB * SUM) + k.r // SB * GB * SUM, GB * SUM)]
                    v.tensor_tensor(dst, banks[6 + k.slot(2)][:, 0:GB * SUM], dst, ALU.add).then_inc(s["sum_ready"], 1)
                if live(2):
                    k = i.back(2)
                    b = k.slot(2)
                    r_ = rows[:, k.slot(4), :, :]
                    held(v, s["wgt_ready"], k.n(1, 1))
                    v.tensor_tensor(msg[:, b, :, 0:HE].rearrange("p t (h e) -> p t h e", h=HEADS), r_[:, :, 0:HE].rearrange("p t (h e) -> p t h e", h=HEADS),
                                    wgt[:, b, :, :].unsqueeze(3).broadcast_to([P, BATCH, HEADS, NE]), ALU.mult).then_inc(s["msg_ready"], 1)
                    v.tensor_copy(msg[:, b, :, HE:SUM], wgt[:, b, :, :]).then_inc(s["e_chain"], 1)
                    held(v, s["msg_ready"], k.n(1, 1))
                    held(v, s["e_chain"], k.n(5, 5))
                    v.tensor_tensor(outer[:, b, :, :, :], hotm[:, k.slot(4), :, :].unsqueeze(3).broadcast_to([P, BATCH, GB, SUM]),
                                    msg[:, b, :, :].unsqueeze(2).broadcast_to([P, BATCH, GB, SUM]), ALU.mult).then_inc(s["outer_ready"], 1)

            steps(v, NB, 3, batch, unroll=2 * SB)
            v.wait_ge(s["sum_ready"], NB)

            m = [0]

            def mlink(ins):
                ins.then_inc(s["m_chain"], 1)
                m[0] += 1
                v.wait_ge(s["m_chain"], m[0])

            def over_nodes(a):
                return a.unsqueeze(1).broadcast_to([P, NT, a.shape[1]])

            def by_head(a):
                return a.rearrange("p i (h e) -> p i h e", h=HEADS)

            def leaky(out_, in_):
                return v.scalar_tensor_tensor(out=out_, in0=in_, scalar=0.2, in1=in_, op0=ALU.mult, op1=ALU.max)

            v.wait_ge(s["last_ld"], 16)
            mlink(v.tensor_tensor(sE[:], adst[:], over_nodes(gm[:, 2, :]), ALU.add))
            mlink(leaky(gate[:], sE[:]))
            mlink(v.tensor_tensor(sE[:], T[:, :, HE:SUM], adst[:], ALU.add))
            mlink(leaky(tE[:], sE[:]))
            mlink(v.tensor_tensor(tE[:], tE[:], gate[:], ALU.subtract))
            mlink(v.tensor_tensor(sE[:], adst[:], over_nodes(lastn[:, HE:SUM]), ALU.add))
            mlink(leaky(rk[:], sE[:]))
            v.tensor_tensor(rk[:], rk[:], gate[:], ALU.subtract).then_inc(s["m_exp"], 1)
            mlink(v.tensor_scalar(over[:, 0:2], over[:, 0:2], 0.0, None, ALU.is_gt))
            mlink(v.tensor_scalar(over[:, 2:3], over[:, 2:3], GROUP_LEAST, None, ALU.is_ge))
            mlink(v.tensor_tensor(gm[:, 0, :], gm[:, 2, :], gm[:, 3, :], ALU.add))
            mlink(v.tensor_reduce(flag[:, 2:3], gm[:, 0, :], AX.X, ALU.max))
            mlink(v.tensor_scalar(over[:, 3:4], flag[:, 2:3], SPREAD, None, ALU.is_gt))
            v.tensor_reduce(flag[:, 0:1], over[:], AX.X, ALU.max).then_inc(s["zone"], 1)
            v.wait_ge(s["m_exp"], 3)
            mlink(v.tensor_tensor(rk[:], rk[:], cnt[:].unsqueeze(2).broadcast_to([P, NT, HEADS]), ALU.mult))
            mlink(v.tensor_tensor(sE[:], tE[:], rk[:], ALU.add))
            mlink(v.tensor_tensor(sums[:, :, HE:SUM], sums[:, :, HE:SUM], sE[:], ALU.add))
            spread = lambda a: a.unsqueeze(3).broadcast_to([P, NT, HEADS, NE])
            mlink(v.tensor_tensor(by_head(gA), by_head(T[:, :, 0:HE]), spread(tE[:]), ALU.mult))
            mlink(v.tensor_tensor(by_head(gB), by_head(over_nodes(lastn[:, 0:HE])), spread(rk[:]), ALU.mult))
            mlink(v.tensor_tensor(gA, gA, gB, ALU.add))
            mlink(v.tensor_tensor(sums[:, :, 0:HE], sums[:, :, 0:HE], gA, ALU.add))
            v.wait_ge(s["zone"], 2)
            v.tensor_copy(flag_i[:], flag[:, 1:2]).then_inc(s["flag_ready"], 1)
            v.wait_ge(s["flag_ready"], 1)
            bad = v.value_load(flag_i[0:1, 0:1], min_val=0, max_val=1)
            with v.If(bad > 0):
                GENERAL.vector(v)

            c = [0]

            def link(ins):
                ins.then_inc(g_chain, 1)
                c[0] += 1
                v.wait_ge(g_chain, c[0])

            def bc(a, n):
                return a.unsqueeze(2).broadcast_to([P, NT, n])

            def over_tiles(k):
                return gbb[:, k, :].unsqueeze(1).broadcast_to([P, NT, HE])

            link(v.reciprocal(sE[:], sums[:, :, HE:SUM]))
            link(v.tensor_tensor(by_head(gA), by_head(sums[:, :, 0:HE]), spread(sE[:]), ALU.mult))
            link(v.tensor_tensor(gB, gA, over_tiles(0), ALU.add))
            link(v.tensor_reduce(g1[:], gB, AX.X, ALU.add))
            link(v.tensor_scalar(g2[:], g1[:], 1.0 / HE, None, ALU.mult))
            link(v.tensor_tensor(gA, gB, bc(g2[:], HE), ALU.subtract))
            link(v.tensor_tensor(gB, gA, gA, ALU.mult))
            link(v.tensor_reduce(g2[:], gB, AX.X, ALU.add))
            v.tensor_scalar(g1[:], g2[:], 1.0 / HE, None, ALU.mult).then_inc(g_sq, 1)
            v.wait_ge(g_sq, 2)
            link(v.reciprocal(g1[:], g2[:]))
            link(v.tensor_tensor(gB, gA, bc(g1[:], HE), ALU.mult))
            link(v.tensor_tensor(gA, gB, over_tiles(1), ALU.mult))
            link(v.tensor_tensor(gB, gA, over_tiles(2), ALU.add))
            link(v.tensor_reduce(rk[:], gB.rearrange("p i (h e) -> p i e h", h=HEADS), AX.X, ALU.add))
            link(v.tensor_scalar(sE[:], rk[:], 1.0 / HEADS, None, ALU.mult))
            link(v.tensor_reduce(g1[:], sE[:], AX.X, ALU.max))
            v.tensor_tensor(tE[:], sE[:], bc(g1[:], NE), ALU.subtract).then_inc(g_exp, 1)
            link(v.memset(rk[:], 0.0))
            for e in range(NE):
                for o in range(NE):
                    if o != e:
                        link(v.tensor_tensor(g2[:], sE[:, :, o], sE[:, :, e], ALU.is_ge if o < e else ALU.is_gt))
                        link(v.tensor_tensor(rk[:, :, e], rk[:, :, e], g2[:], ALU.add))
            v.wait_ge(g_exp, 2)
            link(v.scalar_tensor_tensor(out=gate[:], in0=rk[:], scalar=2.0, in1=tE[:], op0=ALU.is_lt, op1=ALU.mult))
            link(v.tensor_reduce(g1[:], gate[:], AX.X, ALU.add))
            link(v.reciprocal(g2[:], g1[:]))
            link(v.tensor_tensor(gate[:], gate[:], bc(g2[:], NE), ALU.mult))
            assert c[0] == GATES, c[0]

            gate_v = gate[:].rearrange("p i e -> p (i e)")

            def group(i, live):
                if live(0):
                    b = i.slot(2)
                    held(v, tG_ld[b], i.dmas(2))
                    for k in range(G):
                        held(v, y_ps, i.n(G, k + 1))
                        if k >= 2 or live(1):
                            held(v, out_st[k % 2], i.n(2 * 16, 16 * (k // 2)))
                        for e in range(NE):
                            y = banks[4 + 2 * (k % 2) + e // 2][:, (e % 2) * D:(e % 2 + 1) * D]
                            src = tG[:, b, k, :] if e == 0 else acc[:, k % 2, :]
                            g = gate_v[:, bass.ds(i.n(G * NE, k * NE + e), 1)]
                            ins = v.scalar_tensor_tensor(out=acc[:, k % 2, :], in0=y, scalar=g, in1=src, op0=ALU.mult, op1=ALU.add)
                            if e < NE - 1:
                                ins.then_inc(acc_chain, 1)
                                v.wait_ge(acc_chain, i.n(G * (NE - 1), k * (NE - 1) + e + 1))
                            else:
                                ins.then_inc(acc_ready, 1)
            steps(v, NG, 2, group)


class general_path:

    def __init__(self, nc, room, sem, banks, row_d, st_d, edges, ident, M, ROW, ST, HE, HEADS, ET, T, S, sums):
        self.banks, self.row_d, self.st_d, self.edges, self.ident = banks, row_d, st_d, edges, ident
        self.M, self.ROW, self.ST, self.HE, self.HEADS, self.ET = M, ROW, ST, HE, HEADS, ET
        self.T, self.S, self.sums = T, S, sums
        at = [0]

        def sb(_, shape, dt=F32):
            n = 1
            for d in shape[1:]:
                n *= d
            a = room[:, at[0]:at[0] + n]
            at[0] += n
            if dt != F32:
                a = a.bitcast(dt)
            if len(shape) == 3:
                a = a.rearrange("p (a b) -> p a b", a=shape[1])
            return a
        self.lower = sb("lower", [P, P])
        self.ends = sb("ends", [P, 2], I32)
        self.isrc = sb("isrc", [P, 1], U32)
        self.idst = sb("idst", [P, 1], U32)
        self.iwr = sb("iwr", [P, 1], U32)
        self.dstf = sb("dstf", [P, 1])
        self.rs = sb("rs", [P, ROW])
        self.so = sb("so", [P, ST])
        self.sn = sb("sn", [P, ST])
        self.ee = sb("ee", [P, 2, HEADS])
        self.eq = sb("eq", [P, P])
        self.pen = sb("pen", [P, P])
        self.msk = sb("msk", [P, HEADS, P])
        self.tm = sb("tm", [P, HEADS])
        self.df = sb("df", [P, 2, HEADS])
        self.ex = sb("ex", [P, 2, HEADS])
        self.vv = sb("vv", [P, HE + HEADS])
        self.oc = sb("oc", [P, HE + HEADS])
        self.cnt = sb("cnt", [P, 1])
        self.s = {n: sem("gp_" + n) for n in "init stored st_ld ld eq_ps eT_ps v sum_ps exp".split()}
        self.PARTS = 4
        self.dma = [{n: sem(f"gp_{n}{k}") for n in ("rows", "states", "wr")} for k in range(self.PARTS)]

    V = 21

    def sync(self, sp):
        s = self.s
        states = self.st_d.rearrange("(i p) k -> p i k", p=P)
        sp.wait_ge(s["init"], 8)
        sp.dma_start(states, self.S).then_inc(s["stored"], 16)
        with sp.Fori(0, self.ET) as i:
            for k in range(2):
                sp.dma_start(self.ends[:, k:k + 1], self.edges[k, bass.ds(i * P, P)].rearrange("(p o) -> p o", o=1)).then_inc(s["ld"], 16)
            held(sp, s["v"], i * self.V + 3)
        for part in self.dma:
            sp.wait_ge(part["wr"], 16 * self.ET // self.PARTS)
        sp.dma_start(self.S, states).then_inc(s["st_ld"], 16)

    def gpsimd(self, pool):
        s = self.s
        pool.wait_ge(s["init"], 8)
        pool.affine_select(out=self.lower, in_=self.lower, compare_op=ALU.is_gt, fill=0.0, base=0,
                           pattern=[[-1, P]], channel_multiplier=1).then_inc(s["init"], 1)
        pool.wait_ge(s["stored"], 16)
        at = bass.IndirectOffsetOnAxis
        N = self.ET // self.PARTS
        for part, d in enumerate(self.dma):
          with pool.Fori(0, N) as n:
            i = n + part * N
            held(pool, s["v"], i * self.V + 3)
            pool.indirect_dma_start(out=self.rs[:], out_offset=None, in_=self.row_d, in_offset=at(ap=self.isrc[:], axis=0),
                                    bounds_check=self.M - 1, oob_is_err=False).then_inc(d["rows"], 16)
            pool.indirect_dma_start(out=self.so[:], out_offset=None, in_=self.st_d, in_offset=at(ap=self.idst[:], axis=0),
                                    bounds_check=self.M - 1, oob_is_err=False).then_inc(d["states"], 16)
            held(pool, s["v"], i * self.V + self.V)
            pool.indirect_dma_start(out=self.st_d, out_offset=at(ap=self.iwr[:], axis=0), in_=self.sn[:], in_offset=None,
                                    bounds_check=self.M - 1, oob_is_err=False).then_inc(d["wr"], 16)
            held(pool, d["wr"], n * 16 + 16)

    def scalar(self, act):
        s = self.s
        with act.Fori(0, self.ET) as i:
            act.wait_ge(s["v"], i * self.V + 12)
            act.activation(self.ex[:], self.df[:], ACT.Exp).then_inc(s["exp"], 1)

    def tensor(self, pe):
        s, b, H = self.s, self.banks, self.HEADS
        with pe.Fori(0, self.ET) as i:
            pe.wait_ge(s["v"], i * self.V + 3)
            pe.matmul(b[0][:, 0:P], self.dstf[:].broadcast_to([P, P]), self.ident[:], start=True, stop=True).then_inc(s["eq_ps"], 1)
            pe.wait_ge(s["v"], i * self.V + 5)
            for h in range(H):
                mm = pe.matmul(b[1][:, h * P:(h + 1) * P], self.ee[:, 1, h:h + 1].broadcast_to([P, P]), self.ident[:], start=True, stop=True)
            mm.then_inc(s["eT_ps"], 1)
            pe.wait_ge(s["v"], i * self.V + 14)
            pe.matmul(b[2][:, 0:self.HE + H], self.eq[:], self.vv[:], start=True, stop=True).then_inc(s["sum_ps"], 1)

    def vector(self, v):
        s, b, H, HE, M = self.s, self.banks, self.HEADS, self.HE, self.M
        NE = HE // H
        T, S = self.T, self.S
        v.memset(self.rs[:], 0.0).then_inc(s["init"], 1)
        v.memset(self.so[:], 0.0).then_inc(s["init"], 1)
        v.memset(self.lower[:], 1.0).then_inc(s["init"], 1)
        v.tensor_copy(S[:, :, 0:HE], T[:, :, 0:HE]).then_inc(s["init"], 1)
        v.memset(S[:, :, HE:HE + H], 1.0).then_inc(s["init"], 1)
        v.tensor_copy(S[:, :, HE + 2 * H:], T[:, :, HE + H:]).then_inc(s["init"], 1)
        v.tensor_tensor(self.sums[:, :, 0:H], T[:, :, HE:HE + H], T[:, :, HE + H:], ALU.add).then_inc(s["init"], 1)
        v.wait_ge(s["init"], 7)
        v.scalar_tensor_tensor(out=S[:, :, HE + H:HE + 2 * H], in0=self.sums[:, :, 0:H], scalar=0.2, in1=self.sums[:, :, 0:H], op0=ALU.mult, op1=ALU.max).then_inc(s["init"], 1)
        v.wait_ge(s["init"], 9)
        rs, so, sn, ee, eq, pen, msk = self.rs, self.so, self.sn, self.ee, self.eq, self.pen, self.msk
        N = self.ET // self.PARTS
        for part, d in enumerate(self.dma):
          with v.Fori(0, N) as n:
            i = n + part * N
            c = [0]

            def do(ins, wait=True):
                ins.then_inc(s["v"], 1)
                c[0] += 1
                if wait:
                    held(v, s["v"], i * self.V + c[0])
            held(v, s["ld"], i * 32 + 32)
            do(v.tensor_scalar(self.isrc[:], self.ends[:, 0:1], float(M - 1), None, ALU.min), False)
            do(v.tensor_copy(self.idst[:], self.ends[:, 1:2]), False)
            do(v.tensor_copy(self.dstf[:], self.ends[:, 1:2]))
            held(v, d["rows"], n * 16 + 16)
            held(v, d["states"], n * 16 + 16)
            do(v.tensor_tensor(ee[:, 0, :], rs[:, HE:HE + H], so[:, HE + 2 * H:], ALU.add))
            do(v.scalar_tensor_tensor(out=ee[:, 1, :], in0=ee[:, 0, :], scalar=0.2, in1=ee[:, 0, :], op0=ALU.mult, op1=ALU.max), False)
            held(v, s["eq_ps"], i + 1)
            do(v.tensor_scalar(eq[:], b[0][:, 0:P], self.dstf[:], None, ALU.is_equal))
            do(v.tensor_scalar(pen[:], eq[:], BIG, -BIG, ALU.mult, ALU.add))
            held(v, s["eT_ps"], i + 1)
            do(v.tensor_tensor(msk[:], b[1][:].rearrange("p (h j) -> p h j", h=H), pen[:].unsqueeze(1).broadcast_to([P, H, P]), ALU.add))
            do(v.tensor_reduce(self.tm[:], msk[:], AX.X, ALU.max))
            do(v.tensor_tensor(sn[:, HE + H:HE + 2 * H], so[:, HE + H:HE + 2 * H], self.tm[:], ALU.max))
            do(v.tensor_tensor(self.df[:, 0, :], ee[:, 1, :], sn[:, HE + H:HE + 2 * H], ALU.subtract), False)
            do(v.tensor_tensor(self.df[:, 1, :], so[:, HE + H:HE + 2 * H], sn[:, HE + H:HE + 2 * H], ALU.subtract), False)
            held(v, s["exp"], i + 1)
            do(v.tensor_copy(self.vv[:, HE:], self.ex[:, 0, :]), False)
            he = lambda a: a.rearrange("p (h e) -> p h e", h=H)
            do(v.tensor_tensor(he(self.vv[:, 0:HE]), he(rs[:, 0:HE]), self.ex[:, 0, :].unsqueeze(2).broadcast_to([P, H, NE]), ALU.mult), False)
            do(v.tensor_tensor(he(self.oc[:, 0:HE]), he(so[:, 0:HE]), self.ex[:, 1, :].unsqueeze(2).broadcast_to([P, H, NE]), ALU.mult), False)
            do(v.tensor_tensor(self.oc[:, HE:], so[:, HE:HE + H], self.ex[:, 1, :], ALU.mult), False)
            do(v.tensor_tensor(pen[:], eq[:], self.lower[:], ALU.mult))
            do(v.tensor_reduce(self.cnt[:], pen[:], AX.X, ALU.add))
            do(v.scalar_tensor_tensor(out=self.iwr[:], in0=self.cnt[:], scalar=65536.0, in1=self.dstf[:], op0=ALU.mult, op1=ALU.add), False)
            do(v.tensor_copy(sn[:, HE + 2 * H:], so[:, HE + 2 * H:]))
            held(v, s["sum_ps"], i + 1)
            do(v.tensor_tensor(sn[:, 0:HE + H], self.oc[:], b[2][:, 0:HE + H], ALU.add))
            assert c[0] == self.V
        v.wait_ge(s["st_ld"], 16)
        v.tensor_copy(self.sums[:], S[:, :, 0:HE + H]).then_inc(s["init"], 1)
        v.wait_ge(s["init"], 10)


_INS = ["x", "cbT", "cb", "wgat", "att", "b_gat", "gamma", "beta", "w1", "b1", "w2", "b2", "edges"]


def kernel(x, L0_conv_codebook, L0_ffn_W_gat, L0_ffn_att_src, L0_ffn_att_dst, L0_ffn_b_gat, L0_ffn_ln_gamma,
           L0_ffn_ln_beta, L0_ffn_W1, L0_ffn_b1, L0_ffn_W2, L0_ffn_b2, L0_ffn_edge_index):
    import numpy as np
    import concourse.bacc as bacc
    from concourse.bass_utils import run_bass_kernel_spmd

    B, C, H, W = x.shape
    arrays = {
        "x": np.ascontiguousarray(np.asarray(x).reshape(B, C, H * W).transpose(0, 2, 1).reshape(B * H * W, C)),
        "cbT": np.ascontiguousarray(np.asarray(L0_conv_codebook).T),
        "cb": np.ascontiguousarray(L0_conv_codebook),
        "wgat": np.ascontiguousarray(L0_ffn_W_gat),
        "att": np.stack([np.asarray(L0_ffn_att_src).reshape(-1), np.asarray(L0_ffn_att_dst).reshape(-1)]),
        "b_gat": np.ascontiguousarray(L0_ffn_b_gat),
        "gamma": np.ascontiguousarray(L0_ffn_ln_gamma),
        "beta": np.ascontiguousarray(L0_ffn_ln_beta),
        "w1": np.ascontiguousarray(np.asarray(L0_ffn_W1).transpose(1, 0, 2)),
        "b1": np.ascontiguousarray(np.asarray(L0_ffn_b1).reshape(-1, P).T),
        "w2": np.ascontiguousarray(L0_ffn_W2),
        "b2": np.ascontiguousarray(L0_ffn_b2),
        "edges": np.ascontiguousarray(L0_ffn_edge_index),
    }
    nc = bacc.Bacc("TRN2", target_bir_lowering=False, num_devices=1)
    aps = [nc.dram_tensor(n, arrays[n].shape, mybir.dt.from_np(arrays[n].dtype), kind="ExternalInput").ap() for n in _INS]
    out = nc.dram_tensor("out", (B * H * W, C), mybir.dt.float32, kind="ExternalOutput").ap()
    metaformer(nc, *aps, out)
    r = run_bass_kernel_spmd(nc, [arrays], core_ids=[0])
    got = r.results[0]["out"]
    return np.ascontiguousarray(got.reshape(B, H * W, C).transpose(0, 2, 1).reshape(B, C, H, W))
```

```python
from contextlib import ExitStack

import concourse.bass as bass
from concourse import mybir

ALU = mybir.AluOpType
ACT = mybir.ActivationFunctionType
AX = mybir.AxisListType
F32 = mybir.dt.float32
BF16 = mybir.dt.bfloat16
F32R = mybir.dt.float32r
I32 = mybir.dt.int32
U32 = mybir.dt.uint32
RMAX = bass.bass_isa.ReduceOp.max

P = 128
BANK = 512
BIG = 2.0 ** 100
SPREAD = 60.0

PASSES = [(0, 0), (0, 1), (1, 0)]

NODE_BITS = 14
LOW_BITS = 7
CHUNK = 256
COUNTED = 88
TRUE = 40
GROUPS = 8
PLACES = 104
BATCH = 13
HOT = 8


KEYS = 10
V_PREP = 8 + 2 * (COUNTED + TRUE) // 8 - 2 + 9
ROUNDS_C = [(0, 3), (3, 6), (6, 9), (9, 11)]
HOT_AT = [(0, 3), (3, 6), (6, 9), (9, 11)]
BY_ACT = [1, 4, 7, 10]
V_EXT = 1 + 2 * BATCH - 1 + 6
EXT_AT = [(0, 1)] + [(2 * q - 1, 2 * q + 1) for q in range(1, 7)] + [(13, 13)]
GROUP_LEAST = 2.0 ** -67


GATES = 44


class Tile:

    def __init__(self, j, r, unroll):
        self.j, self.r, self.unroll = j, r, unroll

    def back(self, n):
        return Tile(self.j, self.r - n, self.unroll)

    def slot(self, n):
        return self.r % n

    def n(self, per=1, plus=0):
        return self.j * (self.unroll * per) + (self.r * per + plus)

    def dmas(self, n, each=16):
        return self.j * (each * self.unroll // n) + each * (self.r // n + 1)


def held(eng, sem, value):
    eng.wait_ge(sem, value)
    eng.nop(nofuse=True)


def steps(eng, tiles, depth, step, unroll=4):
    first = -(-depth // unroll) * unroll
    for s in range(first):
        step(Tile(0, s, unroll), lambda k, s=s: 0 <= s - k < tiles)
    with eng.Fori(first // unroll, tiles // unroll) as j:
        for r in range(unroll):
            step(Tile(j, r, unroll), lambda k: True)
    for s in range(tiles, tiles + depth):
        step(Tile(tiles // unroll, s - tiles, unroll), lambda k, s=s: 0 <= s - k < tiles)


def metaformer(nc, x, cbT, cb, wgat, att, b_gat, gamma, beta, w1, b1, w2, b2, edges, out):
    M, D = x.shape
    NC = D // P
    K = cb.shape[0]
    _, NE, F = w1.shape
    FC = F // P
    NF = NE * FC
    HE = wgat.shape[1]
    HEADS = HE // NE
    E = edges.shape[1]
    NT = M // P
    G = BANK // P
    NG = M // BANK
    ET = E // P
    QN = K // BANK
    ROW = HE + 2 * HEADS
    SUM = HE + HEADS
    ST = HE + 3 * HEADS
    CHUNKS = E // P // CHUNK
    assert M == 1 << NODE_BITS and CHUNKS * 4 == NT
    CODES = CHUNKS * TRUE
    HB = COUNTED // HOT
    HV = 2 * HB - len(BY_ACT)
    GB = NT // GROUPS
    SB = PLACES // BATCH
    NB = GROUPS * SB

    t_d = nc.dram_tensor("t_scratch", [M, D], F32, kind="Internal").ap()
    tnT_d = nc.dram_tensor("tnT_scratch", [P, NC, M], F32, kind="Internal").ap()
    row_d = nc.dram_tensor("node_rows", [M, ROW], F32, kind="Internal").ap()
    st_d = nc.dram_tensor("node_states", [M, ST], F32, kind="Internal").ap()

    with ExitStack() as ctx:
        placed = {}

        def sb(name, shape, dt=F32):
            placed[name] = -(-nc.sbuf_base // 32) * 32
            return ctx.enter_context(nc.sbuf_tensor(name, shape, dt))

        def split_sb(name, over, at, words, **shape):
            a = nc.alloc_sbuf_tensor_at(name, [P, words], F32R, offset=placed[over] + 4 * at)[:]
            return a.rearrange("p (" + " ".join(shape) + ") -> p " + " ".join(shape), **shape)

        def ps(name, shape):
            return ctx.enter_context(nc.psum_tensor(name, shape, F32))

        def sem(name):
            return ctx.enter_context(nc.semaphore(name))

        ident = sb("ident", [P, P])
        iota = sb("iota", [P, P])
        iotab = sb("iotab", [P, P, HOT], BF16)
        xor_i = sb("xor_i", [P, GROUPS + 1], I32)
        ones2 = sb("ones2", [2, P], F32R)
        sel = sb("sel", [2, 2])
        halves = sb("halves", [P, 2])
        zero_b = sb("zero_b", [P, P], BF16)
        eps_c = sb("eps_c", [P, 1])
        eps_t = sb("eps_t", [P, 1])
        one_c = sb("one_c", [P, 1])
        w1_s = sb("w1_s", [P, NC, NE, F])
        w2_s = sb("w2_s", [P, NF, D])
        wg_s = sb("wg_s", [P, NC, ROW])
        att_s = sb("att_s", [P, 2, HE])
        b1_s = sb("b1_s", [P, NF])
        gbb = sb("gbb", [P, 3, HE])
        nrm_p = sb("nrm_p", [2, K], F32R)
        room = sb("room", [P, 2 * K + 2 * K + 512])
        cbT_s = w1_s[:].rearrange("p c e f -> p (c e f)")[:, 0:NC * K].rearrange("p (c k) -> p c k", c=NC)
        cb_p = (split_sb("cb_hi", "room", 0, NC * K, c=NC, k=K), split_sb("cb_lo", "w1_s", 0, NC * K, c=NC, k=K))
        sc = room[:, NC * K:(NC + 2) * K].rearrange("p (b k) -> p b k", b=2)
        room2 = sb("room2", [P, 2 * 4 * D + 6 * 2 * D])

        def carve(at, words, **shape):
            a = room2[:, at:at + words]
            return a.rearrange("p (" + " ".join(shape) + ") -> p " + " ".join(shape), **shape)
        xt = carve(0, 4 * D, b=4, d=D)
        stat = sb("stat", [P, 2, 6])
        mv = sb("mv", [P, 2, 2])
        std = sb("std", [P, 2])
        rstd = sb("rstd", [P, 2])
        xn = carve(4 * D, 4 * D, b=4, d=D)
        zT = sb("zT", [P, 2, 2, NC, P], F32R)
        mx = sb("mx", [P, 2, 8])
        ix = sb("ix", [P, 2, 8], U32)
        zq, zd, zs, tt, tn = (carve((8 + 2 * k) * D, 2 * D, b=2, d=D) for k in range(5))
        tnT = carve(18 * D, 2 * D, b=2, c=NC, t=P)
        stat2 = sb("stat2", [P, 2, 6])
        mv2 = sb("mv2", [P, 2, 2])
        std2 = sb("std2", [P, 2])
        rstd2 = sb("rstd2", [P, 2])
        T = sb("T", [P, NT, ROW])
        prod = sb("prod", [P, 2, 2, HE])
        ends = sb("ends", [P, 2, CHUNK], I32)
        any_i = sb("any_i", [P, CHUNK], I32)
        code_i = sb("code_i", [P, CHUNK], I32)
        keyt = sb("keyt", [P, CHUNK])
        keyc = sb("keyc", [P, CHUNK])
        gone = sb("gone", [P, CHUNK])
        gott = sb("gott", [P, TRUE])
        gotc = sb("gotc", [P, COUNTED])
        cnt_i = sb("cnt_i", [P, COUNTED], I32)
        cnt_b = sb("cnt_b", [P, 2, COUNTED], I32)
        blk = sb("blk", [P, COUNTED], BF16)
        low = sb("low", [P, COUNTED], BF16)
        low_n = sb("low_n", [P, COUNTED])
        hot_room = sb("hot_room", [P, 2 * P * HOT])
        hotA, hotB = (hot_room[:, k * P * HOT:(k + 1) * P * HOT].bitcast(BF16).rearrange("p (b n t) -> p b n t", b=2, n=P) for k in range(2))
        over = sb("over", [P, 4])
        code_room = sb("code_room", [P, 2 * CODES])
        codes, left = code_room[:, 0:CODES], code_room[:, CODES:2 * CODES]
        cnt = sb("cnt", [P, NT])
        gotg = sb("gotg", [P, PLACES])
        src_i = sb("src_i", [P, 2, PLACES], I32)
        part_i = sb("part_i", [P, 2, PLACES], I32)
        lowg = sb("lowg", [P, 2, PLACES])
        blkg = sb("blkg", [P, 2, PLACES])
        rows = carve(8 * D, 4 * BATCH * ROW, b=4, t=BATCH, k=ROW)
        adst = sb("adst", [P, NT, HEADS])
        gm = sb("gm", [P, 4, HEADS])
        lastn = sb("lastn", [P, ROW])
        hotm = sb("hotm", [P, 4, BATCH, GB])
        adm = carve(8 * D + 4 * BATCH * ROW, BATCH * GB * HEADS, t=BATCH, m=GB, h=HEADS)
        ea = sb("ea", [P, 6, BATCH, HEADS])
        msg = sb("msg", [P, 2, BATCH, SUM])
        outer = room[:, 0:2 * BATCH * GB * SUM].rearrange("p (b t m k) -> p b t m k", b=2, t=BATCH, m=GB)
        S = room[:, 2 * K:2 * K + NT * ST].rearrange("p (i k) -> p i k", k=ST)
        gA, gB = (room[:, k * NT * HE:(k + 1) * NT * HE].rearrange("p (i k) -> p i k", k=HE) for k in range(2))
        sums = sb("sums", [P, NT, SUM])
        g1 = sb("g1", [P, NT])
        g2 = sb("g2", [P, NT])
        sE = sb("sE", [P, NT, NE])
        rk = sb("rk", [P, NT, NE])
        tE = sb("tE", [P, NT, NE])
        gate = sb("gate", [P, NT, NE])
        hh = sb("hh", [P, NF, BANK])
        hv = hh[:].rearrange("p f n -> p (f n)")
        hotl = [a.rearrange("p (t n) -> p t n", t=BATCH) for a in
                (hv[:, 0:BATCH * P], hv[:, BATCH * P:2 * BATCH * P], hot_room[:, 0:BATCH * P], room2[:, 0:BATCH * P])]
        adst_p = [split_sb("adst_" + n, "hh", 4 * BATCH * P + k * NT * HEADS, NT * HEADS, i=NT, h=HEADS) for k, n in enumerate(("hi", "lo"))]
        hotT = split_sb("hotT", "hh", 2 * BATCH * P, 2 * BATCH * P, b=2, t=BATCH, n=P)
        nrm_hi, nrm_t = (hv[0:2, k * K:(k + 1) * K] for k in range(2))
        tG = room[:, 0:2 * G * D].rearrange("p (b k d) -> p b k d", b=2, k=G)
        acc = room[:, 2 * G * D:4 * G * D].rearrange("p (b k d) -> p b k d", b=2, k=G)
        w1_p = [split_sb("w1_" + n, over, 0, NC * NE * F, c=NC, e=NE, f=F) for n, over in (("hi", "room2"), ("lo", "w1_s"))]
        w2_p = [split_sb("w2_" + n, over, at, NF * D, f=NF, d=D) for n, over, at in (("hi", "room", 4 * G * D + 512), ("lo", "w2_s", 0))]
        tnG = carve(NC * NE * F, NC * BANK, c=NC, n=BANK)
        tn_p = [split_sb(f"tn_p{k}", over, 0, 2 * NC * BANK, q=2, c=NC, n=BANK) for k, over in enumerate(("hot_room", "code_room"))]
        Tr = T[:].rearrange("p i k -> p (i k)")
        hx = Tr[:, 0:FC * BANK].rearrange("p (b n) -> p b n", n=BANK)
        b2b = Tr[:, FC * BANK:FC * BANK + NE * D].rearrange("p (e d) -> p e d", e=NE)
        h_p = split_sb("h_p", "hh", 0, 4 * FC * BANK, b=2, q=2, f=FC, n=BANK)
        flag = sb("flag", [P, 3])
        flag_i = sb("flag_i", [P, 1], I32)

        banks = [ps(f"bank{i}", [P, BANK]) for i in range(8)]

        names = """const wld nrm_sq nrm_ps n_chain d_stat d_mv a_std d_rstd xn_ready pzT zT_ready
        sc_ready sc_evac d_mx ix_ready z_diff z_st t_ready d_stat2 d_mv2 a_std2 d_rstd2 tn_ready ptT tnT_ready
        h_ps h_evac fold prep hot_ready hot_used cnt_ps
        node last_ld node_max flag_ready zone extract hot_l hot_m hT_ps hT_evac ad_ps ad_sum scores
        wgt_ready msg_ready outer_ready sum_ps sum_ready e_chain m_chain m_exp""".split()
        s = {n: sem(n) for n in names}
        x_ld = [sem(f"x_ld{i}") for i in range(4)]
        zq_ld = [sem(f"zq_ld{i}") for i in range(2)]
        t_st = [sem(f"t_st{i}") for i in range(2)]
        tnT_st = [sem(f"tnT_st{i}") for i in range(2)]
        row_st = [sem(f"row_st{i}") for i in range(2)]
        ends_ld = sem("ends_ld")
        rows_ld = [sem(f"rows_ld{i}") for i in range(4)]
        tnG_ld = sem("tnG_ld")
        w_ld, cb_hi_done, cb_lo_done, z_lo, ad_split, hot_sq, hot_asq, hot_act, b2_ld, b2_added = (sem(n) for n in ("w_ld", "cb_hi_done", "cb_lo_done", "z_lo", "ad_split", "hot_sq", "hot_asq", "hot_act",
            "b2_ld", "b2_added"))
        tG_ld = [sem(f"tG_ld{i}") for i in range(2)]
        out_st = [sem(f"out_st{i}") for i in range(2)]
        g_chain, g_exp, g_sq = sem("g_chain"), sem("g_exp"), sem("g_sq")
        w_hi, w_lo, tn_hi, tn_lo, w_ps, gelu_out, h_hi, h_lo, y_ps, acc_done = (sem(n) for n in
            ("w_hi", "w_lo", "tn_hi", "tn_lo", "w_ps", "gelu_out", "h_hi", "h_lo", "y_ps", "acc_done"))

        GENERAL = general_path(nc, room, sem, banks, row_d, st_d, edges, ident, M, ROW, ST, HE, HEADS, ET, T, S, sums)

        T_v = T[:].rearrange("p i k -> p (i k)")
        adst_v = [a.rearrange("p i h -> p (i h)") for a in adst_p]
        ALL_T = 16 * NT // 2

        def by_act(h):
            return sum(b <= h for b in BY_ACT)

        def group_of(unit):
            return Tile(unit.j, unit.r // NE, unit.unroll // NE)
        block = ctx.enter_context(nc.Block())

        @block.sync
        def _(sp):
            sp.dma_start(cbT_s, cbT.rearrange("(c p) k -> p c k", p=P)).then_inc(s["wld"], 16)
            sp.dma_start(wg_s[:, :, 0:HE], wgat.rearrange("(c p) h -> p c h", p=P)).then_inc(s["wld"], 16)
            sp.dma_start(att_s[:], att.rearrange("(o a) h -> o a h", o=1).broadcast_to([P, 2, HE])).then_inc(s["wld"], 16)
            for k, v in enumerate((b_gat, gamma, beta)):
                sp.dma_start(gbb[:, k, :], v.rearrange("(o h) -> o h", o=1).broadcast_to([P, HE])).then_inc(s["wld"], 16)
            sp.dma_start(b1_s[:], b1).then_inc(s["wld"], 16)

            edges_v = edges.rearrange("a (p e) -> p a e", p=P)

            def step(i, live):
                if live(0):
                    if live(4):
                        held(sp, s["t_ready"], i.back(4).n(1, 1))
                    sp.dma_start(xt[:, i.slot(4), :], x[bass.ds(i.n(P), P), :]).then_inc(x_ld[i.slot(4)], 16)
                    if i.r == 0:
                        if live(4):
                            held(sp, s["prep"], (i.j - 1) * V_PREP + KEYS)
                        sp.dma_start(ends[:], edges_v[:, :, bass.ds(i.j * CHUNK, CHUNK)]).then_inc(ends_ld, 16)
                if live(3):
                    k = i.back(3)
                    held(sp, s["t_ready"], k.n(1, 1))
                    sp.dma_start(t_d[bass.ds(k.n(P), P), :], tt[:, k.slot(2), :]).then_inc(t_st[k.slot(2)], 16)
                    held(sp, s["tnT_ready"], k.n(1, 1))
                    sp.dma_start(tnT_d[:, :, bass.ds(k.n(P), P)], tnT[:, k.slot(2), :, :]).then_inc(tnT_st[k.slot(2)], 16)
                    held(sp, s["h_evac"], k.n(1, 1))
                    sp.dma_start(row_d[bass.ds(k.n(P), P), :], T_v[:, bass.ds(k.n(ROW), ROW)]).then_inc(row_st[k.slot(2)], 16)
            steps(sp, NT, 3, step)
            sp.wait_ge(s["sc_ready"], NT * QN)
            sp.dma_start(w1_s[:], w1.rearrange("(c p) e f -> p c e f", p=P)).then_inc(w_ld, 16)
            sp.dma_start(w2_s[:], w2.rearrange("e (c p) d -> p (e c) d", p=P)).then_inc(w_ld, 16)
            for q in t_st + tnT_st + row_st:
                sp.wait_ge(q, ALL_T)
            sp.dma_start(lastn[:], row_d[M - 1:M, :].broadcast_to([P, ROW])).then_inc(s["last_ld"], 16)
            sp.wait_ge(s["flag_ready"], 1)
            bad = sp.value_load(flag_i[0:1, 0:1], min_val=0, max_val=1)
            with sp.If(bad > 0):
                GENERAL.sync(sp)

            sp.dma_start(b2b, b2.rearrange("(o e) d -> o e d", o=1).broadcast_to([P, NE, D])).then_inc(b2_ld, 16)

            def unit(i, live):
                if live(0) and i.r % NE == 0:
                    g = group_of(i)
                    if live(NE):
                        held(sp, tn_lo, g.n(1, 0))
                    sp.dma_start(tnG, tnT_d[:, :, bass.ds(g.n(BANK), BANK)]).then_inc(tnG_ld, 16)
                    if live(2 * NE):
                        held(sp, acc_done, g.back(2).n(NE * G, G))
                    elif not live(1):
                        sp.wait_ge(g_chain, GATES)
                    sp.dma_start(tG[:, g.slot(2), :, :], t_d[bass.ds(g.n(BANK), BANK), :].rearrange("(k p) d -> p k d", p=P)).then_inc(tG_ld[g.slot(2)], 16)
                if live(3) and (i.r - 3) % NE == NE - 1:
                    g = group_of(i.back(3))
                    held(sp, acc_done, g.n(NE * G, NE * G))
                    sp.dma_start(out[bass.ds(g.n(BANK), BANK), :].rearrange("(k p) d -> p k d", p=P), acc[:, g.slot(2), :, :]).then_inc(out_st[g.slot(2)], 16)
            steps(sp, NG * NE, 3, unit, unroll=2 * NE)
            for q in out_st:
                sp.wait_ge(q, 16 * NG // 2)

        @block.gpsimd
        def _(pool):
            pool.memset(ident[:], 0.0).then_inc(s["const"], 1)
            pool.memset(halves[:], -0.5).then_inc(s["const"], 1)
            pool.memset(eps_c[:], 1e-6).then_inc(s["const"], 1)
            pool.memset(eps_t[:], 1e-5).then_inc(s["const"], 1)
            pool.memset(one_c[:], 1.0).then_inc(s["const"], 1)
            pool.iota(sel[:, 0:1], [[0, 1]], base=0, channel_multiplier=1, allow_small_or_imprecise_dtypes=True).then_inc(s["const"], 1)
            pool.iota(sel[:, 1:2], [[0, 1]], base=1, channel_multiplier=-2, allow_small_or_imprecise_dtypes=True).then_inc(s["const"], 1)
            pool.iota(iota[:], [[1, P]], base=0, channel_multiplier=0, allow_small_or_imprecise_dtypes=True).then_inc(s["const"], 1)
            pool.iota(iotab[:], [[1, P], [0, HOT]], base=0, channel_multiplier=0, allow_small_or_imprecise_dtypes=True).then_inc(s["const"], 1)
            pool.iota(xor_i[:], [[-1, GROUPS + 1]], base=GROUPS - 1, channel_multiplier=0).then_inc(s["const"], 1)
            pool.wait_ge(s["const"], 10)
            pool.affine_select(out=ident[:], in_=ident[:], compare_op=ALU.not_equal, fill=1.0, base=0,
                               pattern=[[-1, P]], channel_multiplier=1).then_inc(s["const"], 1)

            pool.wait_ge(s["nrm_sq"], NC)
            pool.wait_ge(cb_hi_done, 1)
            pool.tensor_tensor(cb_p[1], cbT_s, cb_p[0].bitcast(F32), ALU.subtract).then_inc(cb_lo_done, 1)

            def step(i, live):
                if live(1):
                    k = i.back(1)
                    b = k.slot(2)
                    held(pool, s["ix_ready"], k.n(1, 1))
                    if live(3):
                        held(pool, s["z_diff"], k.back(2).n(1, 1))
                    pool.indirect_dma_start(out=zq[:, b, :], out_offset=None, in_=cb,
                                            in_offset=bass.IndirectOffsetOnAxis(ap=ix[:, b, 0:1], axis=0),
                                            bounds_check=K - 1, oob_is_err=False).then_inc(zq_ld[b], 16)
                    held(pool, zq_ld[b], k.dmas(2))
                    if live(3):
                        held(pool, s["z_st"], k.back(2).n(1, 1))
                    pool.tensor_tensor(zd[:, b, :], zq[:, b, :], xn[:, k.slot(4), :], ALU.subtract).then_inc(s["z_diff"], 1)
                    held(pool, s["z_diff"], k.n(1, 1))
                    if live(3):
                        held(pool, s["t_ready"], k.back(2).n(1, 1))
                    pool.tensor_tensor(zs[:, b, :], xn[:, k.slot(4), :], zd[:, b, :], ALU.add).then_inc(s["z_st"], 1)
                    held(pool, s["z_st"], k.n(1, 1))
                    if live(3):
                        held(pool, t_st[b], k.back(2).dmas(2))
                        held(pool, s["tn_ready"], k.back(2).n(1, 1))
                    pool.tensor_tensor(tt[:, b, :], xt[:, k.slot(4), :], zs[:, b, :], ALU.add).then_inc(s["t_ready"], 1)
            steps(pool, NT, 3, step)

            pool.wait_ge(s["node"], 3)
            pool.partition_all_reduce(gm[:, 2:4, :].rearrange("p a h -> p (a h)"), gm[:, 0:2, :].rearrange("p a h -> p (a h)"), P, RMAX).then_inc(s["node_max"], 1)
            for q in row_st + t_st + tnT_st:
                pool.wait_ge(q, ALL_T)

            def batch(i, live):
                if live(0):
                    if i.r % SB == 0:
                        held(pool, s["extract"], i.j * (2 * V_EXT) + ((i.r // SB + 1) * V_EXT + 1))
                    if live(4):
                        held(pool, s["msg_ready"], i.back(4).n(1, 1))
                    g = i.r // SB % 2
                    for t in range(BATCH):
                        c = i.r % SB * BATCH + t
                        pool.indirect_dma_start(out=rows[:, i.slot(4), t, :], out_offset=None, in_=row_d,
                                                in_offset=bass.IndirectOffsetOnAxis(ap=src_i[:, g, c:c + 1].bitcast(U32), axis=0),
                                                bounds_check=M - 1, oob_is_err=False).then_inc(rows_ld[i.slot(4)], 16)
            steps(pool, NB, 4, batch, unroll=2 * SB)
            pool.wait_ge(s["zone"], 1)
            pool.partition_all_reduce(flag[:, 1:2], flag[:, 0:1], P, RMAX).then_inc(s["zone"], 1)
            pool.wait_ge(s["flag_ready"], 1)
            bad = pool.value_load(flag_i[0:1, 0:1], min_val=0, max_val=1)
            with pool.If(bad > 0):
                GENERAL.gpsimd(pool)
            pool.wait_ge(w_hi, 1)
            pool.tensor_tensor(w1_p[1], w1_s[:], w1_p[0].bitcast(F32), ALU.subtract).then_inc(w_lo, 1)
            pool.wait_ge(w_hi, 2)
            pool.tensor_tensor(w2_p[1], w2_s[:], w2_p[0].bitcast(F32), ALU.subtract).then_inc(w_lo, 1)

        @block.scalar
        def _(act):
            act.wait_ge(s["wld"], 16 * 7)
            for c in range(NC):
                act.activation(sc[:, c, :], cbT_s[:, c, :], ACT.Square).then_inc(s["nrm_sq"], 1)
            act.activation(cb_p[0], cbT_s, ACT.Copy).then_inc(cb_hi_done, 1)

            def low_rows(j, h):
                n = j * len(BY_ACT) + by_act(h)
                act.wait_ge(s["prep"], j * V_PREP + (V_PREP + 2))
                if h >= 2:
                    act.wait_ge(s["hot_used"], j * HB + (h - 1))
                elif not (isinstance(j, int) and j == 0):
                    act.wait_ge(s["hot_used"], j * HB + (h - 1))
                for t in range(HOT):
                    ins = act.activation(hotA[:, h % 2, :, t], iota[:], ACT.Square, bias=low_n[:, h * HOT + t:h * HOT + t + 1])
                ins.then_inc(hot_asq, 1)
                act.wait_ge(hot_asq, n)
                act.activation(hotA[:, h % 2, :, :], hotA[:, h % 2, :, :], ACT.Relu, bias=one_c[:], scale=-1.0).then_inc(hot_act, 1)

            def step(i, live):
                if live(0):
                    act.wait_ge(s["d_mv"], i.n(1, 1))
                    if live(2):
                        act.wait_ge(s["d_rstd"], i.back(2).n(1, 1))
                    act.activation(std[:, i.slot(2):i.slot(2) + 1], mv[:, i.slot(2), 1:2], ACT.Sqrt, bias=eps_c[:]).then_inc(s["a_std"], 1)
                if live(0):
                    b = i.slot(2)
                    act.wait_ge(s["pzT"], i.n(1, 1))
                    if live(2):
                        act.wait_ge(s["sc_ready"], i.back(2).n(QN, QN))
                    act.activation(zT[:, b, 0, :, :], banks[4][:, 0:D].rearrange("p (c t) -> p c t", c=NC), ACT.Copy).then_inc(s["zT_ready"], 1)
                k = i.back(2)
                if live(2):
                    b2_ = k.slot(2)
                    act.wait_ge(s["d_mv2"], k.n(1, 1))
                    if live(4):
                        act.wait_ge(s["d_rstd2"], k.back(2).n(1, 1))
                    act.activation(std2[:, b2_:b2_ + 1], mv2[:, b2_, 1:2], ACT.Sqrt, bias=eps_t[:]).then_inc(s["a_std2"], 1)

                def tn_evac():
                    act.wait_ge(s["ptT"], k.n(1, 1))
                    if live(4):
                        act.wait_ge(tnT_st[k.slot(2)], k.back(2).dmas(2))
                        act.wait_ge(s["h_ps"], k.back(2).n(1, 1))
                    act.activation(tnT[:, k.slot(2), :, :], banks[5][:, 0:D].rearrange("p (c t) -> p c t", c=NC), ACT.Copy).then_inc(s["tnT_ready"], 1)

                def row_evac():
                    act.wait_ge(s["h_ps"], k.n(1, 1))
                    act.activation(T_v[:, bass.ds(k.n(ROW), ROW)], banks[6][:, 0:ROW], ACT.Copy).then_inc(s["h_evac"], 1)

                if live(0):
                    for q in range(QN):
                        act.wait_ge(s["sc_ready"], i.n(QN, q + 1))
                        if live(2) and q == 0:
                            act.wait_ge(s["ix_ready"], i.back(2).n(1, 1))
                        act.activation(sc[:, b, q * BANK:(q + 1) * BANK], banks[q][:], ACT.Copy).then_inc(s["sc_evac"], 1)
                        if q == 0 and live(4) and HOT_AT[i.r][0] + 1 in BY_ACT:
                            low_rows(i.j - 1, HOT_AT[i.r][0] + 1)
                        if q == 1 and live(2):
                            tn_evac()
                        if q == 2 and live(2):
                            row_evac()
                elif live(2):
                    tn_evac()
                    row_evac()
            steps(act, NT, 3, step)

            for h in BY_ACT:
                low_rows(CHUNKS - 1, h)
            act.wait_ge(s["cnt_ps"], 1)
            for q in t_st + tnT_st:
                act.wait_ge(q, ALL_T)

            def batch(i, live):
                if live(1):
                    k = i.back(1)
                    b = k.slot(2)
                    if live(3):
                        act.wait_ge(s["ad_ps"], k.back(2).n(2, 2))
                    for q in range(4):
                        t0, t1 = 4 * q, min(4 * q + 4, BATCH)
                        act.wait_ge(s["hT_ps"], k.n(4, q + 1))
                        act.activation(hotT[:, b, t0:t1, :], banks[q][:, 0:(t1 - t0) * P].rearrange("p (t n) -> p t n", n=P), ACT.Copy).then_inc(s["hT_evac"], 1)
                if live(0):
                    g, c = i.r // SB % 2, i.r % SB * BATCH
                    if i.r % SB == 0:
                        act.wait_ge(s["extract"], i.j * (2 * V_EXT) + ((i.r // SB + 1) * V_EXT + 1))
                    if live(4):
                        act.wait_ge(s["sum_ps"], i.back(4).n(1, 1))
                    for t in range(BATCH):
                        ins = act.activation(hotl[i.slot(4)][:, t, :], iota[:], ACT.Square, bias=lowg[:, g, c + t:c + t + 1])
                    ins.then_inc(hot_sq, 1)
                if live(2):
                    k = i.back(2)
                    b = k.slot(2)
                    act.wait_ge(s["scores"], k.n(1, 1))
                    if live(4):
                        act.wait_ge(s["outer_ready"], k.back(2).n(1, 1))
                    act.activation(msg[:, b, :, HE:SUM], ea[:, 5, :, :], ACT.Exp).then_inc(s["wgt_ready"], 1)
                if live(0):
                    act.wait_ge(hot_sq, i.n(1, 1))
                    act.activation(hotl[i.slot(4)], hotl[i.slot(4)], ACT.Relu, bias=one_c[:], scale=-1.0).then_inc(s["hot_l"], 1)
            steps(act, NB, 4, batch, unroll=2 * SB)
            act.wait_ge(s["m_exp"], 1)
            act.activation(tE[:], tE[:], ACT.Exp).then_inc(s["m_exp"], 1)
            act.activation(rk[:], rk[:], ACT.Exp).then_inc(s["m_exp"], 1)
            act.wait_ge(s["flag_ready"], 1)
            bad = act.value_load(flag_i[0:1, 0:1], min_val=0, max_val=1)
            with act.If(bad > 0):
                GENERAL.scalar(act)
            act.wait_ge(w_ld, 32)
            act.activation(w1_p[0], w1_s[:], ACT.Copy).then_inc(w_hi, 1)
            act.wait_ge(g_chain, 1)
            act.activation(w2_p[0], w2_s[:], ACT.Copy).then_inc(w_hi, 1)
            act.wait_ge(g_sq, 1)
            act.activation(g2[:], g1[:], ACT.Sqrt, bias=eps_t[:]).then_inc(g_sq, 1)
            act.wait_ge(g_exp, 1)
            act.activation(tE[:], tE[:], ACT.Exp).then_inc(g_exp, 1)

            def unit(i, live):
                if live(0) and i.r % NE == 0:
                    g = group_of(i)
                    act.wait_ge(tnG_ld, g.n(16, 16))
                    if live(2 * NE):
                        act.wait_ge(w_ps, g.back(2).n(NF, NF))
                    act.activation(tn_p[g.slot(2)][:, 0, :, :], tnG, ACT.Copy).then_inc(tn_hi, 1)
                if live(2):
                    k = i.back(2)
                    for f in range(FC):
                        e = k.r % NE
                        act.wait_ge(w_ps, k.n(FC, f + 1))
                        if live(3):
                            act.wait_ge(h_lo, k.back(1).n(FC, f + 1))
                        act.activation(hx[:, f, :], banks[f][:], ACT.Gelu, bias=b1_s[:, e * FC + f:e * FC + f + 1]).then_inc(gelu_out, 1)
                        act.wait_ge(gelu_out, k.n(FC, f + 1))
                        if f == 0 and live(4):
                            act.wait_ge(y_ps, k.back(2).n(G, G))
                        act.activation(h_p[:, k.slot(2), 0, f, :], hx[:, f, :], ACT.Copy).then_inc(h_hi, 1)
            steps(act, NG * NE, 3, unit, unroll=2 * NE)

        @block.tensor
        def _(pe):
            pe.wait_ge(s["nrm_sq"], NC)
            pe.wait_ge(s["const"], 11)
            for q in range(QN):
                for c in range(NC):
                    mm = pe.matmul(banks[q][0:2, :], halves[:], sc[:, c, q * BANK:(q + 1) * BANK], start=c == 0, stop=c == NC - 1)
            mm.then_inc(s["nrm_ps"], 1)
            pe.wait_ge(s["n_chain"], 2 * QN + 2)
            pe.wait_ge(s["prep"], 2)
            pe.wait_ge(cb_lo_done, 1)
            pe.wait_ge(s["fold"], 2 * NC)
            pe.matmul(banks[7][:, 0:NT], zero_b[:], zero_b[:], start=True, stop=False, skip_group_check=True)

            def counts(j, first, last):
                for h in range(first, last):
                    pe.wait_ge(s["hot_ready"], j * HV + (2 * (h + 1) - by_act(h)))
                    if h in BY_ACT:
                        pe.wait_ge(hot_act, j * len(BY_ACT) + by_act(h))
                    for t in range(HOT):
                        mm = pe.matmul(banks[7][:, 0:NT], hotA[:, h % 2, :, t], hotB[:, h % 2, :, t], start=False, stop=False, skip_group_check=True)
                    mm.then_inc(s["hot_used"], 1)

            def step(i, live):
                if live(0):
                    pe.wait_ge(s["xn_ready"], i.n(1, 1))
                    if live(1):
                        pe.wait_ge(z_lo, i.back(1).n(1, 1))
                    for c in range(NC):
                        mm = pe.transpose(banks[4][:, c * P:(c + 1) * P], xn[:, i.slot(4), c * P:(c + 1) * P], ident[:])
                    mm.then_inc(s["pzT"], 1)
                k = i.back(2)

                def tn_transposed():
                    pe.wait_ge(s["tn_ready"], k.n(1, 1))
                    if live(3):
                        pe.wait_ge(s["tnT_ready"], k.back(1).n(1, 1))
                    for c in range(NC):
                        mm = pe.transpose(banks[5][:, c * P:(c + 1) * P], tn[:, k.slot(2), c * P:(c + 1) * P], ident[:])
                    mm.then_inc(s["ptT"], 1)

                def node_row():
                    pe.wait_ge(s["tnT_ready"], k.n(1, 1))
                    if live(3):
                        pe.wait_ge(s["h_evac"], k.back(1).n(1, 1))
                    for c in range(NC):
                        mm = pe.matmul(banks[6][:, 0:ROW], tnT[:, k.slot(2), c, :], wg_s[:, c, :], start=c == 0, stop=c == NC - 1)
                    mm.then_inc(s["h_ps"], 1)

                if live(0):
                    h0, h1 = HOT_AT[i.r] if live(4) else (0, 0)
                    pe.wait_ge(s["zT_ready"], i.n(1, 1))
                    for q in range(QN):
                        if q == 2:
                            counts(i.j - 1, h0, min(h0 + 1, h1))
                            if live(2):
                                tn_transposed()
                        if live(1):
                            pe.wait_ge(s["sc_evac"], i.back(1).n(QN, q + 1))
                        if q == 3 and live(2):
                            node_row()
                        cols = slice(q * BANK, (q + 1) * BANK)
                        pe.matmul(banks[q][:], ones2[:], nrm_p[:, cols], start=True, stop=False)
                        for a, b in PASSES:
                            if q == 0 and a == 1:
                                pe.wait_ge(z_lo, i.n(1, 1))
                            for c in range(NC):
                                mm = pe.matmul(banks[q][:], zT[:, i.slot(2), a, c, :], cb_p[b][:, c, cols], start=False, stop=(a, c) == (1, NC - 1))
                        mm.then_inc(s["sc_ready"], 1)
                    counts(i.j - 1, min(h0 + 1, h1), h1)
                elif live(2):
                    tn_transposed()
                    node_row()
            steps(pe, NT, 3, step)
            counts(CHUNKS - 1, 0, HB)
            pe.matmul(banks[7][:, 0:NT], zero_b[:], zero_b[:], start=False, stop=True, skip_group_check=True).then_inc(s["cnt_ps"], 1)

            pe.wait_ge(ad_split, 2)

            def batch(i, live):
                if live(1):
                    k = i.back(1)
                    b = k.slot(2)
                    pe.wait_ge(s["hot_l"], k.n(1, 1))
                    for q in range(4):
                        if live(2):
                            pe.wait_ge(s["hT_evac"], k.back(1).n(4, q + 1))
                        for t in range(4 * q, min(4 * q + 4, BATCH)):
                            mm = pe.transpose(banks[q][:, (t % 4) * P:(t % 4 + 1) * P], hotl[k.slot(4)][:, t, :], ident[:])
                        mm.then_inc(s["hT_ps"], 1)
                if live(3):
                    k = i.back(3)
                    b = k.slot(2)
                    q, g = k.r % SB, k.r // SB
                    pe.wait_ge(s["outer_ready"], k.n(1, 1))
                    if q == 0 and live(3 + 2 * SB):
                        pe.wait_ge(s["sum_ready"], Tile(k.j, g - 2, 2).n(1, 1))
                    for t in range(BATCH):
                        mm = pe.matmul(banks[6 + g % 2][:, 0:GB * SUM], hotl[k.slot(4)][:, t, :], outer[:, b, t, :, :].rearrange("p m k -> p (m k)"),
                                       start=(q, t) == (0, 0), stop=(q, t) == (SB - 1, BATCH - 1))
                    mm.then_inc(s["sum_ps"], 1)
                if live(1):
                    k = i.back(1)
                    b = k.slot(2)
                    gcol = bass.ds(k.j * (k.unroll // SB * GB * HEADS) + k.r // SB * GB * HEADS, GB * HEADS)
                    pe.wait_ge(s["hT_evac"], k.n(4, 4))
                    for t in range(BATCH):
                        if t % 8 == 0 and live(2):
                            pe.wait_ge(s["ad_sum"], k.back(1).n(3, t // 8 + 1))
                        for q in range(2):
                            mm = pe.matmul(banks[4 + t // 8][:, (t % 8) * GB * HEADS:(t % 8 + 1) * GB * HEADS], hotT[:, b, t, :], adst_v[q][:, gcol], start=q == 0, stop=q == 1)
                        if t in (7, BATCH - 1):
                            mm.then_inc(s["ad_ps"], 1)
            steps(pe, NB, 4, batch, unroll=2 * SB)
            pe.wait_ge(s["flag_ready"], 1)
            bad = pe.value_load(flag_i[0:1, 0:1], min_val=0, max_val=1)
            with pe.If(bad > 0):
                GENERAL.tensor(pe)

            def unit(i, live):
                if live(2):
                    k = i.back(2)
                    e, g = k.r % NE, group_of(k)
                    if e == 0:
                        pe.wait_ge(tn_lo, g.n(1, 1))
                    if not live(3):
                        pe.wait_ge(w_lo, 1)
                    for f in range(FC):
                        if live(3):
                            pe.wait_ge(gelu_out, k.back(1).n(FC, f + 1))
                        for a, b in PASSES:
                            for c in range(NC):
                                mm = pe.matmul(banks[f][:], w1_p[a][:, c, e, f * P:(f + 1) * P], tn_p[g.slot(2)][:, b, c, :],
                                               start=(a, b, c) == (0, 0, 0), stop=(a, b, c) == (1, 0, NC - 1))
                        mm.then_inc(w_ps, 1)
                if live(3):
                    k = i.back(3)
                    e = k.r % NE
                    pe.wait_ge(h_lo, k.n(FC, FC))
                    if not live(4):
                        pe.wait_ge(w_lo, 2)
                    for t in range(G):
                        y = banks[4 + 2 * k.slot(2) + t // 2]
                        if t % 2 == 0:
                            if live(5):
                                pe.wait_ge(acc_done, k.back(2).n(G, t + 2))
                        for f in range(FC):
                            for a, b in PASSES:
                                mm = pe.matmul(y[:, (t % 2) * D:(t % 2 + 1) * D], h_p[:, k.slot(2), a, f, t * P:(t + 1) * P], w2_p[b][:, e * FC + f, :],
                                               start=(f, a, b) == (0, 0, 0), stop=(f, a) == (FC - 1, 1))
                        mm.then_inc(y_ps, 1)
            steps(pe, NG * NE, 3, unit, unroll=2 * NE)

        @block.vector
        def _(v):
            v.memset(over[:], 0.0).then_inc(s["prep"], 1)
            v.memset(zero_b[:], 0.0).then_inc(s["prep"], 1)
            v.wait_ge(s["const"], 11)
            v.tensor_scalar(xor_i[:], xor_i[:], 2 * NODE_BITS - 3, None, ALU.logical_shift_left).then_inc(s["extract"], 1)
            v.wait_ge(s["wld"], 16 * 7)
            for c in range(NC):
                v.tensor_tensor(prod[:, c, :, :], wg_s[:, c, 0:HE].unsqueeze(1).broadcast_to([P, 2, HE]), att_s[:], ALU.mult).then_inc(s["fold"], 1)
            v.wait_ge(s["fold"], NC)
            for c in range(NC):
                v.tensor_reduce(wg_s[:, c, HE:], prod[:, c, :, :].rearrange("p a (h e) -> p (a h) e", h=HEADS), AX.X, ALU.add).then_inc(s["fold"], 1)
            v.tensor_scalar(ones2[:], iota[0:2, :], 0.0, 1.0, ALU.mult, ALU.add).then_inc(s["n_chain"], 1)
            v.wait_ge(s["nrm_ps"], 1)
            for q in range(QN):
                cols = slice(q * BANK, (q + 1) * BANK)
                v.tensor_copy(nrm_hi[:, cols].bitcast(F32R), banks[q][0:2, :]).then_inc(s["n_chain"], 1)
                v.tensor_scalar(nrm_t[:, cols], banks[q][0:2, :], sel[:, 0:1], None, ALU.mult).then_inc(s["n_chain"], 1)
            v.wait_ge(s["n_chain"], 2 * QN + 1)
            v.scalar_tensor_tensor(out=nrm_p[:], in0=nrm_hi, scalar=sel[:, 1:2], in1=nrm_t, op0=ALU.mult, op1=ALU.add).then_inc(s["n_chain"], 1)

            class Prep:

                def __init__(self):
                    self.n = 2

                def did(self, j, ins):
                    ins.then_inc(s["prep"], 1)
                    self.n += 1
                    return self.n

                def wait(self, j, n):
                    held(v, s["prep"], j * V_PREP + n)

            prep = Prep()
            done = {}

            def sort_out(j, r, h0, h1):
                n = [2 * h0]

                def between():
                    if n[0] < 2 * h1:
                        one_hot(j - 1, n[0] // 2, n[0] % 2)
                        n[0] += 1
                if r == 0:
                    prep.n = 2
                    held(v, ends_ld, j * 16 + 16)
                    src, dst = ends[:, 0, :], ends[:, 1, :]
                    prep.did(j, v.tensor_tensor(any_i[:], src, dst, ALU.bitwise_or))
                    n1 = prep.did(j, v.tensor_scalar(code_i[:], dst, NODE_BITS, 1 << 2 * NODE_BITS, ALU.logical_shift_left, ALU.bitwise_or))
                    prep.did(j, v.tensor_scalar(gone[:], src, float(M), None, ALU.is_ge))
                    n2 = prep.did(j, v.tensor_scalar(keyc[:], dst, 1.0, None, ALU.add))
                    prep.wait(j, n1)
                    n3_ = prep.did(j, v.tensor_tensor(code_i[:], code_i[:], src, ALU.bitwise_or))
                    prep.wait(j, n2)
                    n4 = prep.did(j, v.tensor_tensor(keyc[:], keyc[:], gone[:], ALU.mult))
                    prep.wait(j, n3_)
                    done["t"] = prep.did(j, v.scalar_tensor_tensor(out=keyt[:], in0=any_i[:], scalar=float(M), in1=code_i[:].bitcast(F32), op0=ALU.is_lt, op1=ALU.mult))
                    prep.wait(j, n4)
                    done["c"] = prep.did(j, v.scalar_tensor_tensor(out=keyc[:], in0=dst, scalar=float(M), in1=keyc[:], op0=ALU.is_lt, op1=ALU.mult))
                    assert prep.n == KEYS
                for k in range(*ROUNDS_C[r]):
                    prep.wait(j, done["c"])
                    done["c"] = prep.did(j, v.max(gotc[:, 8 * k:8 * k + 8], keyc[:]))
                    if k < TRUE // 8:
                        prep.wait(j, done["t"])
                        done["t"] = prep.did(j, v.max(gott[:, 8 * k:8 * k + 8], keyt[:]))
                    else:
                        between()
                    if k < COUNTED // 8 - 1:
                        prep.wait(j, done["c"])
                        done["c"] = prep.did(j, v.match_replace(keyc[:], gotc[:, 8 * k:8 * k + 8], keyc[:], 0.0))
                    if k < TRUE // 8 - 1:
                        prep.wait(j, done["t"])
                        done["t"] = prep.did(j, v.match_replace(keyt[:], gott[:, 8 * k:8 * k + 8], keyt[:], 0.0))
                    else:
                        between()
                while n[0] < 2 * h1:
                    between()

            def finish(j):
                prep.wait(j, done["c"])
                prep.did(j, v.tensor_copy(codes[:, bass.ds(j * TRUE, TRUE)], gott[:]))
                prep.did(j, v.tensor_tensor(over[:, 0:1], over[:, 0:1], gotc[:, COUNTED - 1:COUNTED], ALU.max))
                prep.did(j, v.tensor_tensor(over[:, 1:2], over[:, 1:2], gott[:, TRUE - 1:TRUE], ALU.max))
                n = prep.did(j, v.tensor_scalar(cnt_i[:], gotc[:], 1.0, None, ALU.subtract))
                prep.wait(j, n)
                prep.did(j, v.tensor_scalar(cnt_b[:, 0, :], cnt_i[:], LOW_BITS, None, ALU.arith_shift_right))
                n = prep.did(j, v.tensor_scalar(cnt_b[:, 1, :], cnt_i[:], P - 1, None, ALU.bitwise_and))
                prep.wait(j, n)
                prep.did(j, v.tensor_copy(blk[:], cnt_b[:, 0, :]))
                if not (isinstance(j, int) and j == 0):
                    held(v, hot_act, j * len(BY_ACT))
                prep.did(j, v.tensor_scalar(low_n[:], cnt_b[:, 1, :], -1.0, None, ALU.mult))
                n = prep.did(j, v.tensor_copy(low[:], cnt_b[:, 1, :]))
                assert n - 2 == V_PREP, n
                prep.wait(j, n)

            def one_hot(j, h, half):
                if half == 0 and h in BY_ACT:
                    return
                if half == 0 or h in BY_ACT:
                    if h >= 2:
                        held(v, s["hot_used"], j * HB + (h - 1))
                    elif not (isinstance(j, int) and j == 0):
                        held(v, s["hot_used"], j * HB)
                dst, bits = ((hotA, low), (hotB, blk))[half]
                v.tensor_tensor(dst[:, h % 2, :, :], iotab[:], bits[:, h * HOT:(h + 1) * HOT].unsqueeze(1).broadcast_to([P, P, HOT]), ALU.is_equal).then_inc(s["hot_ready"], 1)

            def one_hots(j, first, last):
                for h in range(first, last):
                    one_hot(j, h, 0)
                    one_hot(j, h, 1)

            def step(i, live):
                k2 = i.back(2)
                c = k2.slot(2)
                h0, h1 = HOT_AT[i.r] if live(0) and live(4) else (0, 0)
                b = i.slot(2)
                if live(0):
                    held(v, x_ld[i.slot(4)], i.dmas(4))
                    v.bn_stats(stat[:, b, :], xt[:, i.slot(4), :]).then_inc(s["d_stat"], 1)
                if live(0):
                    held(v, s["d_stat"], i.n(1, 1))
                    if live(2):
                        held(v, s["xn_ready"], i.back(2).n(1, 1))
                        held(v, s["a_std"], i.back(2).n(1, 1))
                    v.bn_aggr(mv[:, b, :], stat[:, b, :]).then_inc(s["d_mv"], 1)
                if live(2):
                    held(v, s["t_ready"], k2.n(1, 1))
                    v.bn_stats(stat2[:, c, :], tt[:, c, :]).then_inc(s["d_stat2"], 1)
                if live(0):
                    held(v, s["a_std"], i.n(1, 1))
                    v.reciprocal(rstd[:, b:b + 1], std[:, b:b + 1]).then_inc(s["d_rstd"], 1)
                    held(v, s["d_rstd"], i.n(1, 1))
                    v.tensor_scalar(xn[:, i.slot(4), :], xt[:, i.slot(4), :], mv[:, b, 0:1], rstd[:, b:b + 1], ALU.subtract, ALU.mult).then_inc(s["xn_ready"], 1)
                if live(2):
                    held(v, s["d_stat2"], k2.n(1, 1))
                    if live(4):
                        held(v, s["tn_ready"], k2.back(2).n(1, 1))
                    v.bn_aggr(mv2[:, c, :], stat2[:, c, :]).then_inc(s["d_mv2"], 1)
                if h1:
                    one_hot(i.j - 1, h0, 0)
                if h1:
                    one_hot(i.j - 1, h0, 1)
                if live(0):
                    held(v, s["zT_ready"], i.n(1, 1))
                    v.tensor_tensor(zT[:, b, 1, :, :], banks[4][:, 0:D].rearrange("p (c t) -> p c t", c=NC), zT[:, b, 0, :, :].bitcast(F32), ALU.subtract).then_inc(z_lo, 1)
                if live(2):
                    held(v, s["a_std2"], k2.n(1, 1))
                    v.reciprocal(rstd2[:, c:c + 1], std2[:, c:c + 1]).then_inc(s["d_rstd2"], 1)
                if live(1):
                    k = i.back(1)
                    held(v, s["sc_evac"], k.n(QN, QN))
                    v.max(mx[:, k.slot(2), :], sc[:, k.slot(2), :]).then_inc(s["d_mx"], 1)
                if live(2):
                    held(v, s["d_rstd2"], k2.n(1, 1))
                    if live(4):
                        held(v, s["ptT"], k2.back(2).n(1, 1))
                    v.tensor_scalar(tn[:, c, :], tt[:, c, :], mv2[:, c, 0:1], rstd2[:, c:c + 1], ALU.subtract, ALU.mult).then_inc(s["tn_ready"], 1)
                if live(1):
                    k = i.back(1)
                    held(v, s["d_mx"], k.n(1, 1))
                    if live(3):
                        held(v, zq_ld[k.slot(2)], k.back(2).dmas(2))
                    v.max_index(ix[:, k.slot(2), :], mx[:, k.slot(2), :], sc[:, k.slot(2), :]).then_inc(s["ix_ready"], 1)
                if live(0):
                    sort_out(i.j, i.r, h0 + 1, h1)
                if live(0) and i.r == 3:
                    finish(i.j)
            steps(v, NT, 3, step)

            v.wait_ge(s["h_evac"], NT)
            v.tensor_reduce(gm[:, 0, :], T[:, :, HE:SUM].rearrange("p i h -> p h i"), AX.X, ALU.max).then_inc(s["node"], 1)
            v.tensor_reduce(gm[:, 2, :], T[:, :, HE:SUM].rearrange("p i h -> p h i"), AX.X, ALU.min).then_inc(s["node"], 1)
            v.wait_ge(s["node"], 2)
            v.tensor_scalar(gm[:, 1, :], gm[:, 2, :], -1.0, None, ALU.mult).then_inc(s["node"], 1)
            v.tensor_copy(adst[:], T[:, :, SUM:ROW]).then_inc(s["node"], 1)
            v.tensor_copy(adst_p[0], T[:, :, SUM:ROW]).then_inc(ad_split, 1)
            v.wait_ge(ad_split, 1)
            v.tensor_tensor(adst_p[1], T[:, :, SUM:ROW], adst_p[0].bitcast(F32), ALU.subtract).then_inc(ad_split, 1)

            class Extract:

                def did(self, g, ins):
                    ins.then_inc(s["extract"], 1)
                    self.n += 1

                def wait(self, g):
                    held(v, s["extract"], g[0] * (2 * V_EXT) + (g[1] * V_EXT + 1 + self.n))

            ex = Extract()

            def extract(g, q, quarter):
                if q == 0 and quarter == 0:
                    ex.n = 0
                    ex.wait(g)
                    ex.did(g, v.tensor_scalar(left.bitcast(I32), codes.bitcast(I32), xor_i[:, bass.ds(g[0] * 2 + g[1], 1)], None, ALU.bitwise_xor))
                a, b = EXT_AT[q]
                mid = (a + b + 1) // 2
                for k in range(a, mid) if quarter < 2 else range(mid, b):
                    if quarter % 2 == 0:
                        ex.wait(g)
                        ex.did(g, v.max(gotg[:, 8 * k:8 * k + 8], left))
                    elif k < BATCH - 1:
                        ex.wait(g)
                        ex.did(g, v.match_replace(left, gotg[:, 8 * k:8 * k + 8], left, 0.0))
                if q == SB - 1 and quarter == 3:
                    p = g[1] % 2
                    got = gotg[:].bitcast(I32)
                    ex.wait(g)
                    ex.did(g, v.tensor_tensor(over[:, 2:3], over[:, 2:3], gotg[:, PLACES - 1:PLACES], ALU.max))
                    ex.did(g, v.tensor_scalar(part_i[:, 0, :], got, NODE_BITS, P - 1, ALU.logical_shift_right, ALU.bitwise_and))
                    ex.did(g, v.tensor_scalar(part_i[:, 1, :], got, NODE_BITS + LOW_BITS, None, ALU.logical_shift_right))
                    ex.did(g, v.tensor_scalar(src_i[:, p, :], got, M - 1, None, ALU.bitwise_and))
                    ex.wait(g)
                    ex.did(g, v.tensor_scalar(lowg[:, p, :], part_i[:, 0, :], -1.0, None, ALU.mult))
                    ex.did(g, v.tensor_scalar(blkg[:, p, :], part_i[:, 1, :], float(2 * NT - GB), None, ALU.subtract))
                    assert ex.n == V_EXT, ex.n

            for q in range(SB):
                one_hots(CHUNKS - 1, 2 * q, min(2 * q + 1, HB))
                extract((0, 0), q, 0)
                extract((0, 0), q, 1)
                one_hots(CHUNKS - 1, min(2 * q + 1, HB), min(2 * q + 2, HB))
                extract((0, 0), q, 2)
                extract((0, 0), q, 3)
            v.wait_ge(s["cnt_ps"], 1)
            v.tensor_copy(cnt[:], banks[7][:, 0:NT]).then_inc(s["node"], 1)
            v.wait_ge(s["node_max"], 1)
            for q in t_st + tnT_st:
                v.wait_ge(q, ALL_T)
            sums_v = sums[:].rearrange("p i k -> p (i k)")

            def batch(i, live):
                nxt = (i.j, i.r // SB + 1)
                q = i.r % SB
                if live(4) and (i.r - 4) % SB == SB - 1:
                    k = i.back(4)
                    g = k.r // SB
                    held(v, s["sum_ps"], k.n(1, 1))
                    v.tensor_copy(sums_v[:, bass.ds(k.j * (2 * GB * SUM) + g * GB * SUM, GB * SUM)], banks[6 + g % 2][:, 0:GB * SUM]).then_inc(s["sum_ready"], 1)
                if live(1):
                    k = i.back(1)
                    g, c = k.r // SB % 2, k.r % SB * BATCH
                    held(v, s["extract"], k.j * (2 * V_EXT) + ((k.r // SB + 1) * V_EXT + 1))
                    v.tensor_tensor(hotm[:, k.slot(4), :, :], iota[:, 0:GB].unsqueeze(1).broadcast_to([P, BATCH, GB]),
                                    blkg[:, g, c:c + BATCH].unsqueeze(2).broadcast_to([P, BATCH, GB]), ALU.is_equal).then_inc(s["hot_m"], 1)
                if live(2):
                    k = i.back(2)
                    held(v, s["hot_m"], k.n(1, 1))
                    for h in range(2):
                        t0, t1 = 8 * h, min(8 * h + 8, BATCH)
                        held(v, s["ad_ps"], k.n(2, h + 1))
                        v.tensor_tensor(adm[:, t0:t1, :, :], banks[4 + h][:, 0:(t1 - t0) * GB * HEADS].rearrange("p (t m h) -> p t m h", m=GB, h=HEADS),
                                        hotm[:, k.slot(4), t0:t1, :].unsqueeze(3).broadcast_to([P, t1 - t0, GB, HEADS]), ALU.mult).then_inc(s["ad_sum"], 1)
                if live(0):
                    extract(nxt, q, 0)
                k = i.back(2)
                b = k.slot(2)
                r_ = rows[:, k.slot(4), :, :]
                if live(2):
                    held(v, s["ad_sum"], k.n(3, 2))
                    v.tensor_reduce(ea[:, 0, :, :], adm.rearrange("p t m h -> p t h m"), AX.X, ALU.add).then_inc(s["ad_sum"], 1)
                if live(0):
                    extract(nxt, q, 1)
                if live(2):
                    held(v, s["ad_sum"], k.n(3, 3))
                    held(v, rows_ld[k.slot(4)], k.dmas(4, 16 * BATCH))
                    v.tensor_tensor(ea[:, 1, :, :], r_[:, :, HE:SUM], ea[:, 0, :, :], ALU.add).then_inc(s["e_chain"], 1)
                    v.tensor_tensor(ea[:, 2, :, :], ea[:, 0, :, :], gm[:, 2, :].unsqueeze(1).broadcast_to([P, BATCH, HEADS]), ALU.add).then_inc(s["e_chain"], 1)
                if live(0):
                    extract(nxt, q, 2)
                if live(2):
                    held(v, s["e_chain"], k.n(4, 2))
                    v.scalar_tensor_tensor(out=ea[:, 3:5, :, :], in0=ea[:, 1:3, :, :], scalar=0.2, in1=ea[:, 1:3, :, :], op0=ALU.mult, op1=ALU.max).then_inc(s["e_chain"], 1)
                    held(v, s["e_chain"], k.n(4, 3))
                    v.tensor_tensor(ea[:, 0, :, :], ea[:, 3, :, :], ea[:, 4, :, :], ALU.subtract).then_inc(s["e_chain"], 1)
                    held(v, s["e_chain"], k.n(4, 4))
                    if live(3):
                        held(v, s["wgt_ready"], k.n(1, 0))
                    v.tensor_scalar(ea[:, 5, :, :], ea[:, 0, :, :], 0.0, None, ALU.min).then_inc(s["scores"], 1)
                if live(0):
                    extract(nxt, q, 3)
                if live(2):
                    held(v, s["wgt_ready"], k.n(1, 1))
                    if live(4):
                        held(v, s["sum_ps"], k.back(2).n(1, 1))
                    v.tensor_tensor(msg[:, b, :, 0:HE].rearrange("p t (h e) -> p t h e", h=HEADS), r_[:, :, 0:HE].rearrange("p t (h e) -> p t h e", h=HEADS),
                                    msg[:, b, :, HE:SUM].unsqueeze(3).broadcast_to([P, BATCH, HEADS, NE]), ALU.mult).then_inc(s["msg_ready"], 1)
                    held(v, s["msg_ready"], k.n(1, 1))
                    v.tensor_tensor(outer[:, b, :, :, :], hotm[:, k.slot(4), :, :].unsqueeze(3).broadcast_to([P, BATCH, GB, SUM]),
                                    msg[:, b, :, :].unsqueeze(2).broadcast_to([P, BATCH, GB, SUM]), ALU.mult).then_inc(s["outer_ready"], 1)

            steps(v, NB, 4, batch, unroll=2 * SB)
            v.wait_ge(s["sum_ready"], GROUPS)

            m = [0]

            def mlink(ins):
                ins.then_inc(s["m_chain"], 1)
                m[0] += 1
                v.wait_ge(s["m_chain"], m[0])

            def over_nodes(a):
                return a.unsqueeze(1).broadcast_to([P, NT, a.shape[1]])

            def by_head(a):
                return a.rearrange("p i (h e) -> p i h e", h=HEADS)

            def leaky(out_, in_):
                return v.scalar_tensor_tensor(out=out_, in0=in_, scalar=0.2, in1=in_, op0=ALU.mult, op1=ALU.max)

            v.wait_ge(s["last_ld"], 16)
            mlink(v.tensor_tensor(sE[:], adst[:], over_nodes(gm[:, 2, :]), ALU.add))
            mlink(leaky(gate[:], sE[:]))
            mlink(v.tensor_tensor(sE[:], T[:, :, HE:SUM], adst[:], ALU.add))
            mlink(leaky(tE[:], sE[:]))
            mlink(v.tensor_tensor(tE[:], tE[:], gate[:], ALU.subtract))
            mlink(v.tensor_tensor(sE[:], adst[:], over_nodes(lastn[:, HE:SUM]), ALU.add))
            mlink(leaky(rk[:], sE[:]))
            v.tensor_tensor(rk[:], rk[:], gate[:], ALU.subtract).then_inc(s["m_exp"], 1)
            mlink(v.tensor_scalar(over[:, 0:2], over[:, 0:2], 0.0, None, ALU.is_gt))
            mlink(v.tensor_scalar(over[:, 2:3], over[:, 2:3], GROUP_LEAST, None, ALU.is_ge))
            mlink(v.tensor_tensor(gm[:, 0, :], gm[:, 2, :], gm[:, 3, :], ALU.add))
            mlink(v.tensor_reduce(flag[:, 2:3], gm[:, 0, :], AX.X, ALU.max))
            mlink(v.tensor_scalar(over[:, 3:4], flag[:, 2:3], SPREAD, None, ALU.is_gt))
            v.tensor_reduce(flag[:, 0:1], over[:], AX.X, ALU.max).then_inc(s["zone"], 1)
            v.wait_ge(s["m_exp"], 3)
            mlink(v.tensor_tensor(rk[:], rk[:], cnt[:].unsqueeze(2).broadcast_to([P, NT, HEADS]), ALU.mult))
            mlink(v.tensor_tensor(sE[:], tE[:], rk[:], ALU.add))
            mlink(v.tensor_tensor(sums[:, :, HE:SUM], sums[:, :, HE:SUM], sE[:], ALU.add))
            spread = lambda a: a.unsqueeze(3).broadcast_to([P, NT, HEADS, NE])
            mlink(v.tensor_tensor(by_head(gA), by_head(T[:, :, 0:HE]), spread(tE[:]), ALU.mult))
            mlink(v.tensor_tensor(by_head(gB), by_head(over_nodes(lastn[:, 0:HE])), spread(rk[:]), ALU.mult))
            mlink(v.tensor_tensor(gA, gA, gB, ALU.add))
            mlink(v.tensor_tensor(sums[:, :, 0:HE], sums[:, :, 0:HE], gA, ALU.add))
            v.wait_ge(s["zone"], 2)
            v.tensor_copy(flag_i[:], flag[:, 1:2]).then_inc(s["flag_ready"], 1)
            v.wait_ge(s["flag_ready"], 1)
            bad = v.value_load(flag_i[0:1, 0:1], min_val=0, max_val=1)
            with v.If(bad > 0):
                GENERAL.vector(v)

            c = [0]

            def link(ins):
                ins.then_inc(g_chain, 1)
                c[0] += 1
                v.wait_ge(g_chain, c[0])

            def bc(a, n):
                return a.unsqueeze(2).broadcast_to([P, NT, n])

            def over_tiles(k):
                return gbb[:, k, :].unsqueeze(1).broadcast_to([P, NT, HE])

            link(v.reciprocal(sE[:], sums[:, :, HE:SUM]))
            link(v.tensor_tensor(by_head(gA), by_head(sums[:, :, 0:HE]), spread(sE[:]), ALU.mult))
            link(v.tensor_tensor(gB, gA, over_tiles(0), ALU.add))
            link(v.tensor_reduce(g1[:], gB, AX.X, ALU.add))
            link(v.tensor_scalar(g2[:], g1[:], 1.0 / HE, None, ALU.mult))
            link(v.tensor_tensor(gA, gB, bc(g2[:], HE), ALU.subtract))
            link(v.tensor_tensor(gB, gA, gA, ALU.mult))
            link(v.tensor_reduce(g2[:], gB, AX.X, ALU.add))
            v.tensor_scalar(g1[:], g2[:], 1.0 / HE, None, ALU.mult).then_inc(g_sq, 1)
            v.wait_ge(g_sq, 2)
            link(v.reciprocal(g1[:], g2[:]))
            link(v.tensor_tensor(gB, gA, bc(g1[:], HE), ALU.mult))
            link(v.tensor_tensor(gA, gB, over_tiles(1), ALU.mult))
            link(v.tensor_tensor(gB, gA, over_tiles(2), ALU.add))
            link(v.tensor_reduce(rk[:], gB.rearrange("p i (h e) -> p i e h", h=HEADS), AX.X, ALU.add))
            link(v.tensor_scalar(sE[:], rk[:], 1.0 / HEADS, None, ALU.mult))
            link(v.tensor_reduce(g1[:], sE[:], AX.X, ALU.max))
            v.tensor_tensor(tE[:], sE[:], bc(g1[:], NE), ALU.subtract).then_inc(g_exp, 1)
            link(v.memset(rk[:], 0.0))
            for e in range(NE):
                for o in range(NE):
                    if o != e:
                        link(v.tensor_tensor(g2[:], sE[:, :, o], sE[:, :, e], ALU.is_ge if o < e else ALU.is_gt))
                        link(v.tensor_tensor(rk[:, :, e], rk[:, :, e], g2[:], ALU.add))
            v.wait_ge(g_exp, 2)
            link(v.scalar_tensor_tensor(out=gate[:], in0=rk[:], scalar=2.0, in1=tE[:], op0=ALU.is_lt, op1=ALU.mult))
            link(v.tensor_reduce(g1[:], gate[:], AX.X, ALU.add))
            link(v.reciprocal(g2[:], g1[:]))
            link(v.tensor_tensor(gate[:], gate[:], bc(g2[:], NE), ALU.mult))
            assert c[0] == GATES, c[0]

            gate_v = gate[:].rearrange("p i e -> p (i e)")
            v.wait_ge(b2_ld, 16)

            def unit(i, live):
                if live(0) and i.r % NE == 0:
                    g = group_of(i)
                    p_ = tn_p[g.slot(2)]
                    held(v, tn_hi, g.n(1, 1))
                    v.tensor_tensor(p_[:, 1, :, :], tnG, p_[:, 0, :, :].bitcast(F32), ALU.subtract).then_inc(tn_lo, 1)
                if live(2):
                    k = i.back(2)
                    for f in range(FC):
                        held(v, h_hi, k.n(FC, f + 1))
                        v.tensor_tensor(h_p[:, k.slot(2), 1, f, :], hx[:, f, :], h_p[:, k.slot(2), 0, f, :].bitcast(F32), ALU.subtract).then_inc(h_lo, 1)
                if live(3):
                    k = i.back(3)
                    e, g = k.r % NE, group_of(k)
                    b = g.slot(2)
                    if e == 0:
                        held(v, tG_ld[b], g.dmas(2))
                        if live(3 + 2 * NE):
                            held(v, out_st[b], g.back(2).dmas(2))
                    def g_(t):
                        return gate_v[:, bass.ds(g.n(G * NE, t * NE + e), 1)]
                    for t in range(G):
                        if e:
                            held(v, acc_done, k.back(1).n(G, t + 1))
                        src = acc[:, b, t, :] if e else tG[:, b, t, :]
                        v.scalar_tensor_tensor(out=acc[:, b, t, :], in0=b2b[:, e, :], scalar=g_(t), in1=src, op0=ALU.mult, op1=ALU.add).then_inc(b2_added, 1)
                    for t in range(G):
                        if t % 2 == 0:
                            held(v, y_ps, k.n(G, t + 2))
                        held(v, b2_added, k.n(G, t + 1))
                        y = banks[4 + 2 * k.slot(2) + t // 2][:, (t % 2) * D:(t % 2 + 1) * D]
                        v.scalar_tensor_tensor(out=acc[:, b, t, :], in0=y, scalar=g_(t), in1=acc[:, b, t, :], op0=ALU.mult, op1=ALU.add).then_inc(acc_done, 1)
            steps(v, NG * NE, 3, unit, unroll=2 * NE)


class general_path:

    def __init__(self, nc, room, sem, banks, row_d, st_d, edges, ident, M, ROW, ST, HE, HEADS, ET, T, S, sums):
        self.banks, self.row_d, self.st_d, self.edges, self.ident = banks, row_d, st_d, edges, ident
        self.M, self.ROW, self.ST, self.HE, self.HEADS, self.ET = M, ROW, ST, HE, HEADS, ET
        self.T, self.S, self.sums = T, S, sums
        at = [0]

        def sb(_, shape, dt=F32):
            n = 1
            for d in shape[1:]:
                n *= d
            a = room[:, at[0]:at[0] + n]
            at[0] += n
            if dt != F32:
                a = a.bitcast(dt)
            if len(shape) == 3:
                a = a.rearrange("p (a b) -> p a b", a=shape[1])
            return a
        self.lower = sb("lower", [P, P])
        self.ends = sb("ends", [P, 2], I32)
        self.isrc = sb("isrc", [P, 1], U32)
        self.idst = sb("idst", [P, 1], U32)
        self.iwr = sb("iwr", [P, 1], U32)
        self.dstf = sb("dstf", [P, 1])
        self.rs = sb("rs", [P, ROW])
        self.so = sb("so", [P, ST])
        self.sn = sb("sn", [P, ST])
        self.ee = sb("ee", [P, 2, HEADS])
        self.eq = sb("eq", [P, P])
        self.pen = sb("pen", [P, P])
        self.msk = sb("msk", [P, HEADS, P])
        self.tm = sb("tm", [P, HEADS])
        self.df = sb("df", [P, 2, HEADS])
        self.ex = sb("ex", [P, 2, HEADS])
        self.vv = sb("vv", [P, HE + HEADS])
        self.oc = sb("oc", [P, HE + HEADS])
        self.cnt = sb("cnt", [P, 1])
        self.s = {n: sem("gp_" + n) for n in "init stored st_ld ld eq_ps eT_ps v sum_ps exp".split()}
        self.PARTS = 4
        self.dma = [{n: sem(f"gp_{n}{k}") for n in ("rows", "states", "wr")} for k in range(self.PARTS)]

    V = 21

    def sync(self, sp):
        s = self.s
        states = self.st_d.rearrange("(i p) k -> p i k", p=P)
        sp.wait_ge(s["init"], 8)
        sp.dma_start(states, self.S).then_inc(s["stored"], 16)
        with sp.Fori(0, self.ET) as i:
            for k in range(2):
                sp.dma_start(self.ends[:, k:k + 1], self.edges[k, bass.ds(i * P, P)].rearrange("(p o) -> p o", o=1)).then_inc(s["ld"], 16)
            held(sp, s["v"], i * self.V + 3)
        for part in self.dma:
            sp.wait_ge(part["wr"], 16 * self.ET // self.PARTS)
        sp.dma_start(self.S, states).then_inc(s["st_ld"], 16)

    def gpsimd(self, pool):
        s = self.s
        pool.wait_ge(s["init"], 8)
        pool.affine_select(out=self.lower, in_=self.lower, compare_op=ALU.is_gt, fill=0.0, base=0,
                           pattern=[[-1, P]], channel_multiplier=1).then_inc(s["init"], 1)
        pool.wait_ge(s["stored"], 16)
        at = bass.IndirectOffsetOnAxis
        N = self.ET // self.PARTS
        for part, d in enumerate(self.dma):
          with pool.Fori(0, N) as n:
            i = n + part * N
            held(pool, s["v"], i * self.V + 3)
            pool.indirect_dma_start(out=self.rs[:], out_offset=None, in_=self.row_d, in_offset=at(ap=self.isrc[:], axis=0),
                                    bounds_check=self.M - 1, oob_is_err=False).then_inc(d["rows"], 16)
            pool.indirect_dma_start(out=self.so[:], out_offset=None, in_=self.st_d, in_offset=at(ap=self.idst[:], axis=0),
                                    bounds_check=self.M - 1, oob_is_err=False).then_inc(d["states"], 16)
            held(pool, s["v"], i * self.V + self.V)
            pool.indirect_dma_start(out=self.st_d, out_offset=at(ap=self.iwr[:], axis=0), in_=self.sn[:], in_offset=None,
                                    bounds_check=self.M - 1, oob_is_err=False).then_inc(d["wr"], 16)
            held(pool, d["wr"], n * 16 + 16)

    def scalar(self, act):
        s = self.s
        with act.Fori(0, self.ET) as i:
            act.wait_ge(s["v"], i * self.V + 12)
            act.activation(self.ex[:], self.df[:], ACT.Exp).then_inc(s["exp"], 1)

    def tensor(self, pe):
        s, b, H = self.s, self.banks, self.HEADS
        with pe.Fori(0, self.ET) as i:
            pe.wait_ge(s["v"], i * self.V + 3)
            pe.matmul(b[0][:, 0:P], self.dstf[:].broadcast_to([P, P]), self.ident[:], start=True, stop=True).then_inc(s["eq_ps"], 1)
            pe.wait_ge(s["v"], i * self.V + 5)
            for h in range(H):
                mm = pe.matmul(b[1][:, h * P:(h + 1) * P], self.ee[:, 1, h:h + 1].broadcast_to([P, P]), self.ident[:], start=True, stop=True)
            mm.then_inc(s["eT_ps"], 1)
            pe.wait_ge(s["v"], i * self.V + 14)
            pe.matmul(b[2][:, 0:self.HE + H], self.eq[:], self.vv[:], start=True, stop=True).then_inc(s["sum_ps"], 1)

    def vector(self, v):
        s, b, H, HE, M = self.s, self.banks, self.HEADS, self.HE, self.M
        NE = HE // H
        T, S = self.T, self.S
        v.memset(self.rs[:], 0.0).then_inc(s["init"], 1)
        v.memset(self.so[:], 0.0).then_inc(s["init"], 1)
        v.memset(self.lower[:], 1.0).then_inc(s["init"], 1)
        v.tensor_copy(S[:, :, 0:HE], T[:, :, 0:HE]).then_inc(s["init"], 1)
        v.memset(S[:, :, HE:HE + H], 1.0).then_inc(s["init"], 1)
        v.tensor_copy(S[:, :, HE + 2 * H:], T[:, :, HE + H:]).then_inc(s["init"], 1)
        v.tensor_tensor(self.sums[:, :, 0:H], T[:, :, HE:HE + H], T[:, :, HE + H:], ALU.add).then_inc(s["init"], 1)
        v.wait_ge(s["init"], 7)
        v.scalar_tensor_tensor(out=S[:, :, HE + H:HE + 2 * H], in0=self.sums[:, :, 0:H], scalar=0.2, in1=self.sums[:, :, 0:H], op0=ALU.mult, op1=ALU.max).then_inc(s["init"], 1)
        v.wait_ge(s["init"], 9)
        rs, so, sn, ee, eq, pen, msk = self.rs, self.so, self.sn, self.ee, self.eq, self.pen, self.msk
        N = self.ET // self.PARTS
        for part, d in enumerate(self.dma):
          with v.Fori(0, N) as n:
            i = n + part * N
            c = [0]

            def do(ins, wait=True):
                ins.then_inc(s["v"], 1)
                c[0] += 1
                if wait:
                    held(v, s["v"], i * self.V + c[0])
            held(v, s["ld"], i * 32 + 32)
            do(v.tensor_scalar(self.isrc[:], self.ends[:, 0:1], float(M - 1), None, ALU.min), False)
            do(v.tensor_copy(self.idst[:], self.ends[:, 1:2]), False)
            do(v.tensor_copy(self.dstf[:], self.ends[:, 1:2]))
            held(v, d["rows"], n * 16 + 16)
            held(v, d["states"], n * 16 + 16)
            do(v.tensor_tensor(ee[:, 0, :], rs[:, HE:HE + H], so[:, HE + 2 * H:], ALU.add))
            do(v.scalar_tensor_tensor(out=ee[:, 1, :], in0=ee[:, 0, :], scalar=0.2, in1=ee[:, 0, :], op0=ALU.mult, op1=ALU.max), False)
            held(v, s["eq_ps"], i + 1)
            do(v.tensor_scalar(eq[:], b[0][:, 0:P], self.dstf[:], None, ALU.is_equal))
            do(v.tensor_scalar(pen[:], eq[:], BIG, -BIG, ALU.mult, ALU.add))
            held(v, s["eT_ps"], i + 1)
            do(v.tensor_tensor(msk[:], b[1][:].rearrange("p (h j) -> p h j", h=H), pen[:].unsqueeze(1).broadcast_to([P, H, P]), ALU.add))
            do(v.tensor_reduce(self.tm[:], msk[:], AX.X, ALU.max))
            do(v.tensor_tensor(sn[:, HE + H:HE + 2 * H], so[:, HE + H:HE + 2 * H], self.tm[:], ALU.max))
            do(v.tensor_tensor(self.df[:, 0, :], ee[:, 1, :], sn[:, HE + H:HE + 2 * H], ALU.subtract), False)
            do(v.tensor_tensor(self.df[:, 1, :], so[:, HE + H:HE + 2 * H], sn[:, HE + H:HE + 2 * H], ALU.subtract), False)
            held(v, s["exp"], i + 1)
            do(v.tensor_copy(self.vv[:, HE:], self.ex[:, 0, :]), False)
            he = lambda a: a.rearrange("p (h e) -> p h e", h=H)
            do(v.tensor_tensor(he(self.vv[:, 0:HE]), he(rs[:, 0:HE]), self.ex[:, 0, :].unsqueeze(2).broadcast_to([P, H, NE]), ALU.mult), False)
            do(v.tensor_tensor(he(self.oc[:, 0:HE]), he(so[:, 0:HE]), self.ex[:, 1, :].unsqueeze(2).broadcast_to([P, H, NE]), ALU.mult), False)
            do(v.tensor_tensor(self.oc[:, HE:], so[:, HE:HE + H], self.ex[:, 1, :], ALU.mult), False)
            do(v.tensor_tensor(pen[:], eq[:], self.lower[:], ALU.mult))
            do(v.tensor_reduce(self.cnt[:], pen[:], AX.X, ALU.add))
            do(v.scalar_tensor_tensor(out=self.iwr[:], in0=self.cnt[:], scalar=65536.0, in1=self.dstf[:], op0=ALU.mult, op1=ALU.add), False)
            do(v.tensor_copy(sn[:, HE + 2 * H:], so[:, HE + 2 * H:]))
            held(v, s["sum_ps"], i + 1)
            do(v.tensor_tensor(sn[:, 0:HE + H], self.oc[:], b[2][:, 0:HE + H], ALU.add))
            assert c[0] == self.V
        v.wait_ge(s["st_ld"], 16)
        v.tensor_copy(self.sums[:], S[:, :, 0:HE + H]).then_inc(s["init"], 1)
        v.wait_ge(s["init"], 10)


_INS = ["x", "cbT", "cb", "wgat", "att", "b_gat", "gamma", "beta", "w1", "b1", "w2", "b2", "edges"]


def kernel(x, L0_conv_codebook, L0_ffn_W_gat, L0_ffn_att_src, L0_ffn_att_dst, L0_ffn_b_gat, L0_ffn_ln_gamma,
           L0_ffn_ln_beta, L0_ffn_W1, L0_ffn_b1, L0_ffn_W2, L0_ffn_b2, L0_ffn_edge_index):
    import numpy as np
    import concourse.bacc as bacc
    from concourse.bass_utils import run_bass_kernel_spmd

    B, C, H, W = x.shape
    arrays = {
        "x": np.ascontiguousarray(np.asarray(x).reshape(B, C, H * W).transpose(0, 2, 1).reshape(B * H * W, C)),
        "cbT": np.ascontiguousarray(np.asarray(L0_conv_codebook).T),
        "cb": np.ascontiguousarray(L0_conv_codebook),
        "wgat": np.ascontiguousarray(L0_ffn_W_gat),
        "att": np.stack([np.asarray(L0_ffn_att_src).reshape(-1), np.asarray(L0_ffn_att_dst).reshape(-1)]),
        "b_gat": np.ascontiguousarray(L0_ffn_b_gat),
        "gamma": np.ascontiguousarray(L0_ffn_ln_gamma),
        "beta": np.ascontiguousarray(L0_ffn_ln_beta),
        "w1": np.ascontiguousarray(np.asarray(L0_ffn_W1).transpose(1, 0, 2)),
        "b1": np.ascontiguousarray(np.asarray(L0_ffn_b1).reshape(-1, P).T),
        "w2": np.ascontiguousarray(L0_ffn_W2),
        "b2": np.ascontiguousarray(L0_ffn_b2),
        "edges": np.ascontiguousarray(L0_ffn_edge_index),
    }
    nc = bacc.Bacc("TRN2", target_bir_lowering=False, num_devices=1)
    aps = [nc.dram_tensor(n, arrays[n].shape, mybir.dt.from_np(arrays[n].dtype), kind="ExternalInput").ap() for n in _INS]
    out = nc.dram_tensor("out", (B * H * W, C), mybir.dt.float32, kind="ExternalOutput").ap()
    metaformer(nc, *aps, out)
    r = run_bass_kernel_spmd(nc, [arrays], core_ids=[0])
    got = r.results[0]["out"]
    return np.ascontiguousarray(got.reshape(B, H * W, C).transpose(0, 2, 1).reshape(B, C, H, W))
```
